# Optimizing a Trainium2 kernel written in Bass

```python
import numpy as np
import jax
import jax.numpy as jnp

def _softmax(x, axis=-1):
    return jax.nn.softmax(x, axis=axis)

def _gelu(x):
    return jax.nn.gelu(x, approximate=True)

def _silu(x):
    return jax.nn.silu(x)

def _sigmoid(x):
    return jax.nn.sigmoid(x)

def _layernorm(x, axis=-1, eps=1e-05):
    m = jnp.mean(x, axis=axis, keepdims=True)
    v = jnp.var(x, axis=axis, keepdims=True)
    return (x - m) / jnp.sqrt(v + eps)

def _scatter_add(tgt, idx, src, axis=0):
    return tgt.at[idx].add(src)

def _segment_sum(src, seg, n):
    return jax.ops.segment_sum(src, seg, n)
kernel_name = 'mk_decoder_postln_d1_seqx_r8_9555d8'

def setup_inputs(seed: int=0):
    np.random.seed(seed)
    _w = jnp.asarray

    def _rec_inputs():
        import jax
        import jax.numpy as jnp
        _rk = jax.random.key(seed)
        x = -0.000125 + 0.9999 * jax.random.normal(jax.random.fold_in(_rk, 1), (4, 256, 256), jnp.float32)
        _lenS = 256 - jax.random.randint(jax.random.fold_in(_rk, 7), (4,), 0, max(1, 256 // 4) + 1, jnp.int32)
        _lenS2 = 64 - jax.random.randint(jax.random.fold_in(_rk, 8), (4,), 0, max(1, 64 // 4) + 1, jnp.int32)
        _ctx_2048P = jax.random.normal(jax.random.fold_in(_rk, 11), (4, 16, 256), jnp.float32)
        _ctx_2048c = jax.random.dirichlet(jax.random.fold_in(_rk, 511), 0.3 * jnp.ones((16,), jnp.float32), (4, 64))
        _ctx_2048t = jnp.einsum('bsk,bkd->bsd', _ctx_2048c, _ctx_2048P)
        _ctx_2048t = _ctx_2048t * jax.lax.rsqrt(jnp.mean(jnp.square(_ctx_2048t)) + 1e-12) * 0.953939
        ctx_2048 = -0.000514642 + 1.00011 * (_ctx_2048t + 0.3 * jax.random.normal(jax.random.fold_in(_rk, 611), (4, 64, 256), jnp.float32))
        _validS = jnp.arange(256)[None, :] < _lenS[:, None]
        _validS2 = jnp.arange(64)[None, :] < _lenS2[:, None]
        _causal = jnp.tril(jnp.ones((256, 256), dtype=bool))
        mask_BxS2_bk0 = jnp.logical_not(jnp.broadcast_to(_validS2[:, :], (4, 64)))
        return (x, ctx_2048, mask_BxS2_bk0)
    x, ctx_2048, mask_BxS2_bk0 = _rec_inputs()

    def _L0_attn_setup():
        import jax, jax.numpy as jnp
        import numpy as np
        HIDDEN = 256
        N_HEADS = 16
        HEAD_DIM = HIDDEN // N_HEADS

        def rotate_half(x):
            x1, x2 = jnp.split(x, 2, axis=-1)
            return jnp.concatenate([-x2, x1], axis=-1)
        key = jax.random.key(seed)
        k0, k1, k2, k3, k4 = jax.random.split(key, 5)
        B, S = (1, 256)
        scale = 1.0 / np.sqrt(HIDDEN)
        return {'hidden_states': jax.random.normal(k0, (B, S, HIDDEN), dtype=jnp.float32), 'Wq': jax.random.normal(k1, (HIDDEN, HIDDEN), dtype=jnp.float32) * scale, 'Wk': jax.random.normal(k2, (HIDDEN, HIDDEN), dtype=jnp.float32) * scale, 'Wv': jax.random.normal(k3, (HIDDEN, HIDDEN), dtype=jnp.float32) * scale, 'Wo': jax.random.normal(k4, (HIDDEN, HIDDEN), dtype=jnp.float32) * scale, 'gate': jnp.zeros((1, N_HEADS, 1, 1), dtype=jnp.float32)}
    _L0_attn_all = _L0_attn_setup()
    _L0_attn_in = {k: v for k, v in _L0_attn_all.items() if k in ('Wq', 'Wk', 'Wv', 'Wo', 'gate')}
    del _L0_attn_all

    def _L0_xattn_setup():
        import jax, jax.numpy as jnp
        import numpy as np
        H = 256
        NH = 16
        HD = H // NH
        EPS = 1e-06

        def rmsnorm(x, w, eps=EPS):
            var = jnp.mean(x * x, axis=-1, keepdims=True)
            return x * jax.lax.rsqrt(var + eps) * w
        key = jax.random.key(seed)
        ks = jax.random.split(key, 9)
        B, L, M = (4, 512, 32)
        s = 1.0 / np.sqrt(H)
        return {'hidden_states': jax.random.normal(ks[0], (B, L, H), dtype=jnp.float32), 'memory_tokens': jax.random.normal(ks[1], (B, M, H), dtype=jnp.float32), 'memory_mask': jax.random.randint(ks[2], (B, M), 0, 2).astype(bool), 'norm_w': jnp.ones((H,), dtype=jnp.float32), 'wq': jax.random.normal(ks[3], (H, H), dtype=jnp.float32) * s, 'wk': jax.random.normal(ks[4], (H, H), dtype=jnp.float32) * s, 'wv': jax.random.normal(ks[5], (H, H), dtype=jnp.float32) * s, 'wo': jax.random.normal(ks[6], (H, H), dtype=jnp.float32) * s, 'wg': jax.random.normal(ks[7], (H, H), dtype=jnp.float32) * s}
    _L0_xattn_all = _L0_xattn_setup()
    _L0_xattn_in = {k: v for k, v in _L0_xattn_all.items() if k in ('norm_w', 'wq', 'wk', 'wv', 'wo', 'wg')}
    del _L0_xattn_all

    def _L0_ffn_setup():
        import jax, jax.numpy as jnp
        import numpy as np
        E = 64
        K = 8
        H = 256
        I = 96
        CAP = 64

        def _moe(hidden_states, gate_w, wg, wu, wd):
            B, S, Hd = hidden_states.shape
            x = hidden_states.reshape(-1, Hd)
            T = x.shape[0]
            logits = x @ gate_w.T
            probs = jax.nn.softmax(logits.astype(jnp.float32), axis=-1)
            w, sel = jax.lax.top_k(probs, K)
            w = w / jnp.sum(w, axis=-1, keepdims=True)
            w = w.astype(x.dtype)
            eid = sel.reshape(-1)
            tok = jnp.repeat(jnp.arange(T), K)
            oh = jax.nn.one_hot(eid, E, dtype=jnp.int32)
            pos = jnp.sum(jnp.cumsum(oh, axis=0) * oh, axis=-1) - 1
            valid = pos < CAP
            slot = jnp.where(valid, pos, CAP)
            xin = jnp.zeros((E, CAP + 1, Hd), x.dtype).at[eid, slot].set(x[tok])
            inp = xin[:, :CAP]
            h = jax.nn.silu(jnp.einsum('ech,ehi->eci', inp, wg)) * jnp.einsum('ech,ehi->eci', inp, wu)
            out = jnp.einsum('eci,eih->ech', h, wd)
            out_pad = jnp.concatenate([out, jnp.zeros((E, 1, Hd), out.dtype)], axis=1)
            g = out_pad[eid, slot] * (w.reshape(-1) * valid.astype(w.dtype))[:, None]
            y = jnp.zeros((T, Hd), x.dtype).at[tok].add(g)
            return y.reshape(B, S, Hd)
        key = jax.random.key(seed)
        k1, k2, k3, k4, k5 = jax.random.split(key, 5)
        hidden_states = jax.random.normal(k1, (1, 256, H), dtype=jnp.float32)
        gate_w = jax.random.normal(k2, (E, H), dtype=jnp.float32) * 0.02
        wg = jax.random.normal(k3, (E, H, I), dtype=jnp.float32) * 0.02
        wu = jax.random.normal(k4, (E, H, I), dtype=jnp.float32) * 0.02
        wd = jax.random.normal(k5, (E, I, H), dtype=jnp.float32) * 0.02
        return {'hidden_states': hidden_states, 'gate_w': gate_w, 'wg': wg, 'wu': wu, 'wd': wd}
    _L0_ffn_all = _L0_ffn_setup()
    _L0_ffn_in = {k: v for k, v in _L0_ffn_all.items() if k in ('gate_w', 'wg', 'wu', 'wd')}
    del _L0_ffn_all
    return {'x': x, 'ctx_2048': ctx_2048, 'mask_BxS2_bk0': mask_BxS2_bk0, 'L0_attn_Wq': _L0_attn_in['Wq'], 'L0_attn_Wk': _L0_attn_in['Wk'], 'L0_attn_Wv': _L0_attn_in['Wv'], 'L0_attn_Wo': _L0_attn_in['Wo'], 'L0_attn_gate': _L0_attn_in['gate'], 'L0_xattn_norm_w': _L0_xattn_in['norm_w'], 'L0_xattn_wq': _L0_xattn_in['wq'], 'L0_xattn_wk': _L0_xattn_in['wk'], 'L0_xattn_wv': _L0_xattn_in['wv'], 'L0_xattn_wo': _L0_xattn_in['wo'], 'L0_xattn_wg': _L0_xattn_in['wg'], 'L0_ffn_gate_w': _L0_ffn_in['gate_w'], 'L0_ffn_wg': _L0_ffn_in['wg'], 'L0_ffn_wu': _L0_ffn_in['wu'], 'L0_ffn_wd': _L0_ffn_in['wd']}

def reference(x, ctx_2048, mask_BxS2_bk0, L0_attn_Wq, L0_attn_Wk, L0_attn_Wv, L0_attn_Wo, L0_attn_gate, L0_xattn_norm_w, L0_xattn_wq, L0_xattn_wk, L0_xattn_wv, L0_xattn_wo, L0_xattn_wg, L0_ffn_gate_w, L0_ffn_wg, L0_ffn_wu, L0_ffn_wd):
    import jax
    import jax.numpy as jnp

    def _L0_attn_ref(hidden_states, Wq, Wk, Wv, Wo, gate):
        import jax, jax.numpy as jnp
        import numpy as np
        HIDDEN = 256
        N_HEADS = 16
        HEAD_DIM = HIDDEN // N_HEADS

        def rotate_half(x):
            x1, x2 = jnp.split(x, 2, axis=-1)
            return jnp.concatenate([-x2, x1], axis=-1)
        B, S, H = hidden_states.shape
        q = hidden_states @ Wq.T
        k = hidden_states @ Wk.T
        v = hidden_states @ Wv.T
        inv_freq = 1.0 / 10000.0 ** (jnp.arange(0, H, 2, dtype=jnp.float32) / H)
        t = jnp.arange(S, dtype=jnp.float32)
        freqs = t[:, None] * inv_freq[None, :]
        emb = jnp.concatenate([freqs, freqs], axis=-1)[None]
        cos, sin = (jnp.cos(emb), jnp.sin(emb))
        q = q * cos + rotate_half(q) * sin
        k = k * cos + rotate_half(k) * sin

        def split_heads(x):
            return x.reshape(B, S, N_HEADS, HEAD_DIM).transpose(0, 2, 1, 3)
        q, k, v = (split_heads(q), split_heads(k), split_heads(v))
        k_feat = jax.nn.elu(k) + 1.0
        memory = jnp.einsum('bhsd,bhse->bhde', k_feat, v)
        norm_term = k_feat.sum(axis=2)
        q_feat = jax.nn.elu(q) + 1.0
        mem_out = jnp.einsum('bhsd,bhde->bhse', q_feat, memory)
        denom = jnp.einsum('bhsd,bhd->bhs', q_feat, norm_term)[..., None]
        mem_out = mem_out / denom
        scale = 1.0 / jnp.sqrt(jnp.float32(HEAD_DIM))
        scores = jnp.einsum('bhqd,bhkd->bhqk', q, k) * scale
        attn = jnp.einsum('bhqk,bhkd->bhqd', jax.nn.softmax(scores, axis=-1), v)
        g = jax.nn.sigmoid(gate)
        combined = g * mem_out + (1.0 - g) * attn
        combined = combined.transpose(0, 2, 1, 3).reshape(B, S, H)
        return combined @ Wo.T

    def _L0_xattn_ref(hidden_states, memory_tokens, memory_mask, norm_w, wq, wk, wv, wo, wg):
        import jax, jax.numpy as jnp
        import numpy as np
        H = 256
        NH = 16
        HD = H // NH
        EPS = 1e-06

        def rmsnorm(x, w, eps=EPS):
            var = jnp.mean(x * x, axis=-1, keepdims=True)
            return x * jax.lax.rsqrt(var + eps) * w
        B, L, C = hidden_states.shape
        M = memory_tokens.shape[1]
        scale = HD ** (-0.5)
        x = rmsnorm(hidden_states, norm_w)
        q = (x @ wq.T).reshape(B, L, NH, HD)
        k = (memory_tokens @ wk.T).reshape(B, M, NH, HD)
        v = (memory_tokens @ wv.T).reshape(B, M, NH, HD)
        attn = jnp.einsum('blhd,bmhd->bhlm', q, k) * scale
        attn = jnp.where(memory_mask[:, None, None, :], attn, -jnp.inf)
        attn = jax.nn.softmax(attn, axis=-1)
        attn = jnp.nan_to_num(attn, nan=0.0)
        out = jnp.einsum('bhlm,bmhd->blhd', attn, v).reshape(B, L, C)
        out = out @ wo.T
        gate = jax.nn.sigmoid(x @ wg.T)
        return gate * out

    def _L0_ffn_ref(hidden_states, gate_w, wg, wu, wd):
        import jax, jax.numpy as jnp
        import numpy as np
        E = 64
        K = 8
        H = 256
        I = 96
        CAP = 64

        def _moe(hidden_states, gate_w, wg, wu, wd):
            B, S, Hd = hidden_states.shape
            x = hidden_states.reshape(-1, Hd)
            T = x.shape[0]
            logits = x @ gate_w.T
            probs = jax.nn.softmax(logits.astype(jnp.float32), axis=-1)
            w, sel = jax.lax.top_k(probs, K)
            w = w / jnp.sum(w, axis=-1, keepdims=True)
            w = w.astype(x.dtype)
            eid = sel.reshape(-1)
            tok = jnp.repeat(jnp.arange(T), K)
            oh = jax.nn.one_hot(eid, E, dtype=jnp.int32)
            pos = jnp.sum(jnp.cumsum(oh, axis=0) * oh, axis=-1) - 1
            valid = pos < CAP
            slot = jnp.where(valid, pos, CAP)
            xin = jnp.zeros((E, CAP + 1, Hd), x.dtype).at[eid, slot].set(x[tok])
            inp = xin[:, :CAP]
            h = jax.nn.silu(jnp.einsum('ech,ehi->eci', inp, wg)) * jnp.einsum('ech,ehi->eci', inp, wu)
            out = jnp.einsum('eci,eih->ech', h, wd)
            out_pad = jnp.concatenate([out, jnp.zeros((E, 1, Hd), out.dtype)], axis=1)
            g = out_pad[eid, slot] * (w.reshape(-1) * valid.astype(w.dtype))[:, None]
            y = jnp.zeros((T, Hd), x.dtype).at[tok].add(g)
            return y.reshape(B, S, Hd)
        return _moe(hidden_states, gate_w, wg, wu, wd)
    x = _layernorm(x + _L0_attn_ref(x, L0_attn_Wq, L0_attn_Wk, L0_attn_Wv, L0_attn_Wo, L0_attn_gate), axis=-1)
    x = _layernorm(x + _L0_xattn_ref(x, ctx_2048, mask_BxS2_bk0, L0_xattn_norm_w, L0_xattn_wq, L0_xattn_wk, L0_xattn_wv, L0_xattn_wo, L0_xattn_wg), axis=-1)
    x = _layernorm(x + _L0_ffn_ref(x, L0_ffn_gate_w, L0_ffn_wg, L0_ffn_wu, L0_ffn_wd), axis=-1)
    return x

_drawn_inputs = setup_inputs


def setup_inputs(seed=0):
    import zlib

    import numpy as np

    out = dict(_drawn_inputs(seed))
    spreads = {'L0_attn_gate': (0.0, 0.8), 'L0_xattn_norm_w': (1.0, 0.2)}
    factors = {'L0_ffn_gate_w': 8.0, 'L0_ffn_wg': 8.0, 'L0_ffn_wu': 8.0, 'L0_ffn_wd': 8.0}
    for name, (base, spread) in spreads.items():
        noise = np.random.default_rng([zlib.crc32(name.encode()), seed]).standard_normal(out[name].shape)
        drawn = base * np.exp(spread * noise) if base else spread * noise
        out[name] = jnp.asarray(drawn.astype(out[name].dtype))
    for name, factor in factors.items():
        out[name] = (out[name] * factor).astype(out[name].dtype)
    return out
```

```python
from contextlib import ExitStack

import concourse.bass as bass
from concourse import mybir
import numpy as np

ALU = mybir.AluOpType
ACT = mybir.ActivationFunctionType
F32 = mybir.dt.float32
BF16 = mybir.dt.bfloat16
I32 = mybir.dt.int32
U8 = mybir.dt.uint8
AX = mybir.AxisListType

B, T, D = 4, 256, 256
P = 128
NT, NC = T // P, D // P
NH, HD = 16, 16
HC = NH // NC
HV = HD + 1
MEM = 64
E, TOPK, INNER, CAP = 64, 8, 96, 64
PAIRS = E // 2
RING = 8
ROW = D + E
NTOK = B * T
ROWS = NTOK + CAP
GRING = 4
CHAINS = 2
NEG = -1.0e30
GROUPS_Q = ((0, 3), (0, 2), (0, 1))
GROUPS_K = ((0, 1), (0, 1), (0, 1), (1, 2), (1, 2), (2, 3))
SPLIT_ROWS = 6 * HD
GRP = 8

W_NAMES = ("q", "k", "v", "o", "xq", "xg", "xo", "xk", "xv")
CONST = {}
_at = 0
for _n, _w in (("cos", T), ("sin", T), ("ident", P), ("head_of_row", HC), ("xhead_of_row", HC),
               ("half_of_row", 2), ("key", NT), ("slot", CAP), ("place_of_row", NH)):
    CONST[_n] = slice(_at, _at + _w)
    _at += _w
CONST_W = _at
PARAM_W = NH + NC


def build(nc, x_tok, x_feat, weights, router, params, ctx_feat, mask_row, mask_col, consts,
          wgu, wd, out):
    with ExitStack() as ctx:
        def sb(name, shape, dt=F32):
            return ctx.enter_context(nc.sbuf_tensor(name, shape, dt))

        def ps(name, shape, dt=F32):
            return ctx.enter_context(nc.psum_tensor(name, shape, dt))

        w_sb = {n: sb(f"w_{n}", [P, NC, D]) for n in W_NAMES}
        router_sb = sb("router_sb", [P, NC, E])
        con = sb("con", [P, CONST_W])
        identb = sb("identb", [P, P], BF16)
        par = sb("par", [P, PARAM_W])
        gate_mem = sb("gate_mem", [P, NH])
        gate_att = sb("gate_att", [P, NH])
        gate_tmp = sb("gate_tmp", [P, NH])
        cos, sin, ident = (con[:, CONST[n]] for n in ("cos", "sin", "ident"))

        xf = sb("xf", [P, NC, T])
        xt = sb("xt", [P, NT, D])
        vaug = sb("vaug", [P, NT, NH, HV])
        rot_a = sb("rot_a", [P, 2, NC, T])
        rot_b = sb("rot_b", [P, 2, NC, T])
        qk = sb("qk", [P, 2, NC, T])
        parts = sb("parts", [P, 2, 3, NC, T], BF16)
        rest = rot_b
        feat = sb("feat", [P, 2, NC, T])
        kfeat_tok = sb("kfeat_tok", [P, NT, D])
        memory = sb("memory", [P, NC, HC * HV])
        q_op = sb("q_op", [P, NH, T], BF16)
        k_op = sb("k_op", [P, NH, T], BF16)
        nmax = sb("nmax", [P, NH, NT])
        nmax_parts = sb("nmax_parts", [P, NT, 2, NH], BF16)
        probs = sb("probs", [P, 2, 2, NT, T])
        r_lin = sb("r_lin", [P, NT, NH])
        r_att = sb("r_att", [P, NT, NH])
        mix_a = sb("mix_a", [P, NT, NH, HD])
        mix_b = sb("mix_b", [P, NT, NH, HD])
        mixed = sb("mixed", [P, NT, D])
        mixed_f = sb("mixed_f", [P, NC, T])
        res = sb("res", [P, NT, D])
        stats = sb("stats", [P, NT, 6])
        mv = sb("mv", [P, NT, 2])
        mhalf = sb("mhalf", [P, 8])
        rstd = sb("rstd", [P, NT])
        x1 = sb("x1", [P, NT, D])
        sq = sb("sq", [P, NT, D])
        ssum = sb("ssum", [P, NT])
        rinv = sb("rinv", [P, NT])
        xn = sb("xn", [P, NT, D])
        xn_f = sb("xn_f", [P, NC, T])
        xq_f = sb("xq_f", [P, NC, T])
        ctx_sb = sb("ctx_sb", [P, NC, B, 2, MEM])
        maskr = sb("maskr", [1, B, MEM], U8)
        maskc = sb("maskc", [P, B], U8)
        maskf = sb("maskf", [P, B])
        mbias = sb("mbias", [1, B, HC, MEM], BF16)
        ones_row = sb("ones_row", [1, P], BF16)
        xk_f = sb("xk_f", [P, NC, B, MEM])
        xk_blk = sb("xk_blk", [P, NC, HC, MEM])
        xv_m = sb("xv_m", [P, B, NH, HV])
        xv_blk = sb("xv_blk", [P, B, NH // 2, 2, HV])
        xmax = sb("xmax", [P, NT, NH])
        xp = sb("xp", [P, NT, NH, MEM])
        xp_t = sb("xp_t", [P, NT, NH // 2, P])
        egate = sb("egate", [P, NT, D])
        sgate = sb("sgate", [P, NT, D])
        rsum = sb("rsum", [P, NT, NH])
        xatt = sb("xatt", [P, NT, D])
        xatt_f = sb("xatt_f", [P, NC, T])
        ygate = sb("ygate", [P, NT, D])
        row = sb("row", [P, NT, ROW])
        x2_f = sb("x2_f", [P, NC, T])
        lmax = sb("lmax", [P, NT])
        eprob = sb("eprob", [P, NT, E])
        top = sb("top", [P, NT, TOPK])
        tsum = sb("tsum", [P, NT])
        left = sb("left", [P, NT, E])
        wrow = sb("wrow", [P, NT, E])
        keycol = sb("keycol", [P, NT])
        keys = sb("keys", [P, NT, E])
        cand = sb("cand", [E, CAP + T])
        chosen = sb("chosen", [E, CAP])
        zslot = sb("zslot", [E, CAP])
        tok = sb("tok", [E, CAP])
        tokd = sb("tokd", [E, 2, CAP])
        idx_in = sb("idx_in", [P, PAIRS], I32)
        idx_out = sb("idx_out", [P, PAIRS], I32)
        zeros = sb("zeros", [P, ROW])

        flat = probs[:].rearrange("p a b k t -> p (a b k t)")
        gath = flat[:, 0:GRING * ROW].rearrange("p (g r) -> p g r", g=GRING)
        at = GRING * ROW
        hexp, hsig, hid = (flat[0:INNER, at + i * 2 * P:at + (i + 1) * 2 * P].rearrange("p (g s) -> p g s", g=2)
                           for i in range(3))
        flat = xp_t[:].rearrange("p t j q -> p (t j q)")
        yw = flat[:, 0:4 * D].rearrange("p (g d) -> p g d", g=4)
        xin = flat[:, 4 * D:6 * D].rearrange("p (g c s) -> p g c s", g=2, c=NC)
        fsum = flat[:, 6 * D:8 * D].rearrange("p (g d) -> p g d", g=2)
        fin = xp[:].rearrange("p t h m -> p (t h m)").rearrange("p (g f d) -> p g f d", g=2, f=4)
        gu_sb = sb("gu_sb", [P, RING, 2, 2, NC, INNER])
        wd_sb = sb("wd_sb", [INNER, RING, 2, D])

        SA = ps("SA", [P, 1024])
        SB = ps("SB", [P, 1024])
        O = ps("O", [P, 2, 512])
        M = ps("M", [P, 2, 512])
        slot = (SA, SB)

        part_d = nc.dram_tensor("part_d", [B, 2, 3, P, NC, T], BF16, kind="Internal").ap()
        row_d = nc.dram_tensor("row_d", [ROWS, ROW], F32, kind="Internal").ap()
        acc_d = [nc.dram_tensor(f"acc_d{c}", [2 * ROWS, D], F32, kind="Internal").ap() for c in range(CHAINS)]

        PER = dict(
            xf_in=16, xt_in=16, qk_mm=1, v_mm=1, rot=2, rope=2, v_ev=1, high=1, rest_r=1, mid=1, low=1, parts_out=16,
            op_in=16 * (len(GROUPS_Q) + len(GROUPS_K)), fmin=1, fexp=1, feat=1, kfeat_mm=1, kfeat_ev=1,
            mem_mm=1, memory=1, lin_mm=1, s1_mm=GRP, s1_max=GRP, nmax_hi=1, nmax_lo=1, nmax_mm=1, nmax_rows=1,
            s2_mm=GRP, s2_exp=GRP, av_mm=GRP, r_lin=2, r_att=2, mix=2, mixed=1, mixed_mm=1, mixed_ev=1, o_mm=1,
            res1=1, stats=4, mv=4, var=2, rstd=2, x1=2, sq=2, ssum=1, rinv=1, xn=2, xn_mm=1, xn_ev=2,
            xq_mm=1, xq_ev=1, gate_mm=1, gate_exp=1, gate_1=1, gate_r=1, kblk=2, x_mm=2, xmax=2, xsub=2, xexp=2,
            xpt_mm=2, xpt_ev=2, xav_mm=2, rsum=2, xatt=1, xatt_mm=1, xatt_ev=1, xo_mm=1, ygate=1, res2=1,
            x2=2, x2_mm=1, x2_ev=1, lg_mm=1, lmax=1, eprob=2, top=2, tsum=1,
            trec=1, left=2, wraw=1, wrow=2, keys=2, keycol=1, keys_mm=1, keys_ev=1, first=CAP // 8, drop=CAP // 8,
            kept=1, row_out=32,
        )
        S = {n: ctx.enter_context(nc.semaphore(n)) for n in PER}
        for n in ("consts", "wqk_in", "w_in", "par_in", "ctx_in", "gates", "setup", "zeroed",
                  "zero_out", "maskf", "mbias", "xk_mm", "xk_ev", "xv_mm", "xv_ev", "xv_blk", "k_rows",
                  "slots", "tok_mm", "gt_mm", "xin", "gu_mm", "hexp",
                  "hstep", "hid", "wd_mm", "yw", "fadd", "fstat", "fmv", "fvar",
                  "frstd", "fout", "passed", "spare"):
            S[n] = ctx.enter_context(nc.semaphore(n))
        S["gu"] = [ctx.enter_context(nc.semaphore(f"gu_in{r}")) for r in range(RING)]
        S["gath"] = [ctx.enter_context(nc.semaphore(f"gathered{r}")) for r in range(GRING)]
        S["fin"] = [ctx.enter_context(nc.semaphore(f"fin_in{r}")) for r in range(2)]
        S["stored"] = [ctx.enter_context(nc.semaphore(f"stored{r}")) for r in range(2)]
        S["scat"] = [ctx.enter_context(nc.semaphore(f"scatter{c}")) for c in range(CHAINS)]

        SEEDED = dict(
            sync=("parts_out", "row_out"), gpsimd=("low",), scalar=("xatt_ev", "eprob", "gate_exp"),
            vector=("x2", "xn", "gate_r", "feat", "nmax_lo", "drop", "kept", "ygate", "xatt", "keys_ev"),
            tensor=("x_mm", "s1_mm", "s2_mm", "av_mm", "lin_mm"))
        BASE = {n: 1 for names in SEEDED.values() for n in names}

        def seed(eng, names):
            for n in names:
                eng.sem_inc(S[n], 1)

        def need(eng, name, b, k=None):
            eng.wait_ge(S[name], b * PER[name] + (PER[name] if k is None else k) + BASE.get(name, 0))
            if eng is nc.sync:
                passed(eng, "passed")

        def prev(eng, name, b):
            eng.wait_ge(S[name], b * PER[name] + BASE[name])
            if eng is nc.sync:
                passed(eng, "passed")

        def passed(eng, which="passed"):
            eng.sem_inc(S[which], 1)

        block = ctx.enter_context(nc.Block())

        @block.sync
        def _(sp):
            seed(sp, SEEDED["sync"])
            sp.dma_start(xf[:], x_feat[0]).then_inc(S["xf_in"], 16)
            sp.dma_start(w_sb["q"][:], weights[0]).then_inc(S["wqk_in"], 16)
            sp.dma_start(w_sb["k"][:], weights[1]).then_inc(S["wqk_in"], 16)
            sp.dma_start(con[:], consts).then_inc(S["consts"], 16)
            sp.dma_start(w_sb["v"][:], weights[2]).then_inc(S["w_in"], 16)
            sp.dma_start(xt[:], x_tok[0]).then_inc(S["xt_in"], 16)
            for i, n in enumerate(W_NAMES[3:], 3):
                sp.dma_start(w_sb[n][:], weights[i]).then_inc(S["w_in"], 16)
            sp.dma_start(router_sb[:], router).then_inc(S["w_in"], 16)
            sp.wait_ge(S["zeroed"], 1)
            sp.dma_start(row_d[NTOK:ROWS, :], zeros[0:CAP, 0:ROW]).then_inc(S["zero_out"], 16)
            for c in range(CHAINS):
                sp.dma_start(acc_d[c].rearrange("(p r) d -> p r d", p=P),
                             zeros[:, 0:D].unsqueeze(1).broadcast_to([P, 2 * ROWS // P, D])).then_inc(S["zero_out"], 16)

            def body(b):
                need(sp, "high", b)
                need(sp, "mid", b)
                need(sp, "low", b)
                sp.dma_start(part_d[b].rearrange("a s p c t -> p (a s) (c t)"),
                             parts[:].rearrange("p a s c t -> p (a s) (c t)")).then_inc(S["parts_out"], 16)
                need(sp, "parts_out", b)
                prev(sp, "s2_mm", b)
                prev(sp, "s1_mm", b)
                for op, a, groups in ((q_op, 0, GROUPS_Q), (k_op, 1, GROUPS_K)):
                    at = 0
                    for lo, hi in groups:
                        n = (hi - lo) * HD
                        sp.dma_start(op[at:at + n].rearrange("r h t -> r (h t)"),
                                     part_d[b, a, lo:hi].rearrange("s (d h) c t -> (s d) (h c t)", h=HC)
                                     ).then_inc(S["op_in"], 16)
                        at += n
                need(sp, "v_mm", b)
                need(sp, "qk_mm", b)
                sp.dma_start(xf[:], x_feat[b + 1]).then_inc(S["xf_in"], 16)
                need(sp, "res1", b)
                sp.dma_start(xt[:], x_tok[b + 1]).then_inc(S["xt_in"], 16)
                need(sp, "x2", b)
                need(sp, "wrow", b)
                sp.dma_start(row_d[0:NTOK].rearrange("(b t p) d -> b p t d", t=NT, p=P)[b], row[:]).then_inc(S["row_out"], 16)
                sp.wait_ge(S["zero_out"], 16 * (1 + CHAINS))
                sp.dma_start(acc_d[0][0:NTOK].rearrange("(b t p) d -> b p t d", t=NT, p=P)[b],
                             row[:, :, 0:D]).then_inc(S["row_out"], 16)

            with sp.Fori(0, B) as b:
                body(b)
            sp.wait_ge(S["xf_in"], 16 * (B + 1))
            sp.wait_ge(S["xt_in"], 16 * (B + 1))

            for c in range(CHAINS):
                sp.wait_ge(S["scat"][c], 16 * (PAIRS // CHAINS))
            for t in range(NTOK // P):
                if t >= 2:
                    sp.wait_ge(S["fadd"], 3 * (t - 1))
                for c in range(CHAINS):
                    sp.dma_start(fin[:, t % 2, 2 * c:2 * c + 2, :],
                                 acc_d[c].rearrange("(h r) d -> r h d", h=2)[t * P:(t + 1) * P]).then_inc(S["fin"][t % 2], 16)
                if t >= 1:
                    sp.wait_ge(S["fout"], t)
                    sp.dma_start(out[t - 1], fsum[:, (t - 1) % 2, :]).then_inc(S["stored"][(t - 1) % 2], 16)
            sp.wait_ge(S["fout"], NTOK // P)
            sp.dma_start(out[NTOK // P - 1], fsum[:, (NTOK // P - 1) % 2, :]).then_inc(S["stored"][(NTOK // P - 1) % 2], 16)
            for r in range(2):
                sp.wait_ge(S["stored"][r], 16 * (NTOK // P // 2))
            sp.wait_ge(S["row_out"], 32 * B + 1)

        @block.gpsimd
        def _(pool):
            seed(pool, SEEDED["gpsimd"])
            nc.gpsimd.memset(zeros[:], 0.0).then_inc(S["zeroed"], 1)
            nc.gpsimd.memset(mhalf[:], -0.5).then_inc(S["setup"], 1)
            nc.gpsimd.memset(vaug[:], 1.0).then_inc(S["setup"], 1)
            nc.gpsimd.memset(ones_row[:], 1.0).then_inc(S["setup"], 1)
            nc.gpsimd.memset(cand[:], 0.0).then_inc(S["setup"], 1)
            pool.wait_ge(S["xk_ev"], 1)
            pool.wait_ge(S["consts"], 16)

            def body(b):
                need(pool, "high", b)
                prev(pool, "low", b)
                nc.gpsimd.tensor_tensor(rest[:], qk[:], parts[:, :, 0], ALU.subtract).then_inc(S["rest_r"], 1)
                need(pool, "mid", b)
                nc.gpsimd.tensor_tensor(parts[:, :, 2], rest[:], parts[:, :, 1], ALU.subtract).then_inc(S["low"], 1)
                prev(pool, "x_mm", b)
                for c in range(NC):
                    nc.gpsimd.tensor_tensor(
                        xk_blk[:, c], xk_f[:, c, bass.ds(b, 1), :].broadcast_to([P, HC, MEM]),
                        con[:, CONST["xhead_of_row"]].unsqueeze(2).broadcast_to([P, HC, MEM]), ALU.mult
                    ).then_inc(S["kblk"], 1)
                for ln in (1, 2):
                    need(pool, "mv", b, NT * ln)
                    if ln == 2:
                        need(pool, "x1", b)
                    else:
                        prev(pool, "x2", b)
                    passed(pool, "passed")
                    nc.gpsimd.tensor_scalar(rstd[:], mv[:, :, 1], 1e-5, None, ALU.add).then_inc(S["var"], 1)
                    need(pool, "var", b, ln)
                    nc.gpsimd.tensor_tensor(rstd[:], rstd[:], mhalf[:, 0:NT], ALU.pow).then_inc(S["rstd"], 1)
                    if ln == 1:
                        need(pool, "sq", b)
                        prev(pool, "xn", b)
                        passed(pool, "passed")
                        nc.gpsimd.tensor_scalar(rinv[:], ssum[:], 1.0 / D, 1e-6, ALU.mult, ALU.add).then_inc(S["ssum"], 1)
                        need(pool, "ssum", b)
                        nc.gpsimd.tensor_tensor(rinv[:], rinv[:], mhalf[:, 0:NT], ALU.pow).then_inc(S["rinv"], 1)

            with pool.Fori(0, B) as b:
                body(b)

            pool.wait_ge(S["slots"], 8)
            pool.wait_ge(S["row_out"], 32 * B + 1)
            pool.wait_ge(S["zero_out"], 16 * (1 + CHAINS))

            def gather(p):
                if p >= GRING:
                    pool.wait_ge(S["yw"], 2 * (p - GRING + 1))
                nc.gpsimd.indirect_dma_start(gath[:, p % GRING, :], None, row_d,
                                             bass.IndirectOffsetOnAxis(ap=idx_in[:, p:p + 1], axis=0)).then_inc(S["gath"][p % GRING], 16)

            def scatter(p):
                pool.wait_ge(S["yw"], 2 * (p + 1))
                if p >= CHAINS:
                    pool.wait_ge(S["scat"][p % CHAINS], 16 * (p // CHAINS))
                nc.gpsimd.indirect_dma_start(acc_d[p % CHAINS], bass.IndirectOffsetOnAxis(ap=idx_out[:, p:p + 1], axis=0),
                                             yw[:, p % 4, :], None, bounds_check=2 * ROWS - 1, oob_is_err=True,
                                             compute_op=ALU.add).then_inc(S["scat"][p % CHAINS], 16)

            for p in range(PAIRS + 3):
                if p < PAIRS:
                    gather(p)
                if p >= 3:
                    scatter(p - 3)

            for t in range(NTOK // P):
                pool.wait_ge(S["fmv"], t + 1)
                nc.gpsimd.tensor_scalar(rstd[:, t % 2:t % 2 + 1], mv[:, t % 2, 1:2], 1e-5, None, ALU.add).then_inc(S["fvar"], 1)
                pool.wait_ge(S["fvar"], t + 1)
                nc.gpsimd.tensor_tensor(rstd[:, t % 2:t % 2 + 1], rstd[:, t % 2:t % 2 + 1], mhalf[:, 0:1],
                                        ALU.pow).then_inc(S["frstd"], 1)

        @block.scalar
        def _(act):
            seed(act, SEEDED["scalar"])
            act.dma_start(par[:], params).then_inc(S["par_in"], 16)
            act.dma_start(ctx_sb[:], ctx_feat).then_inc(S["ctx_in"], 16)
            act.dma_start(maskr[:], mask_row).then_inc(S["ctx_in"], 16)
            act.dma_start(maskc[:], mask_col).then_inc(S["ctx_in"], 16)

            def load_pair(p):
                act.dma_start(gu_sb[:, p % RING], wgu[p]).then_inc(S["gu"][p % RING], 16)
                act.dma_start(wd_sb[:, p % RING], wd[p]).then_inc(S["gu"][p % RING], 16)

            act.wait_ge(S["par_in"], 16)
            nc.scalar.activation(gate_tmp[:], par[:, 0:NH], ACT.Exp, scale=-1.0).then_inc(S["gates"], 1)
            act.wait_ge(S["xk_mm"], 1)
            nc.scalar.activation(xk_f[:].rearrange("p c b m -> p (c b m)"), SA[:, 0:512], ACT.Copy).then_inc(S["xk_ev"], 1)
            act.wait_ge(S["w_in"], 16 * 8)
            for p in range(RING):
                load_pair(p)
            act.wait_ge(S["consts"], 16)
            nc.scalar.activation(k_op[SPLIT_ROWS:P],
                                 con[SPLIT_ROWS:P, CONST["place_of_row"]].unsqueeze(2).broadcast_to([32, NH, T]),
                                 ACT.Copy).then_inc(S["k_rows"], 1)
            nc.scalar.activation(identb[:], ident, ACT.Copy).then_inc(S["k_rows"], 1)

            def body(b):
                need(act, "v_mm", b)
                prev(act, "av_mm", b)
                act.wait_ge(S["setup"], 4)
                nc.scalar.activation(vaug[:, :, :, 0:HD], M[:, 0, :].rearrange("p (t h d) -> p t h d", t=NT, h=NH),
                                     ACT.Copy).then_inc(S["v_ev"], 1)
                need(act, "rope", b)
                prev(act, "parts_out", b)
                nc.scalar.activation(parts[:, :, 0], qk[:], ACT.Copy).then_inc(S["high"], 1)
                need(act, "fmin", b)
                nc.scalar.activation(rot_a[:], rot_a[:], ACT.Exp).then_inc(S["fexp"], 1)
                need(act, "rest_r", b)
                nc.scalar.activation(parts[:, :, 1], rest[:], ACT.Copy).then_inc(S["mid"], 1)
                need(act, "kfeat_mm", b)
                nc.scalar.activation(kfeat_tok[:].rearrange("p t d -> p (t d)"), M[:, 1, :], ACT.Copy).then_inc(S["kfeat_ev"], 1)
                need(act, "nmax_mm", b)
                nc.scalar.activation(q_op[SPLIT_ROWS:P],
                                     O[0:32, 0, :].bitcast(BF16)[:, 0:T].unsqueeze(1).broadcast_to([32, NH, T]),
                                     ACT.Copy).then_inc(S["nmax_rows"], 1)
                for g in range(GRP):
                    need(act, "s2_mm", b, g + 1)
                    if g >= 2:
                        need(act, "av_mm", b, g - 1)
                    nc.scalar.activation(probs[:, g % 2].rearrange("p a k t -> p (a k t)"), slot[g % 2][:], ACT.Exp,
                                         scale=HD ** -0.5).then_inc(S["s2_exp"], 1)
                need(act, "mixed_mm", b)
                nc.scalar.activation(mixed_f[:].rearrange("p c t -> p (c t)"), SA[:, 0:512], ACT.Copy).then_inc(S["mixed_ev"], 1)
                for t in range(NT):
                    need(act, "x1", b, t + 1)
                    nc.scalar.activation(sq[:, t], x1[:, t], ACT.Square, accum_out=ssum[:, t:t + 1]).then_inc(S["sq"], 1)
                need(act, "xn_mm", b)
                for c in range(NC):
                    nc.scalar.activation(xn_f[:, c], SB[:, c * T:(c + 1) * T], ACT.Copy,
                                         scale=par[:, NH + c:NH + c + 1]).then_inc(S["xn_ev"], 1)
                need(act, "xq_mm", b)
                nc.scalar.activation(xq_f[:].rearrange("p c t -> p (c t)"), SB[:, 512:1024], ACT.Copy).then_inc(S["xq_ev"], 1)
                need(act, "gate_mm", b)
                prev(act, "gate_r", b)
                nc.scalar.activation(egate[:].rearrange("p t d -> p (t d)"), O[:, 0, :], ACT.Exp, scale=-1.0).then_inc(S["gate_exp"], 1)
                for t in range(NT):
                    need(act, "xsub", b, t + 1)
                    nc.scalar.activation(xp[:, t], xp[:, t], ACT.Exp, scale=HD ** -0.5).then_inc(S["xexp"], 1)
                for t in range(NT):
                    need(act, "xpt_mm", b, t + 1)
                    nc.scalar.activation(xp_t[:, t].rearrange("p j q -> p (j q)"), slot[t][:], ACT.Copy).then_inc(S["xpt_ev"], 1)
                need(act, "xatt_mm", b)
                nc.scalar.activation(xatt_f[:].rearrange("p c t -> p (c t)"), SA[:, 0:512], ACT.Copy).then_inc(S["xatt_ev"], 1)
                need(act, "x2_mm", b)
                nc.scalar.activation(x2_f[:].rearrange("p c t -> p (c t)"), SB[:, 0:512], ACT.Copy).then_inc(S["x2_ev"], 1)
                need(act, "lmax", b)
                for t in range(NT):
                    nc.scalar.activation(eprob[:, t], SB[:, 512 + t * E:512 + (t + 1) * E], ACT.Exp,
                                         bias=lmax[:, t:t + 1]).then_inc(S["eprob"], 1)

            with act.Fori(0, B) as b:
                body(b)

            def weigh(p):
                act.wait_ge(S["wd_mm"], p + 1)
                if p >= 4:
                    act.wait_ge(S["scat"][p % CHAINS], 16 * ((p - 4) // CHAINS + 1))
                for e in range(2):
                    r = slice(e * CAP, (e + 1) * CAP)
                    c = D + 2 * p + e
                    nc.scalar.activation(yw[r, p % 4, :], slot[p % 2][r, 0:D], ACT.Copy,
                                         scale=gath[r, p % GRING, c:c + 1]).then_inc(S["yw"], 1)

            for p in range(PAIRS + 1):
                if p < PAIRS:
                    act.wait_ge(S["gu_mm"], p + 1)
                    if p >= 2:
                        act.wait_ge(S["hstep"], 3 * (p - 2) + 1)
                    nc.scalar.activation(hexp[:, p % 2, :], M[0:INNER, p % 2, 0:P], ACT.Exp, scale=-1.0).then_inc(S["hexp"], 1)
                if p >= 1:
                    weigh(p - 1)
                    if p - 1 + RING < PAIRS:
                        act.wait_ge(S["gu_mm"], p)
                        load_pair(p - 1 + RING)

        @block.vector
        def _(dve):
            seed(dve, SEEDED["vector"])
            dve.wait_ge(S["consts"], 16)
            nc.vector.tensor_copy(keycol[:], con[:, CONST["key"]]).then_inc(S["setup"], 1)
            dve.wait_ge(S["gates"], 1)
            nc.vector.tensor_scalar(gate_tmp[:], gate_tmp[:], 1.0, None, ALU.add).then_inc(S["gates"], 1)
            dve.wait_ge(S["gates"], 2)
            nc.vector.reciprocal(gate_mem[:], gate_tmp[:]).then_inc(S["gates"], 1)
            dve.wait_ge(S["gates"], 3)
            nc.vector.tensor_scalar(gate_att[:], gate_mem[:], -1.0, 1.0, ALU.mult, ALU.add).then_inc(S["gates"], 1)
            dve.wait_ge(S["ctx_in"], 48)
            nc.vector.tensor_copy(maskf[:], maskc[:]).then_inc(S["maskf"], 1)
            nc.vector.tensor_scalar(mbias[:], maskr[:].unsqueeze(2).broadcast_to([1, B, HC, MEM]), -1.0, -NEG,
                                    ALU.add, ALU.mult).then_inc(S["mbias"], 1)
            dve.wait_ge(S["maskf"], 1)
            nc.vector.tensor_copy(xv_m[:, :, :, HD:HV], maskf[:].unsqueeze(2).unsqueeze(3).broadcast_to([P, B, NH, 1])
                                  ).then_inc(S["xv_ev"], 1)
            for b in range(B):
                if b % 2 == 0:
                    dve.wait_ge(S["xv_mm"], b // 2 + 1)
                nc.vector.tensor_scalar(xv_m[:, b, :, 0:HD],
                                        O[:, b // 2, (b % 2) * D:(b % 2 + 1) * D].rearrange("p (h d) -> p h d", h=NH),
                                        maskf[:, b:b + 1], None, ALU.mult).then_inc(S["xv_ev"], 1)
            dve.wait_ge(S["xv_ev"], 1 + B)
            for e in range(2):
                nc.vector.tensor_scalar(
                    xv_blk[:, :, :, e, :].rearrange("p b j v -> p (b j) v"),
                    xv_m[:].rearrange("p b (j e) v -> p (b j) e v", e=2)[:, :, e, :],
                    con[:, CONST["half_of_row"]][:, e:e + 1], None, ALU.mult).then_inc(S["xv_blk"], 1)

            def norm(b, ln, dst, x_sem):
                need(dve, f"res{ln}", b)
                for t in range(NT):
                    nc.vector.bn_stats(stats[:, t], res[:, t]).then_inc(S["stats"], 1)
                need(dve, "stats", b, NT * ln)
                passed(dve, "passed")
                for t in range(NT):
                    nc.vector.bn_aggr(mv[:, t], stats[:, t]).then_inc(S["mv"], 1)
                need(dve, "mv", b, NT * ln)
                need(dve, "rstd", b, ln)
                for t in range(NT):
                    nc.vector.tensor_scalar(dst[:, t, 0:D], res[:, t], mv[:, t, 0:1], rstd[:, t:t + 1],
                                            ALU.subtract, ALU.mult).then_inc(S[x_sem], 1)

            def body(b):
                need(dve, "qk_mm", b)
                prev(dve, "feat", b)
                src = SA[:].rearrange("p (ac t) -> p ac t", t=T)
                nc.vector.tensor_tensor(rot_a[:].rearrange("p a c t -> p (a c) t"), src,
                                        cos.unsqueeze(1).broadcast_to([P, 2 * NC, T]), ALU.mult).then_inc(S["rot"], 1)
                nc.vector.tensor_tensor(rot_b[:].rearrange("p a c t -> p (a c) t"), src,
                                        sin.unsqueeze(1).broadcast_to([P, 2 * NC, T]), ALU.mult).then_inc(S["rot"], 1)
                need(dve, "rot", b)
                prev(dve, "low", b)
                nc.vector.tensor_tensor(qk[:, :, 0], rot_a[:, :, 0], rot_b[:, :, 1], ALU.subtract).then_inc(S["rope"], 1)
                nc.vector.tensor_tensor(qk[:, :, 1], rot_a[:, :, 1], rot_b[:, :, 0], ALU.add).then_inc(S["rope"], 1)
                need(dve, "rope", b)
                nc.vector.tensor_scalar(rot_a[:], qk[:], 0.0, None, ALU.min).then_inc(S["fmin"], 1)
                need(dve, "fexp", b)
                prev(dve, "lin_mm", b)
                nc.vector.scalar_tensor_tensor(feat[:].rearrange("p a c t -> p (a c t)"),
                                               qk[:].rearrange("p a c t -> p (a c t)"), 0.0,
                                               rot_a[:].rearrange("p a c t -> p (a c t)"), ALU.max, ALU.add
                                               ).then_inc(S["feat"], 1)
                need(dve, "mem_mm", b)
                nc.vector.tensor_tensor(
                    memory[:].rearrange("p c (h v) -> p c h v", v=HV),
                    M[:, 0, 0:NC * HC * HV].rearrange("p (c h v) -> p c h v", c=NC, h=HC),
                    con[:, CONST["head_of_row"]].unsqueeze(1).unsqueeze(3).broadcast_to([P, NC, HC, HV]), ALU.mult
                ).then_inc(S["memory"], 1)
                prev(dve, "nmax_lo", b)
                for g in range(GRP):
                    need(dve, "s1_mm", b, g + 1)
                    nc.vector.tensor_reduce(nmax[:, 2 * g:2 * g + 2, :].rearrange("p h t -> p (h t)"),
                                            slot[g % 2][:].rearrange("p (n k) -> p n k", k=T), AX.X, ALU.max,
                                            negate=True).then_inc(S["s1_max"], 1)
                need(dve, "s1_max", b)
                by_t = nmax[:].rearrange("p h t -> p t h")
                nc.vector.tensor_copy(nmax_parts[:, :, 0, :], by_t).then_inc(S["nmax_hi"], 1)
                need(dve, "nmax_hi", b)
                nc.vector.tensor_tensor(nmax_parts[:, :, 1, :], by_t, nmax_parts[:, :, 0, :], ALU.subtract
                                        ).then_inc(S["nmax_lo"], 1)
                need(dve, "lin_mm", b)
                lin = M[:, :, 0:NH * HV].rearrange("p t (h v) -> p t h v", v=HV)
                att = O[:, :, 0:NH * HV].rearrange("p t (h v) -> p t h v", v=HV)
                nc.vector.reciprocal(r_lin[:], lin[:, :, :, HD]).then_inc(S["r_lin"], 1)
                need(dve, "r_lin", b, 1)
                nc.vector.tensor_tensor(r_lin[:], r_lin[:], gate_mem[:].unsqueeze(1).broadcast_to([P, NT, NH]),
                                        ALU.mult).then_inc(S["r_lin"], 1)
                need(dve, "r_lin", b)
                nc.vector.tensor_tensor(mix_a[:], lin[:, :, :, 0:HD], r_lin[:].unsqueeze(3).broadcast_to([P, NT, NH, HD]),
                                        ALU.mult).then_inc(S["mix"], 1)
                need(dve, "av_mm", b)
                nc.vector.reciprocal(r_att[:], att[:, :, :, HD]).then_inc(S["r_att"], 1)
                need(dve, "r_att", b, 1)
                nc.vector.tensor_tensor(r_att[:], r_att[:], gate_att[:].unsqueeze(1).broadcast_to([P, NT, NH]),
                                        ALU.mult).then_inc(S["r_att"], 1)
                need(dve, "r_att", b)
                nc.vector.tensor_tensor(mix_b[:], att[:, :, :, 0:HD], r_att[:].unsqueeze(3).broadcast_to([P, NT, NH, HD]),
                                        ALU.mult).then_inc(S["mix"], 1)
                need(dve, "mix", b)
                nc.vector.tensor_tensor(mixed[:].rearrange("p t d -> p (t d)"), mix_a[:].rearrange("p t h d -> p (t h d)"),
                                        mix_b[:].rearrange("p t h d -> p (t h d)"), ALU.add).then_inc(S["mixed"], 1)
                need(dve, "o_mm", b)
                need(dve, "xt_in", b)
                nc.vector.tensor_tensor(res[:].rearrange("p t d -> p (t d)"), SA[:, 512:1024],
                                        xt[:].rearrange("p t d -> p (t d)"), ALU.add).then_inc(S["res1"], 1)
                norm(b, 1, x1, "x1")
                need(dve, "rinv", b)
                for t in range(NT):
                    nc.vector.tensor_scalar(xn[:, t], x1[:, t], rinv[:, t:t + 1], None, ALU.mult).then_inc(S["xn"], 1)
                need(dve, "gate_exp", b)
                nc.vector.tensor_scalar(egate[:], egate[:], 1.0, None, ALU.add).then_inc(S["gate_1"], 1)
                need(dve, "gate_1", b)
                nc.vector.reciprocal(sgate[:], egate[:]).then_inc(S["gate_r"], 1)
                for t in range(NT):
                    need(dve, "x_mm", b, t + 1)
                    sc = slot[t][:].rearrange("p (h m) -> p h m", m=MEM)
                    nc.vector.tensor_reduce(xmax[:, t], sc, AX.X, ALU.max).then_inc(S["xmax"], 1)
                    need(dve, "xmax", b, t + 1)
                    nc.vector.tensor_tensor(xp[:, t], sc, xmax[:, t].unsqueeze(2).broadcast_to([P, NH, MEM]),
                                            ALU.subtract).then_inc(S["xsub"], 1)
                need(dve, "xav_mm", b)
                xo = M[:, :, 0:NH * HV].rearrange("p t (h v) -> p t h v", v=HV)
                nc.vector.tensor_scalar(rsum[:], xo[:, :, :, HD], 1e-30, None, ALU.max).then_inc(S["rsum"], 1)
                need(dve, "rsum", b, 1)
                nc.vector.reciprocal(rsum[:], rsum[:]).then_inc(S["rsum"], 1)
                need(dve, "rsum", b)
                nc.vector.tensor_tensor(xatt[:].rearrange("p t (h d) -> p t h d", h=NH), xo[:, :, :, 0:HD],
                                        rsum[:].unsqueeze(3).broadcast_to([P, NT, NH, HD]), ALU.mult).then_inc(S["xatt"], 1)
                need(dve, "xo_mm", b)
                nc.vector.tensor_tensor(ygate[:].rearrange("p t d -> p (t d)"), SA[:, 512:1024],
                                        sgate[:].rearrange("p t d -> p (t d)"), ALU.mult).then_inc(S["ygate"], 1)
                need(dve, "ygate", b)
                nc.vector.tensor_tensor(res[:], ygate[:], x1[:], ALU.add).then_inc(S["res2"], 1)
                prev(dve, "row_out", b)
                norm(b, 2, row, "x2")
                need(dve, "lg_mm", b)
                nc.vector.tensor_reduce(lmax[:], SB[:, 512:512 + NT * E].rearrange("p (t e) -> p t e", e=E), AX.X, ALU.max,
                                        negate=True).then_inc(S["lmax"], 1)
                need(dve, "eprob", b)
                passed(dve, "passed")
                for t in range(NT):
                    nc.vector.max(top[:, t], eprob[:, t]).then_inc(S["top"], 1)
                need(dve, "top", b)
                nc.vector.tensor_reduce(tsum[:], top[:], AX.X, ALU.add).then_inc(S["tsum"], 1)
                need(dve, "tsum", b)
                nc.vector.reciprocal(tsum[:], tsum[:]).then_inc(S["trec"], 1)
                for t in range(NT):
                    nc.vector.match_replace(left[:, t], top[:, t], eprob[:, t], -1.0).then_inc(S["left"], 1)
                need(dve, "left", b)
                nc.vector.scalar_tensor_tensor(wrow[:].rearrange("p t e -> p (t e)"), left[:].rearrange("p t e -> p (t e)"),
                                               0.0, eprob[:].rearrange("p t e -> p (t e)"), ALU.is_lt, ALU.mult
                                               ).then_inc(S["wraw"], 1)
                dve.wait_ge(S["setup"], 5)
                for t in range(NT):
                    nc.vector.tensor_scalar(keys[:, t], left[:, t], 0.0, keycol[:, t:t + 1], ALU.is_lt, ALU.mult
                                            ).then_inc(S["keys"], 1)
                need(dve, "trec", b)
                need(dve, "wraw", b)
                for t in range(NT):
                    nc.vector.tensor_scalar(row[:, t, D:ROW], wrow[:, t], tsum[:, t:t + 1], None, ALU.mult
                                            ).then_inc(S["wrow"], 1)
                need(dve, "keys", b)
                nc.vector.tensor_scalar(keycol[:], keycol[:], -float(T), None, ALU.add).then_inc(S["keycol"], 1)
                need(dve, "keys_mm", b)
                prev(dve, "drop", b)
                nc.vector.tensor_copy(cand[:, CAP:], SB[0:E, 768:1024]).then_inc(S["keys_ev"], 1)
                prev(dve, "kept", b)
                need(dve, "keys_ev", b)
                passed(dve, "passed")
                for r in range(CAP // 8):
                    eight = chosen[:, 8 * r:8 * r + 8]
                    nc.vector.max(eight, cand[:]).then_inc(S["first"], 1)
                    need(dve, "first", b, r + 1)
                    passed(dve, "passed")
                    nc.vector.match_replace(cand[:], eight, cand[:], 0.0).then_inc(S["drop"], 1)
                    need(dve, "drop", b, r + 1)
                    passed(dve, "passed")
                nc.vector.tensor_copy(cand[:, 0:CAP], chosen[:]).then_inc(S["kept"], 1)

            with dve.Fori(0, B) as b:
                body(b)

            cslot = con[0:E, CONST["slot"]]
            nc.vector.scalar_tensor_tensor(zslot[:], chosen[:], 0.0, cslot, ALU.is_equal, ALU.mult).then_inc(S["slots"], 1)
            nc.vector.tensor_scalar(tok[:], chosen[:], -1.0, float(NTOK), ALU.mult, ALU.add).then_inc(S["slots"], 1)
            dve.wait_ge(S["slots"], 2)
            for e in range(2):
                nc.vector.tensor_tensor(tokd[:, e], tok[:], zslot[:], ALU.add).then_inc(S["slots"], 1)
            dve.wait_ge(S["tok_mm"], 1)
            for e in range(2):
                r = slice(e * CAP, (e + 1) * CAP)
                src = SB[r, 0:E].rearrange("p (j e) -> p j e", e=2)[:, :, e]
                nc.vector.tensor_copy(idx_in[r], src).then_inc(S["slots"], 1)
                nc.vector.tensor_scalar(idx_out[r], src, float(e * ROWS), None, ALU.add).then_inc(S["slots"], 1)

            def gathered(p):
                dve.wait_ge(S["gt_mm"], p + 1)
                if p >= 2:
                    dve.wait_ge(S["gu_mm"], p - 1)
                nc.vector.tensor_copy(xin[:, p % 2].rearrange("p c s -> p (c s)"), O[:, p % 2, 0:D]).then_inc(S["xin"], 1)

            def hidden(p):
                dve.wait_ge(S["hexp"], p + 1)
                he, hs = hexp[:, p % 2, :], hsig[:, p % 2, :]
                nc.vector.tensor_scalar(hs, he, 1.0, None, ALU.add).then_inc(S["hstep"], 1)
                dve.wait_ge(S["hstep"], 3 * p + 1)
                nc.vector.reciprocal(hs, hs).then_inc(S["hstep"], 1)
                dve.wait_ge(S["hstep"], 3 * p + 2)
                nc.vector.tensor_tensor(hs, M[0:INNER, p % 2, 0:P], hs, ALU.mult).then_inc(S["hstep"], 1)
                dve.wait_ge(S["hstep"], 3 * p + 3)
                if p >= 2:
                    dve.wait_ge(S["wd_mm"], p - 1)
                nc.vector.tensor_tensor(hid[:, p % 2, :], M[0:INNER, p % 2, P:2 * P], hs, ALU.mult).then_inc(S["hid"], 1)

            for p in range(PAIRS + 1):
                if p < PAIRS:
                    gathered(p)
                if p >= 1:
                    hidden(p - 1)

            for t in range(NTOK // P):
                dve.wait_ge(S["fin"][t % 2], 16 * CHAINS * (t // 2 + 1))
                f = fin[:, t % 2]
                nc.vector.tensor_tensor(f[:, 0], f[:, 0], f[:, 1], ALU.add).then_inc(S["fadd"], 1)
                nc.vector.tensor_tensor(f[:, 2], f[:, 2], f[:, 3], ALU.add).then_inc(S["fadd"], 1)
                dve.wait_ge(S["fadd"], 3 * t + 2)
                if t >= 2:
                    dve.wait_ge(S["stored"][t % 2], 16 * (t // 2))
                nc.vector.tensor_tensor(fsum[:, t % 2], f[:, 0], f[:, 2], ALU.add).then_inc(S["fadd"], 1)
                dve.wait_ge(S["fadd"], 3 * t + 3)
                nc.vector.bn_stats(stats[:, t % 2], fsum[:, t % 2]).then_inc(S["fstat"], 1)
                dve.wait_ge(S["fstat"], t + 1)
                nc.vector.bn_aggr(mv[:, t % 2], stats[:, t % 2]).then_inc(S["fmv"], 1)
                dve.wait_ge(S["fmv"], t + 1)
                dve.wait_ge(S["frstd"], t + 1)
                nc.vector.tensor_scalar(fsum[:, t % 2], fsum[:, t % 2], mv[:, t % 2, 0:1], rstd[:, t % 2:t % 2 + 1],
                                        ALU.subtract, ALU.mult).then_inc(S["fout"], 1)

        @block.tensor
        def _(pe):
            seed(pe, SEEDED["tensor"])
            def mm(o, l, r, start=True, stop=True):
                return nc.tensor.matmul(o, l, r, start=start, stop=stop)

            pe.wait_ge(S["ctx_in"], 48)
            pe.wait_ge(S["w_in"], 16 * 8)
            for o in range(NC):
                for c in range(NC):
                    i = mm(SA[:, o * 256:(o + 1) * 256], w_sb["xk"][:, c, o * P:(o + 1) * P], ctx_sb[:, c, :, 0, :],
                           c == 0, c == NC - 1)
            i.then_inc(S["xk_mm"], 1)
            for b in range(B):
                for c in range(NC):
                    i = mm(O[:, b // 2, (b % 2) * D:(b % 2 + 1) * D], ctx_sb[:, c, b], w_sb["xv"][:, c], c == 0, c == NC - 1)
                if b % 2:
                    i.then_inc(S["xv_mm"], 1)
            pe.wait_ge(S["xk_ev"], 1)
            pe.wait_ge(S["wqk_in"], 32)
            pe.wait_ge(S["consts"], 16)
            pe.wait_ge(S["setup"], 4)
            pe.wait_ge(S["k_rows"], 2)
            pe.wait_ge(S["mbias"], 1)
            pe.wait_ge(S["xv_blk"], 2)

            def project(dst, wname, src):
                for o in range(NC):
                    for c in range(NC):
                        i = mm(dst[:, o * T:(o + 1) * T], w_sb[wname][:, c, o * P:(o + 1) * P], src[:, c, :], c == 0, c == NC - 1)
                return i

            def project_tok(dst, wname, src):
                for t in range(NT):
                    for c in range(NC):
                        i = mm(dst[:, t * D:(t + 1) * D], src[:, c, t * P:(t + 1) * P], w_sb[wname][:, c], c == 0, c == NC - 1)
                return i

            def turn(dst, src):
                for t in range(NT):
                    for c in range(NC):
                        i = nc.tensor.transpose(dst[:, c * T + t * P:c * T + (t + 1) * P], src[:, t, c * P:(c + 1) * P], ident)
                return i

            def body(b):
                need(pe, "xf_in", b)
                prev(pe, "ygate", b)
                prev(pe, "xatt_ev", b)
                project(SA[:, 0:512], "q", xf)
                project(SA[:, 512:1024], "k", xf).then_inc(S["qk_mm"], 1)
                prev(pe, "xatt", b)
                project_tok(M[:, 0, :], "v", xf).then_inc(S["v_mm"], 1)
                need(pe, "feat", b)
                for t in range(NT):
                    for c in range(NC):
                        i = nc.tensor.transpose(M[:, 1, t * D + c * P:t * D + (c + 1) * P], feat[:, 1, c, t * P:(t + 1) * P], ident)
                i.then_inc(S["kfeat_mm"], 1)
                need(pe, "kfeat_ev", b)
                need(pe, "v_ev", b)
                for c in range(NC):
                    for t in range(NT):
                        i = mm(M[:, 0, c * HC * HV:(c + 1) * HC * HV], kfeat_tok[:, t, c * P:(c + 1) * P],
                               vaug[:, t, c * HC:(c + 1) * HC, :], t == 0, t == NT - 1)
                i.then_inc(S["mem_mm"], 1)
                need(pe, "memory", b)
                for t in range(NT):
                    for c in range(NC):
                        i = mm(M[:, t, c * HC * HV:(c + 1) * HC * HV], feat[:, 0, c, t * P:(t + 1) * P], memory[:, c])
                i.then_inc(S["lin_mm"], 1)
                need(pe, "op_in", b)
                need(pe, "rope", b)
                prev(pe, "keys_ev", b)
                prev(pe, "eprob", b)
                for g in range(GRP):
                    if g >= 2:
                        need(pe, "s1_max", b, g - 1)
                    for a in range(2):
                        for t in range(NT):
                            n = a * NT + t
                            i = mm(slot[g % 2][:, n * T:(n + 1) * T], q_op[0:SPLIT_ROWS, 2 * g + a, t * P:(t + 1) * P],
                                   k_op[0:SPLIT_ROWS, 2 * g + a, :])
                    i.then_inc(S["s1_mm"], 1)
                need(pe, "nmax_lo", b)
                prev(pe, "gate_exp", b)
                for t in range(NT):
                    i = nc.tensor.transpose(O[0:32, 0, :].bitcast(BF16)[:, t * P:(t + 1) * P],
                                            nmax_parts[:, t].rearrange("p s h -> p (s h)"), identb[:])
                i.then_inc(S["nmax_mm"], 1)
                need(pe, "nmax_rows", b)

                def second(g):
                    if g < 2:
                        need(pe, "s1_max", b)
                    else:
                        need(pe, "s2_exp", b, g - 1)
                    for a in range(2):
                        for k in range(NT):
                            n = a * NT + k
                            i = mm(slot[g % 2][:, n * T:(n + 1) * T], k_op[:, 2 * g + a, k * P:(k + 1) * P], q_op[:, 2 * g + a, :])
                    i.then_inc(S["s2_mm"], 1)

                def weighted(g):
                    need(pe, "s2_exp", b, g + 1)
                    for a in range(2):
                        h = head_of(2 * g + a)
                        for t in range(NT):
                            for k in range(NT):
                                i = mm(O[:, t, h * HV:(h + 1) * HV], probs[:, g % 2, a, k, t * P:(t + 1) * P],
                                       vaug[:, k, h, :], k == 0, k == NT - 1)
                    i.then_inc(S["av_mm"], 1)

                for g in range(GRP + 1):
                    if g < GRP:
                        second(g)
                    if g >= 1:
                        weighted(g - 1)
                need(pe, "mixed", b)
                turn(SA[:, 0:512], mixed).then_inc(S["mixed_mm"], 1)
                need(pe, "mixed_ev", b)
                project_tok(SA[:, 512:1024], "o", mixed_f).then_inc(S["o_mm"], 1)
                need(pe, "xn", b)
                turn(SB[:, 0:512], xn).then_inc(S["xn_mm"], 1)
                need(pe, "xn_ev", b)
                project(SB[:, 512:1024], "xq", xn_f).then_inc(S["xq_mm"], 1)
                project_tok(O[:, 0, :], "xg", xn_f).then_inc(S["gate_mm"], 1)
                need(pe, "xq_ev", b)
                need(pe, "kblk", b)
                for t in range(NT):
                    if t == 0:
                        need(pe, "res1", b)
                    for c in range(NC):
                        mm(slot[t][:, c * 512:(c + 1) * 512], xq_f[:, c, t * P:(t + 1) * P], xk_blk[:, c], True, False)
                        i = mm(slot[t][:, c * 512:(c + 1) * 512], ones_row[:],
                               mbias[:, bass.ds(b, 1)].rearrange("o b h m -> o (b h m)"), False, True)
                    i.then_inc(S["x_mm"], 1)
                for t in range(NT):
                    need(pe, "xexp", b, t + 1)
                    for j in range(NH // 2):
                        i = nc.tensor.transpose(slot[t][:, j * P:(j + 1) * P],
                                                xp[:, t, 2 * j:2 * j + 2, :].rearrange("p h m -> p (h m)"), ident)
                    i.then_inc(S["xpt_mm"], 1)
                for t in range(NT):
                    need(pe, "xpt_ev", b, t + 1)
                    for j in range(NH // 2):
                        i = mm(M[:, t, 2 * j * HV:(2 * j + 2) * HV], xp_t[:, t, j, :],
                               xv_blk[:, bass.ds(b, 1), j].rearrange("p b e v -> p (b e v)"))
                    i.then_inc(S["xav_mm"], 1)
                need(pe, "xatt", b)
                turn(SA[:, 0:512], xatt).then_inc(S["xatt_mm"], 1)
                need(pe, "xatt_ev", b)
                project_tok(SA[:, 512:1024], "xo", xatt_f).then_inc(S["xo_mm"], 1)
                need(pe, "x2", b)
                turn(SB[:, 0:512], row).then_inc(S["x2_mm"], 1)
                need(pe, "x2_ev", b)
                for t in range(NT):
                    for c in range(NC):
                        i = mm(SB[:, 512 + t * E:512 + (t + 1) * E], x2_f[:, c, t * P:(t + 1) * P], router_sb[:, c], c == 0, c == NC - 1)
                i.then_inc(S["lg_mm"], 1)
                need(pe, "keys", b)
                passed(pe, "passed")
                for t in range(NT):
                    i = nc.tensor.transpose(SB[0:E, 768 + t * P:768 + (t + 1) * P], keys[:, t], ident)
                i.then_inc(S["keys_mm"], 1)

            pe.wait_ge(S["w_in"], 16 * 8)
            with pe.Fori(0, B) as b:
                body(b)

            pe.wait_ge(S["slots"], 4)
            nc.tensor.transpose(SB[:, 0:E], tokd[:].rearrange("e a c -> e (a c)"), ident[0:E, 0:E]).then_inc(S["tok_mm"], 1)
            pe.wait_ge(S["slots"], 8)

            def turn_rows(p):
                pe.wait_ge(S["gath"][p % GRING], 16 * (p // GRING + 1))
                if p >= 2:
                    pe.wait_ge(S["xin"], p - 1)
                for c in range(NC):
                    i = nc.tensor.transpose(O[:, p % 2, c * P:(c + 1) * P], gath[:, p % GRING, c * P:(c + 1) * P], ident)
                i.then_inc(S["gt_mm"], 1)

            def gate_up(p):
                pe.wait_ge(S["xin"], p + 1)
                pe.wait_ge(S["gu"][p % RING], 32 * (p // RING + 1))
                if p >= 2:
                    pe.wait_ge(S["hid"], p - 1)
                for e in range(2):
                    for u in range(2):
                        for c in range(NC):
                            i = mm(M[0:INNER, p % 2, u * P + e * CAP:u * P + (e + 1) * CAP], gu_sb[:, p % RING, e, u, c, :],
                                   xin[:, p % 2, c, e * CAP:(e + 1) * CAP], c == 0, c == NC - 1)
                i.then_inc(S["gu_mm"], 1)

            def down(p):
                pe.wait_ge(S["hid"], p + 1)
                if p >= 2:
                    pe.wait_ge(S["yw"], 2 * (p - 1))
                for e in range(2):
                    i = mm(slot[p % 2][e * CAP:(e + 1) * CAP, 0:D], hid[:, p % 2, e * CAP:(e + 1) * CAP], wd_sb[:, p % RING, e])
                i.then_inc(S["wd_mm"], 1)

            for p in range(PAIRS + 2):
                if p < PAIRS:
                    turn_rows(p)
                if 1 <= p <= PAIRS:
                    gate_up(p - 1)
                if p >= 2:
                    down(p - 2)


def head_of(j):
    return (j % NC) * HC + j // NC


_IN = ["x_tok", "x_feat", "weights", "router", "params", "ctx_feat", "mask_row", "mask_col", "consts",
       "wgu", "wd"]


def lay_out(i):
    f = np.float32
    x = np.asarray(i["x"])
    x = np.concatenate([x, np.zeros_like(x[:1])])
    a = {"x_tok": x.reshape(B + 1, NT, P, D).transpose(0, 2, 1, 3),
         "x_feat": x.transpose(0, 2, 1).reshape(B + 1, NC, P, T).transpose(0, 2, 1, 3)}
    perm = np.arange(D).reshape(NC, HC, HD).transpose(0, 2, 1).ravel()
    ws = {"q": np.asarray(i["L0_attn_Wq"])[perm].T, "k": np.asarray(i["L0_attn_Wk"])[perm].T,
          "v": np.asarray(i["L0_attn_Wv"]).T, "o": np.asarray(i["L0_attn_Wo"]).T,
          "xq": np.asarray(i["L0_xattn_wq"]).T, "xk": np.asarray(i["L0_xattn_wk"]).T, "xv": np.asarray(i["L0_xattn_wv"]).T,
          "xo": np.asarray(i["L0_xattn_wo"]).T, "xg": np.asarray(i["L0_xattn_wg"]).T}
    a["weights"] = np.stack([ws[n].reshape(NC, P, D).transpose(1, 0, 2) for n in W_NAMES])
    a["router"] = np.asarray(i["L0_ffn_gate_w"]).T.reshape(NC, P, E).transpose(1, 0, 2)
    gate = np.broadcast_to(np.asarray(i["L0_attn_gate"]).reshape(1, NH), (P, NH))
    a["params"] = np.concatenate([gate, np.asarray(i["L0_xattn_norm_w"]).reshape(NC, P).T], 1)
    c = np.asarray(i["ctx_2048"]).transpose(2, 0, 1).reshape(NC, P, B, 1, MEM).transpose(1, 0, 2, 3, 4)
    a["ctx_feat"] = np.broadcast_to(c, (P, NC, B, 2, MEM))
    m = np.asarray(i["mask_BxS2_bk0"])
    a["mask_row"] = m[None]
    a["mask_col"] = np.concatenate([m.T, m.T])
    con = np.zeros((P, CONST_W), f)
    inv = (f(1) / np.power(f(10000), np.arange(0, D, 2, dtype=f) / f(D))).astype(f)
    ang = np.arange(T, dtype=f)[None, :] * inv[perm[:P]][:, None]
    p = np.arange(P)[:, None]
    con[:, CONST["cos"]], con[:, CONST["sin"]] = np.cos(ang), np.sin(ang)
    con[:, CONST["ident"]] = np.eye(P)
    con[:, CONST["head_of_row"]] = p % HC == np.arange(HC)
    con[:, CONST["xhead_of_row"]] = p // HD == np.arange(HC)
    con[:, CONST["half_of_row"]] = p // MEM == np.arange(2)
    con[:, CONST["key"]] = NTOK - (np.arange(NT) * P + p)
    con[:, CONST["slot"]] = np.arange(CAP)
    a["consts"] = con
    con[:, CONST["place_of_row"]] = p % NH == np.arange(NH)
    gu = np.stack([np.asarray(i["L0_ffn_wg"]), np.asarray(i["L0_ffn_wu"])], 1).reshape(PAIRS, 2, 2, NC, P, INNER)
    a["wgu"] = gu.transpose(0, 4, 1, 2, 3, 5)
    a["wd"] = np.asarray(i["L0_ffn_wd"]).reshape(PAIRS, 2, INNER, D).transpose(0, 2, 1, 3)
    return {n: np.ascontiguousarray(a[n]) for n in _IN}


def kernel(**inputs):
    import concourse.bacc as bacc
    from concourse.bass_utils import run_bass_kernel_spmd

    nc = bacc.Bacc("TRN2", target_bir_lowering=False, num_devices=1)
    arrays = lay_out(inputs)
    args = [nc.dram_tensor(n, a.shape, mybir.dt.from_np(a.dtype), kind="ExternalInput").ap() for n, a in arrays.items()]
    out = nc.dram_tensor("out", (NTOK // P, P, D), F32, kind="ExternalOutput").ap()
    build(nc, *args, out)
    r = run_bass_kernel_spmd(nc, [arrays], core_ids=[0])
    return r.results[0]["out"].reshape(B, T, D)
```

```python
from contextlib import ExitStack

import concourse.bass as bass
from concourse import mybir
import numpy as np

ALU = mybir.AluOpType
ACT = mybir.ActivationFunctionType
F32 = mybir.dt.float32
BF16 = mybir.dt.bfloat16
I32 = mybir.dt.int32
U8 = mybir.dt.uint8
AX = mybir.AxisListType

B, T, D = 4, 256, 256
P = 128
NT, NC = T // P, D // P
NH, HD = 16, 16
HC = NH // NC
HV = HD + 1
VW = 32
HG = P // VW
MEM = 64
E, TOPK, INNER, CAP = 64, 8, 96, 64
PAIRS = E // 2
RING = 8
ROW = D + E
NTOK = B * T
ROWS = NTOK + CAP
GRING = 4
CHAINS = 2
NEG = -1.0e30
GROUPS_Q = ((0, 3), (0, 2), (0, 1))
GROUPS_K = ((0, 1), (0, 1), (0, 1), (1, 2), (1, 2), (2, 3))
SPLIT_ROWS = 6 * HD
GRP = 8
X2_AT, LG_AT, KEYS_AT = 2, 4, 7

W_NAMES = ("q", "k", "v", "o", "xq", "xg", "xo", "xk", "xv")
CONST = {}
_at = 0
for _n, _w in (("cos", T), ("sin", T), ("ident", P), ("head_of_row", HC), ("xhead_of_row", HC),
               ("half_of_row", 2), ("key", NT), ("slot", CAP), ("place_of_row", NH)):
    CONST[_n] = slice(_at, _at + _w)
    _at += _w
CONST_W = _at
PARAM_W = NH + NC


def build(nc, x_tok, x_feat, weights, router, params, ctx_feat, mask_row, mask_col, consts,
          wgu, wd, out):
    with ExitStack() as ctx:
        def sb(name, shape, dt=F32):
            return ctx.enter_context(nc.sbuf_tensor(name, shape, dt))

        def ps(name, shape, dt=F32):
            return ctx.enter_context(nc.psum_tensor(name, shape, dt))

        w_sb = {n: sb(f"w_{n}", [P, NC, D]) for n in W_NAMES}
        router_sb = sb("router_sb", [P, NC, E])
        con = sb("con", [P, CONST_W])
        identb = sb("identb", [P, P], BF16)
        par = sb("par", [P, PARAM_W])
        gate_mem = sb("gate_mem", [P, NH])
        gate_att = sb("gate_att", [P, NH])
        gate_tmp = sb("gate_tmp", [P, NH])
        cos, sin, ident = (con[:, CONST[n]] for n in ("cos", "sin", "ident"))

        xf = sb("xf", [P, NC, T])
        xt = sb("xt", [P, NT, D])
        vaug = sb("vaug", [P, NT, NH, VW])
        rot_a = sb("rot_a", [P, 2, NC, T])
        rot_b = sb("rot_b", [P, 2, NC, T])
        qk = sb("qk", [P, 2, NC, T])
        parts = sb("parts", [P, 2, 3, NC, T], BF16)
        rest = rot_b
        feat = sb("feat", [P, 2, NC, T])
        kfeat_tok = sb("kfeat_tok", [P, NT, D])
        memory = sb("memory", [P, NC, HC * HV])
        q_op = sb("q_op", [P, NH, T], BF16)
        k_op = sb("k_op", [P, NH, T], BF16)
        nmax = sb("nmax", [P, NH, NT])
        nmax_parts = sb("nmax_parts", [P, NT, 2, NH], BF16)
        probs = sb("probs", [P, 2, 2, NT, T])
        r_lin = sb("r_lin", [P, NT, NH])
        r_att = sb("r_att", [P, NT, NH])
        att_f = sb("att_f", [P, NH // HG, T])
        mix_a = sb("mix_a", [P, NT, NH, HD])
        mix_b = sb("mix_b", [P, NT, NH, HD])
        mixed = sb("mixed", [P, NT, D])
        mixed_f = sb("mixed_f", [P, NC, T])
        res = sb("res", [P, NT, D])
        stats = sb("stats", [P, NT, 6])
        mv = sb("mv", [P, NT, 2])
        mhalf = sb("mhalf", [P, 8])
        rstd = sb("rstd", [P, NT])
        x1 = sb("x1", [P, NT, D])
        sq = sb("sq", [P, NT, D])
        ssum = sb("ssum", [P, NT])
        rinv = sb("rinv", [P, NT])
        xn = sb("xn", [P, NT, D])
        xn_f = sb("xn_f", [P, NC, T])
        xq_f = sb("xq_f", [P, NC, T])
        ctx_sb = sb("ctx_sb", [P, NC, B, 2, MEM])
        maskr = sb("maskr", [1, B, MEM], U8)
        maskc = sb("maskc", [P, B], U8)
        maskf = sb("maskf", [P, B])
        mbias = sb("mbias", [1, B, HC, MEM], BF16)
        ones_row = sb("ones_row", [1, P], BF16)
        xk_f = sb("xk_f", [P, NC, B, MEM])
        xk_blk = sb("xk_blk", [P, NC, HC, MEM])
        xv_m = sb("xv_m", [P, B, NH, HV])
        xv_blk = sb("xv_blk", [P, B, NH // 2, 2, HV])
        xmax = sb("xmax", [P, NT, NH])
        xp = sb("xp", [P, NT, NH, MEM])
        xp_t = sb("xp_t", [P, NT, NH // 2, P])
        sgate = sb("sgate", [P, NT, D])
        rsum = sb("rsum", [P, NT, NH])
        xatt = sb("xatt", [P, NT, D])
        xatt_f = sb("xatt_f", [P, NC, T])
        ygate = sb("ygate", [P, NT, D])
        row = sb("row", [P, NT, ROW])
        x2_f = sb("x2_f", [P, NC, T])
        lmax = sb("lmax", [P, NT])
        eprob = sb("eprob", [P, NT, E])
        top = sb("top", [P, NT, TOPK])
        tsum = sb("tsum", [P, NT])
        left = sb("left", [P, NT, E])
        wrow = sb("wrow", [P, NT, E])
        keycol = sb("keycol", [P, NT])
        keys = sb("keys", [P, NT, E])
        cand = sb("cand", [E, CAP + T])
        chosen = sb("chosen", [E, CAP])
        zslot = sb("zslot", [E, CAP])
        tok = sb("tok", [E, CAP])
        tokd = sb("tokd", [E, 2, CAP])
        idx_in = sb("idx_in", [P, PAIRS], I32)
        idx_out = sb("idx_out", [P, PAIRS], I32)
        zeros = sb("zeros", [P, ROW])

        flat = probs[:].rearrange("p a b k t -> p (a b k t)")
        gath = flat[:, 0:GRING * ROW].rearrange("p (g r) -> p g r", g=GRING)
        at = GRING * ROW
        hexp, hsig, hid = (flat[0:INNER, at + i * 2 * P:at + (i + 1) * 2 * P].rearrange("p (g s) -> p g s", g=2)
                           for i in range(3))
        flat = xp_t[:].rearrange("p t j q -> p (t j q)")
        yw = flat[:, 0:4 * D].rearrange("p (g d) -> p g d", g=4)
        xin = flat[:, 4 * D:6 * D].rearrange("p (g c s) -> p g c s", g=2, c=NC)
        fsum = flat[:, 6 * D:8 * D].rearrange("p (g d) -> p g d", g=2)
        fin = xp[:].rearrange("p t h m -> p (t h m)").rearrange("p (g f d) -> p g f d", g=2, f=4)
        gu_sb = sb("gu_sb", [P, RING, 2, 2, NC, INNER])
        wd_sb = sb("wd_sb", [INNER, RING, 2, D])

        SA = ps("SA", [P, 1024])
        SB = ps("SB", [P, 1024])
        O = ps("O", [P, 2, 512])
        M = ps("M", [P, 2, 512])
        slot = (SA, SB)

        part_d = nc.dram_tensor("part_d", [B, 2, 3, P, NC, T], BF16, kind="Internal").ap()
        row_d = nc.dram_tensor("row_d", [ROWS, ROW], F32, kind="Internal").ap()
        acc_d = [nc.dram_tensor(f"acc_d{c}", [2 * ROWS, D], F32, kind="Internal").ap() for c in range(CHAINS)]

        PER = dict(
            xf_in=16, xt_in=16, qk_mm=1, v_mm=1, rot=2, rope=2, v_ev=1, high=1, rest_r=1, mid=1, low=1, parts_out=16,
            op_in=16 * (len(GROUPS_Q) + len(GROUPS_K)), fmin=1, fexp=1, feat=1, kfeat_mm=1, kfeat_ev=1,
            mem_mm=1, memory=1, lin_mm=1, s1_mm=GRP, s1_max=GRP, nmax_hi=1, nmax_lo=1, nmax_mm=1, nmax_rows=4,
            s2_mm=GRP, s2_exp=GRP, av_mm=GRP, att_ev=2, att_mm=1, r_lin=2, r_att=2, mix=2, mixed=1, mixed_mm=1, mixed_ev=1, o_mm=1,
            res1=1, stats=4, mv=4, var=2, rstd=2, x1=2, sq=2, ssum=1, rinv=1, xn=2, xn_mm=1, xn_ev=2,
            xq_mm=1, xq_ev=1, gate_mm=1, gate_th=1, kblk=2, x_mm=2, xmax=2, xsub=2, xexp=2,
            xpt_mm=2, xpt_ev=2, xav_mm=2, rsum=2, xatt=1, xatt_mm=1, xatt_ev=1, xo_mm=1, ygate=1, res2=1,
            x2=2, x2_mm=1, x2_ev=1, lg_mm=1, lmax=1, eprob=2, top=2, tsum=1,
            trec=1, left=2, wraw=1, wrow=2, keys=2, keycol=1, keys_mm=1, keys_ev=1, first=CAP // 8, drop=CAP // 8,
            kept=1, row_out=32,
        )
        S = {n: ctx.enter_context(nc.semaphore(n)) for n in PER}
        for n in ("consts", "wqk_in", "w_in", "par_in", "ctx_in", "gates", "setup", "zeroed", "first_key", "vzero",
                  "zero_out", "maskf", "mbias", "xk_mm", "xk_ev", "xv_mm", "xv_ev", "xv_blk", "k_rows",
                  "slots", "tok_mm", "gt_mm", "xin", "gu_mm", "hexp",
                  "hstep", "hid", "wd_mm", "yw", "fadd", "fstat", "fmv", "fvar",
                  "frstd", "fout", "passed"):
            S[n] = ctx.enter_context(nc.semaphore(n))
        S["gu"] = [ctx.enter_context(nc.semaphore(f"gu_in{r}")) for r in range(RING)]
        S["gath"] = [ctx.enter_context(nc.semaphore(f"gathered{r}")) for r in range(GRING)]
        S["fin"] = [ctx.enter_context(nc.semaphore(f"fin_in{r}")) for r in range(2)]
        S["stored"] = [ctx.enter_context(nc.semaphore(f"stored{r}")) for r in range(2)]
        S["scat"] = [ctx.enter_context(nc.semaphore(f"scatter{c}")) for c in range(CHAINS)]

        SEEDED = dict(
            sync=("parts_out", "row_out"), gpsimd=("low",), scalar=("mixed_ev", "eprob"),
            vector=("x2", "xn", "feat", "nmax_lo", "drop", "kept", "ygate", "mix", "mixed", "res1", "keys_ev"),
            tensor=("x_mm", "s1_mm", "s2_mm", "av_mm", "lin_mm", "xn_mm", "gate_mm"))
        BASE = {n: 1 for names in SEEDED.values() for n in names}

        def seed(eng, names):
            for n in names:
                eng.sem_inc(S[n], 1)

        def need(eng, name, b, k=None):
            eng.wait_ge(S[name], b * PER[name] + (PER[name] if k is None else k) + BASE.get(name, 0))
            if eng is nc.sync:
                passed(eng, "passed")

        def prev(eng, name, b):
            eng.wait_ge(S[name], b * PER[name] + BASE[name])
            if eng is nc.sync:
                passed(eng, "passed")

        def passed(eng, which="passed"):
            eng.sem_inc(S[which], 1)

        def pipelined(eng, iteration):
            iteration(0, None)
            with eng.Fori(1, B) as a:
                iteration(a, a - 1)
            iteration(None, B - 1)

        block = ctx.enter_context(nc.Block())

        @block.sync
        def _(sp):
            seed(sp, SEEDED["sync"])
            sp.dma_start(xf[:], x_feat[0]).then_inc(S["xf_in"], 16)
            sp.dma_start(w_sb["q"][:], weights[0]).then_inc(S["wqk_in"], 16)
            sp.dma_start(w_sb["k"][:], weights[1]).then_inc(S["wqk_in"], 16)
            sp.dma_start(con[:], consts).then_inc(S["consts"], 16)
            sp.dma_start(w_sb["v"][:], weights[2]).then_inc(S["w_in"], 16)
            sp.dma_start(xt[:], x_tok[0]).then_inc(S["xt_in"], 16)
            for i, n in enumerate(W_NAMES[3:], 3):
                sp.dma_start(w_sb[n][:], weights[i]).then_inc(S["w_in"], 16)
            sp.dma_start(router_sb[:], router).then_inc(S["w_in"], 16)
            sp.wait_ge(S["zeroed"], 1)
            sp.dma_start(row_d[NTOK:ROWS, :], zeros[0:CAP, 0:ROW]).then_inc(S["zero_out"], 16)
            for c in range(CHAINS):
                sp.dma_start(acc_d[c].rearrange("(p r) d -> p r d", p=P),
                             zeros[:, 0:D].unsqueeze(1).broadcast_to([P, 2 * ROWS // P, D])).then_inc(S["zero_out"], 16)

            def iteration(a, b):
                if a is not None:
                    need(sp, "high", a)
                    need(sp, "mid", a)
                    need(sp, "low", a)
                    sp.dma_start(part_d[a].rearrange("a s p c t -> p (a s) (c t)"),
                                 parts[:].rearrange("p a s c t -> p (a s) (c t)")).then_inc(S["parts_out"], 16)
                    need(sp, "parts_out", a)
                    prev(sp, "s2_mm", a)
                    for op, w, groups in ((q_op, 0, GROUPS_Q), (k_op, 1, GROUPS_K)):
                        at = 0
                        for lo, hi in groups:
                            n = (hi - lo) * HD
                            sp.dma_start(op[at:at + n].rearrange("r h t -> r (h t)"),
                                         part_d[a, w, lo:hi].rearrange("s (d h) c t -> (s d) (h c t)", h=HC)
                                         ).then_inc(S["op_in"], 16)
                            at += n
                    need(sp, "v_mm", a)
                    sp.dma_start(xf[:], x_feat[a + 1]).then_inc(S["xf_in"], 16)
                if b is not None:
                    need(sp, "x2", b)
                    need(sp, "wrow", b)
                    sp.dma_start(row_d[0:NTOK].rearrange("(b t p) d -> b p t d", t=NT, p=P)[b], row[:]).then_inc(S["row_out"], 16)
                    sp.wait_ge(S["zero_out"], 16 * (1 + CHAINS))
                    sp.dma_start(acc_d[0][0:NTOK].rearrange("(b t p) d -> b p t d", t=NT, p=P)[b],
                                 row[:, :, 0:D]).then_inc(S["row_out"], 16)
                if a is not None:
                    need(sp, "res1", a)
                    sp.dma_start(xt[:], x_tok[a + 1]).then_inc(S["xt_in"], 16)

            pipelined(sp, iteration)
            sp.wait_ge(S["xf_in"], 16 * (B + 1))
            sp.wait_ge(S["xt_in"], 16 * (B + 1))

            for c in range(CHAINS):
                sp.wait_ge(S["scat"][c], 16 * (PAIRS // CHAINS))
            for t in range(NTOK // P):
                if t >= 2:
                    sp.wait_ge(S["fadd"], 3 * (t - 1))
                for c in range(CHAINS):
                    sp.dma_start(fin[:, t % 2, 2 * c:2 * c + 2, :],
                                 acc_d[c].rearrange("(h r) d -> r h d", h=2)[t * P:(t + 1) * P]).then_inc(S["fin"][t % 2], 16)
                if t >= 1:
                    sp.wait_ge(S["fout"], t)
                    sp.dma_start(out[t - 1], fsum[:, (t - 1) % 2, :]).then_inc(S["stored"][(t - 1) % 2], 16)
            sp.wait_ge(S["fout"], NTOK // P)
            sp.dma_start(out[NTOK // P - 1], fsum[:, (NTOK // P - 1) % 2, :]).then_inc(S["stored"][(NTOK // P - 1) % 2], 16)
            for r in range(2):
                sp.wait_ge(S["stored"][r], 16 * (NTOK // P // 2))
            sp.wait_ge(S["row_out"], 32 * B + 1)

        @block.gpsimd
        def _(pool):
            seed(pool, SEEDED["gpsimd"])
            nc.gpsimd.memset(zeros[:], 0.0).then_inc(S["zeroed"], 1)
            nc.gpsimd.memset(mhalf[:], -0.5).then_inc(S["setup"], 1)
            nc.gpsimd.memset(vaug[:], 0.0).then_inc(S["vzero"], 1)
            pool.wait_ge(S["vzero"], 1)
            nc.gpsimd.memset(vaug[:, :, :, HD:HV], 1.0).then_inc(S["setup"], 1)
            nc.gpsimd.memset(ones_row[:], 1.0).then_inc(S["setup"], 1)
            nc.gpsimd.memset(cand[:], 0.0).then_inc(S["setup"], 1)
            pool.wait_ge(S["xk_ev"], 1)
            pool.wait_ge(S["consts"], 16)

            def norm_scale(b, ln):
                need(pool, "mv", b, NT * ln)
                if ln == 2:
                    need(pool, "x1", b)
                else:
                    prev(pool, "x2", b)
                passed(pool)
                nc.gpsimd.tensor_scalar(rstd[:], mv[:, :, 1], 1e-5, None, ALU.add).then_inc(S["var"], 1)
                need(pool, "var", b, ln)
                nc.gpsimd.tensor_tensor(rstd[:], rstd[:], mhalf[:, 0:NT], ALU.pow).then_inc(S["rstd"], 1)

            def iteration(a, b):
                if b is not None:
                    prev(pool, "x_mm", b)
                    for c in range(NC):
                        nc.gpsimd.tensor_tensor(
                            xk_blk[:, c], xk_f[:, c, bass.ds(b, 1), :].broadcast_to([P, HC, MEM]),
                            con[:, CONST["xhead_of_row"]].unsqueeze(2).broadcast_to([P, HC, MEM]), ALU.mult
                        ).then_inc(S["kblk"], 1)
                if a is not None:
                    need(pool, "high", a)
                    nc.gpsimd.tensor_tensor(rest[:], qk[:], parts[:, :, 0], ALU.subtract).then_inc(S["rest_r"], 1)
                    need(pool, "mid", a)
                    nc.gpsimd.tensor_tensor(parts[:, :, 2], rest[:], parts[:, :, 1], ALU.subtract).then_inc(S["low"], 1)
                if b is not None:
                    norm_scale(b, 2)
                if a is not None:
                    norm_scale(a, 1)
                    need(pool, "sq", a)
                    prev(pool, "xn", a)
                    passed(pool)
                    nc.gpsimd.tensor_scalar(rinv[:], ssum[:], 1.0 / D, 1e-6, ALU.mult, ALU.add).then_inc(S["ssum"], 1)
                    need(pool, "ssum", a)
                    nc.gpsimd.tensor_tensor(rinv[:], rinv[:], mhalf[:, 0:NT], ALU.pow).then_inc(S["rinv"], 1)

            pipelined(pool, iteration)

            pool.wait_ge(S["slots"], 8)
            pool.wait_ge(S["row_out"], 32 * B + 1)
            pool.wait_ge(S["zero_out"], 16 * (1 + CHAINS))

            def gather(p):
                if p >= GRING:
                    pool.wait_ge(S["yw"], 2 * (p - GRING + 1))
                nc.gpsimd.indirect_dma_start(gath[:, p % GRING, :], None, row_d,
                                             bass.IndirectOffsetOnAxis(ap=idx_in[:, p:p + 1], axis=0)).then_inc(S["gath"][p % GRING], 16)

            def scatter(p):
                pool.wait_ge(S["yw"], 2 * (p + 1))
                if p >= CHAINS:
                    pool.wait_ge(S["scat"][p % CHAINS], 16 * (p // CHAINS))
                nc.gpsimd.indirect_dma_start(acc_d[p % CHAINS], bass.IndirectOffsetOnAxis(ap=idx_out[:, p:p + 1], axis=0),
                                             yw[:, p % 4, :], None, bounds_check=2 * ROWS - 1, oob_is_err=True,
                                             compute_op=ALU.add).then_inc(S["scat"][p % CHAINS], 16)

            for p in range(PAIRS + 3):
                if p < PAIRS:
                    gather(p)
                if p >= 3:
                    scatter(p - 3)

            for t in range(NTOK // P):
                pool.wait_ge(S["fmv"], t + 1)
                nc.gpsimd.tensor_scalar(rstd[:, t % 2:t % 2 + 1], mv[:, t % 2, 1:2], 1e-5, None, ALU.add).then_inc(S["fvar"], 1)
                pool.wait_ge(S["fvar"], t + 1)
                nc.gpsimd.tensor_tensor(rstd[:, t % 2:t % 2 + 1], rstd[:, t % 2:t % 2 + 1], mhalf[:, 0:1],
                                        ALU.pow).then_inc(S["frstd"], 1)

        @block.scalar
        def _(act):
            seed(act, SEEDED["scalar"])
            act.dma_start(par[:], params).then_inc(S["par_in"], 16)
            act.dma_start(ctx_sb[:], ctx_feat).then_inc(S["ctx_in"], 16)
            act.dma_start(maskr[:], mask_row).then_inc(S["ctx_in"], 16)
            act.dma_start(maskc[:], mask_col).then_inc(S["ctx_in"], 16)

            def load_pair(p):
                act.dma_start(gu_sb[:, p % RING], wgu[p]).then_inc(S["gu"][p % RING], 16)
                act.dma_start(wd_sb[:, p % RING], wd[p]).then_inc(S["gu"][p % RING], 16)

            act.wait_ge(S["par_in"], 16)
            nc.scalar.activation(gate_tmp[:], par[:, 0:NH], ACT.Exp, scale=-1.0).then_inc(S["gates"], 1)
            act.wait_ge(S["xk_mm"], 1)
            nc.scalar.activation(xk_f[:].rearrange("p c b m -> p (c b m)"), SA[:, 0:512], ACT.Copy).then_inc(S["xk_ev"], 1)
            act.wait_ge(S["w_in"], 16 * 8)
            for p in range(RING):
                load_pair(p)
            act.wait_ge(S["consts"], 16)
            nc.scalar.activation(k_op[SPLIT_ROWS:P],
                                 con[SPLIT_ROWS:P, CONST["place_of_row"]].unsqueeze(2).broadcast_to([32, NH, T]),
                                 ACT.Copy).then_inc(S["k_rows"], 1)
            nc.scalar.activation(identb[:], ident, ACT.Copy).then_inc(S["k_rows"], 1)

            def iteration(a, b):
                if b is not None:
                    need(act, "xn_mm", b)
                    for c in range(NC):
                        nc.scalar.activation(xn_f[:, c], M[:, 0, c * T:(c + 1) * T], ACT.Copy,
                                             scale=par[:, NH + c:NH + c + 1]).then_inc(S["xn_ev"], 1)
                if a is not None:
                    need(act, "v_mm", a)
                    prev(act, "av_mm", a)
                    act.wait_ge(S["setup"], 4)
                    nc.scalar.activation(vaug[:, :, :, 0:HD], O[:, 0, :].rearrange("p (t h d) -> p t h d", t=NT, h=NH),
                                         ACT.Copy).then_inc(S["v_ev"], 1)
                    need(act, "rope", a)
                    prev(act, "parts_out", a)
                    nc.scalar.activation(parts[:, :, 0], qk[:], ACT.Copy).then_inc(S["high"], 1)
                if b is not None:
                    need(act, "xq_mm", b)
                    nc.scalar.activation(xq_f[:].rearrange("p c t -> p (c t)"), M[:, 1, :], ACT.Copy).then_inc(S["xq_ev"], 1)
                if a is not None:
                    need(act, "fmin", a)
                    nc.scalar.activation(rot_a[:], rot_a[:], ACT.Exp).then_inc(S["fexp"], 1)
                if b is not None:
                    need(act, "gate_mm", b)
                    prev(act, "ygate", b)
                    nc.scalar.activation(sgate[:].rearrange("p t d -> p (t d)"), M[:, 0, :], ACT.Tanh, scale=0.5
                                         ).then_inc(S["gate_th"], 1)
                if a is not None:
                    need(act, "rest_r", a)
                    nc.scalar.activation(parts[:, :, 1], rest[:], ACT.Copy).then_inc(S["mid"], 1)
                    need(act, "kfeat_mm", a)
                    nc.scalar.activation(kfeat_tok[:].rearrange("p t d -> p (t d)"), O[:, 1, :], ACT.Copy).then_inc(S["kfeat_ev"], 1)
                if b is not None:
                    for t in range(NT):
                        need(act, "xsub", b, t + 1)
                        nc.scalar.activation(xp[:, t], xp[:, t], ACT.Exp, scale=HD ** -0.5).then_inc(S["xexp"], 1)
                    for t in range(NT):
                        need(act, "xpt_mm", b, t + 1)
                        nc.scalar.activation(xp_t[:, t].rearrange("p j q -> p (j q)"), M[:].rearrange("p a c -> p (a c)"),
                                             ACT.Copy).then_inc(S["xpt_ev"], 1)
                    need(act, "xatt_mm", b)
                    nc.scalar.activation(xatt_f[:].rearrange("p c t -> p (c t)"), M[:, 0, :], ACT.Copy).then_inc(S["xatt_ev"], 1)
                if a is not None:
                    need(act, "nmax_mm", a)
                    for i in range(4):
                        nc.scalar.activation(q_op[SPLIT_ROWS:P, 4 * i:4 * i + 4],
                                             SA[0:32, 0:512].bitcast(BF16)[:, 0:T].unsqueeze(1).broadcast_to([32, 4, T]),
                                             ACT.Copy).then_inc(S["nmax_rows"], 1)

                def exp_group(g):
                    need(act, "s2_mm", a, g + 1)
                    if g >= 2:
                        need(act, "av_mm", a, g - 1)
                    nc.scalar.activation(probs[:, g % 2].rearrange("p a k t -> p (a k t)"), slot[g % 2][:], ACT.Exp,
                                         scale=HD ** -0.5).then_inc(S["s2_exp"], 1)

                def router_rows():
                    need(act, "x2_mm", b)
                    nc.scalar.activation(x2_f[:].rearrange("p c t -> p (c t)"), M[:, 0, :], ACT.Copy).then_inc(S["x2_ev"], 1)

                def router_exp():
                    need(act, "lmax", b)
                    for t in range(NT):
                        nc.scalar.activation(eprob[:, t], M[:, 1, t * E:(t + 1) * E], ACT.Exp,
                                             bias=lmax[:, t:t + 1]).then_inc(S["eprob"], 1)

                for g in range(GRP):
                    if a is not None:
                        exp_group(g)
                    if b is not None and g == X2_AT:
                        router_rows()
                    if b is not None and g == LG_AT:
                        router_exp()
                if a is not None:
                    for i in range(2):
                        need(act, "av_mm", a)
                        nc.scalar.activation(att_f[:, 2 * i:2 * i + 2].rearrange("p g t -> p (g t)"), O[:, i, :],
                                             ACT.Copy).then_inc(S["att_ev"], 1)
                    need(act, "mixed_mm", a)
                    nc.scalar.activation(mixed_f[:].rearrange("p c t -> p (c t)"), SB[:, 0:512], ACT.Copy).then_inc(S["mixed_ev"], 1)
                    for t in range(NT):
                        need(act, "x1", a, t + 1)
                        nc.scalar.activation(sq[:, t], x1[:, t], ACT.Square, accum_out=ssum[:, t:t + 1]).then_inc(S["sq"], 1)

            pipelined(act, iteration)

            def weigh(p):
                act.wait_ge(S["wd_mm"], p + 1)
                if p >= 4:
                    act.wait_ge(S["scat"][p % CHAINS], 16 * ((p - 4) // CHAINS + 1))
                for e in range(2):
                    r = slice(e * CAP, (e + 1) * CAP)
                    c = D + 2 * p + e
                    nc.scalar.activation(yw[r, p % 4, :], slot[p % 2][r, 0:D], ACT.Copy,
                                         scale=gath[r, p % GRING, c:c + 1]).then_inc(S["yw"], 1)

            for p in range(PAIRS + 1):
                if p < PAIRS:
                    act.wait_ge(S["gu_mm"], p + 1)
                    if p >= 2:
                        act.wait_ge(S["hstep"], 3 * (p - 2) + 1)
                    nc.scalar.activation(hexp[:, p % 2, :], M[0:INNER, p % 2, 0:P], ACT.Exp, scale=-1.0).then_inc(S["hexp"], 1)
                if p >= 1:
                    weigh(p - 1)
                    if p - 1 + RING < PAIRS:
                        act.wait_ge(S["gu_mm"], p)
                        load_pair(p - 1 + RING)

        @block.vector
        def _(dve):
            seed(dve, SEEDED["vector"])
            dve.wait_ge(S["consts"], 16)
            nc.vector.tensor_copy(keycol[:], con[:, CONST["key"]]).then_inc(S["first_key"], 1)
            dve.wait_ge(S["gates"], 1)
            nc.vector.tensor_scalar(gate_tmp[:], gate_tmp[:], 1.0, None, ALU.add).then_inc(S["gates"], 1)
            dve.wait_ge(S["gates"], 2)
            nc.vector.reciprocal(gate_mem[:], gate_tmp[:]).then_inc(S["gates"], 1)
            dve.wait_ge(S["gates"], 3)
            nc.vector.tensor_scalar(gate_att[:], gate_mem[:], -1.0, 1.0, ALU.mult, ALU.add).then_inc(S["gates"], 1)
            dve.wait_ge(S["ctx_in"], 48)
            nc.vector.tensor_copy(maskf[:], maskc[:]).then_inc(S["maskf"], 1)
            nc.vector.tensor_scalar(mbias[:], maskr[:].unsqueeze(2).broadcast_to([1, B, HC, MEM]), -1.0, -NEG,
                                    ALU.add, ALU.mult).then_inc(S["mbias"], 1)
            dve.wait_ge(S["maskf"], 1)
            nc.vector.tensor_copy(xv_m[:, :, :, HD:HV], maskf[:].unsqueeze(2).unsqueeze(3).broadcast_to([P, B, NH, 1])
                                  ).then_inc(S["xv_ev"], 1)
            for b in range(B):
                if b % 2 == 0:
                    dve.wait_ge(S["xv_mm"], b // 2 + 1)
                nc.vector.tensor_scalar(xv_m[:, b, :, 0:HD],
                                        O[:, b // 2, (b % 2) * D:(b % 2 + 1) * D].rearrange("p (h d) -> p h d", h=NH),
                                        maskf[:, b:b + 1], None, ALU.mult).then_inc(S["xv_ev"], 1)
            dve.wait_ge(S["xv_ev"], 1 + B)
            for e in range(2):
                nc.vector.tensor_scalar(
                    xv_blk[:, :, :, e, :].rearrange("p b j v -> p (b j) v"),
                    xv_m[:].rearrange("p b (j e) v -> p (b j) e v", e=2)[:, :, e, :],
                    con[:, CONST["half_of_row"]][:, e:e + 1], None, ALU.mult).then_inc(S["xv_blk"], 1)

            def norm(b, ln, dst, x_sem):
                need(dve, f"res{ln}", b)
                for t in range(NT):
                    nc.vector.bn_stats(stats[:, t], res[:, t]).then_inc(S["stats"], 1)
                need(dve, "stats", b, NT * ln)
                passed(dve, "passed")
                for t in range(NT):
                    nc.vector.bn_aggr(mv[:, t], stats[:, t]).then_inc(S["mv"], 1)
                need(dve, "mv", b, NT * ln)
                need(dve, "rstd", b, ln)
                for t in range(NT):
                    nc.vector.tensor_scalar(dst[:, t, 0:D], res[:, t], mv[:, t, 0:1], rstd[:, t:t + 1],
                                            ALU.subtract, ALU.mult).then_inc(S[x_sem], 1)

            def scores_less_max(b, t):
                need(dve, "x_mm", b, t + 1)
                sc = M[:].rearrange("p a c -> p (a c)").rearrange("p (h m) -> p h m", m=MEM)
                nc.vector.tensor_reduce(xmax[:, t], sc, AX.X, ALU.max).then_inc(S["xmax"], 1)
                need(dve, "xmax", b, t + 1)
                nc.vector.tensor_tensor(xp[:, t], sc, xmax[:, t].unsqueeze(2).broadcast_to([P, NH, MEM]),
                                        ALU.subtract).then_inc(S["xsub"], 1)

            def iteration(a, b):
                if a is not None:
                    need(dve, "qk_mm", a)
                    prev(dve, "feat", a)
                    src = SA[:].rearrange("p (ac t) -> p ac t", t=T)
                    nc.vector.tensor_tensor(rot_a[:].rearrange("p a c t -> p (a c) t"), src,
                                            cos.unsqueeze(1).broadcast_to([P, 2 * NC, T]), ALU.mult).then_inc(S["rot"], 1)
                    nc.vector.tensor_tensor(rot_b[:].rearrange("p a c t -> p (a c) t"), src,
                                            sin.unsqueeze(1).broadcast_to([P, 2 * NC, T]), ALU.mult).then_inc(S["rot"], 1)
                    need(dve, "rot", a)
                    prev(dve, "low", a)
                    nc.vector.tensor_tensor(qk[:, :, 0], rot_a[:, :, 0], rot_b[:, :, 1], ALU.subtract).then_inc(S["rope"], 1)
                    nc.vector.tensor_tensor(qk[:, :, 1], rot_a[:, :, 1], rot_b[:, :, 0], ALU.add).then_inc(S["rope"], 1)
                    need(dve, "rope", a)
                    nc.vector.tensor_scalar(rot_a[:], qk[:], 0.0, None, ALU.min).then_inc(S["fmin"], 1)
                    need(dve, "fexp", a)
                    prev(dve, "lin_mm", a)
                    nc.vector.scalar_tensor_tensor(feat[:].rearrange("p a c t -> p (a c t)"),
                                                   qk[:].rearrange("p a c t -> p (a c t)"), 0.0,
                                                   rot_a[:].rearrange("p a c t -> p (a c t)"), ALU.max, ALU.add
                                                   ).then_inc(S["feat"], 1)
                if b is not None:
                    scores_less_max(b, 0)
                if a is not None:
                    need(dve, "mem_mm", a)
                    nc.vector.tensor_tensor(
                        memory[:].rearrange("p c (h v) -> p c h v", v=HV),
                        O[:, 0, 0:NC * HC * HV].rearrange("p (c h v) -> p c h v", c=NC, h=HC),
                        con[:, CONST["head_of_row"]].unsqueeze(1).unsqueeze(3).broadcast_to([P, NC, HC, HV]), ALU.mult
                    ).then_inc(S["memory"], 1)
                if b is not None:
                    scores_less_max(b, 1)
                if a is not None:
                    need(dve, "lin_mm", a)
                    lin = O[:, :, 0:NH * HV].rearrange("p t (h v) -> p t h v", v=HV)
                    nc.vector.reciprocal(r_lin[:], lin[:, :, :, HD]).then_inc(S["r_lin"], 1)
                    need(dve, "r_lin", a, 1)
                    nc.vector.tensor_tensor(r_lin[:], r_lin[:], gate_mem[:].unsqueeze(1).broadcast_to([P, NT, NH]),
                                            ALU.mult).then_inc(S["r_lin"], 1)
                    need(dve, "r_lin", a)
                    nc.vector.tensor_tensor(mix_a[:], lin[:, :, :, 0:HD], r_lin[:].unsqueeze(3).broadcast_to([P, NT, NH, HD]),
                                            ALU.mult).then_inc(S["mix"], 1)
                if b is not None:
                    need(dve, "xav_mm", b)
                    xo = M[:, :, 0:NH * HV].rearrange("p t (h v) -> p t h v", v=HV)
                    nc.vector.tensor_scalar(rsum[:], xo[:, :, :, HD], 1e-30, None, ALU.max).then_inc(S["rsum"], 1)
                    need(dve, "rsum", b, 1)
                    nc.vector.reciprocal(rsum[:], rsum[:]).then_inc(S["rsum"], 1)
                    need(dve, "rsum", b)
                    nc.vector.tensor_tensor(xatt[:].rearrange("p t (h d) -> p t h d", h=NH), xo[:, :, :, 0:HD],
                                            rsum[:].unsqueeze(3).broadcast_to([P, NT, NH, HD]), ALU.mult).then_inc(S["xatt"], 1)

                def score_max(g):
                    need(dve, "s1_mm", a, g + 1)
                    nc.vector.tensor_reduce(nmax[:, 2 * g:2 * g + 2, :].rearrange("p h t -> p (h t)"),
                                            slot[g % 2][:].rearrange("p (n k) -> p n k", k=T), AX.X, ALU.max,
                                            negate=True).then_inc(S["s1_max"], 1)

                if a is not None:
                    for g in range(GRP):
                        score_max(g)
                    need(dve, "s1_max", a)
                    prev(dve, "nmax_lo", a)
                    by_t = nmax[:].rearrange("p h t -> p t h")
                    nc.vector.tensor_copy(nmax_parts[:, :, 0, :], by_t).then_inc(S["nmax_hi"], 1)
                    need(dve, "nmax_hi", a)
                    nc.vector.tensor_tensor(nmax_parts[:, :, 1, :], by_t, nmax_parts[:, :, 0, :], ALU.subtract
                                            ).then_inc(S["nmax_lo"], 1)
                if b is not None:
                    need(dve, "xo_mm", b)
                    nc.vector.scalar_tensor_tensor(ygate[:].rearrange("p t d -> p (t d)"), sgate[:].rearrange("p t d -> p (t d)"),
                                                   1.0, M[:, 1, :], ALU.add, ALU.mult).then_inc(S["ygate"], 1)
                    need(dve, "ygate", b)
                    nc.vector.scalar_tensor_tensor(res[:].rearrange("p t d -> p (t d)"), ygate[:].rearrange("p t d -> p (t d)"),
                                                   0.5, x1[:].rearrange("p t d -> p (t d)"), ALU.mult, ALU.add
                                                   ).then_inc(S["res2"], 1)
                    prev(dve, "row_out", b)
                    norm(b, 2, row, "x2")
                    need(dve, "lg_mm", b)
                    nc.vector.tensor_reduce(lmax[:], M[:, 1, 0:NT * E].rearrange("p (t e) -> p t e", e=E), AX.X, ALU.max,
                                            negate=True).then_inc(S["lmax"], 1)
                    need(dve, "eprob", b)
                    passed(dve)
                    for t in range(NT):
                        nc.vector.max(top[:, t], eprob[:, t]).then_inc(S["top"], 1)
                    need(dve, "top", b)
                    nc.vector.tensor_reduce(tsum[:], top[:], AX.X, ALU.add).then_inc(S["tsum"], 1)
                    need(dve, "tsum", b)
                    nc.vector.reciprocal(tsum[:], tsum[:]).then_inc(S["trec"], 1)
                    for t in range(NT):
                        nc.vector.match_replace(left[:, t], top[:, t], eprob[:, t], -1.0).then_inc(S["left"], 1)
                    need(dve, "left", b)
                    dve.wait_ge(S["first_key"], 1)
                    for t in range(NT):
                        nc.vector.tensor_scalar(keys[:, t], left[:, t], 0.0, keycol[:, t:t + 1], ALU.is_lt, ALU.mult
                                                ).then_inc(S["keys"], 1)
                    nc.vector.scalar_tensor_tensor(wrow[:].rearrange("p t e -> p (t e)"), left[:].rearrange("p t e -> p (t e)"),
                                                   0.0, eprob[:].rearrange("p t e -> p (t e)"), ALU.is_lt, ALU.mult
                                                   ).then_inc(S["wraw"], 1)
                    need(dve, "trec", b)
                    need(dve, "wraw", b)
                    for t in range(NT):
                        nc.vector.tensor_scalar(row[:, t, D:ROW], wrow[:, t], tsum[:, t:t + 1], None, ALU.mult
                                                ).then_inc(S["wrow"], 1)
                    need(dve, "keys", b)
                    nc.vector.tensor_scalar(keycol[:], keycol[:], -float(T), None, ALU.add).then_inc(S["keycol"], 1)
                    need(dve, "keys_mm", b)
                    prev(dve, "drop", b)
                    nc.vector.tensor_copy(cand[:, CAP:], M[0:E, 1, 256:512]).then_inc(S["keys_ev"], 1)
                    prev(dve, "kept", b)
                    need(dve, "keys_ev", b)
                    passed(dve)
                    for r in range(CAP // 8):
                        eight = chosen[:, 8 * r:8 * r + 8]
                        nc.vector.max(eight, cand[:]).then_inc(S["first"], 1)
                        need(dve, "first", b, r + 1)
                        passed(dve)
                        nc.vector.match_replace(cand[:], eight, cand[:], 0.0).then_inc(S["drop"], 1)
                        need(dve, "drop", b, r + 1)
                        passed(dve)
                    nc.vector.tensor_copy(cand[:, 0:CAP], chosen[:]).then_inc(S["kept"], 1)
                if a is not None:
                    need(dve, "att_mm", a)
                    att = SA[:].rearrange("p (t h v) -> p t h v", t=NT, v=VW)
                    nc.vector.reciprocal(r_att[:], att[:, :, :, HD]).then_inc(S["r_att"], 1)
                    need(dve, "r_att", a, 1)
                    nc.vector.tensor_tensor(r_att[:], r_att[:], gate_att[:].unsqueeze(1).broadcast_to([P, NT, NH]),
                                            ALU.mult).then_inc(S["r_att"], 1)
                    need(dve, "r_att", a)
                    nc.vector.tensor_tensor(mix_b[:], att[:, :, :, 0:HD], r_att[:].unsqueeze(3).broadcast_to([P, NT, NH, HD]),
                                            ALU.mult).then_inc(S["mix"], 1)
                    need(dve, "mix", a)
                    nc.vector.tensor_tensor(mixed[:].rearrange("p t d -> p (t d)"), mix_a[:].rearrange("p t h d -> p (t h d)"),
                                            mix_b[:].rearrange("p t h d -> p (t h d)"), ALU.add).then_inc(S["mixed"], 1)
                    need(dve, "o_mm", a)
                    need(dve, "xt_in", a)
                    nc.vector.tensor_tensor(res[:].rearrange("p t d -> p (t d)"), SB[:, 512:1024],
                                            xt[:].rearrange("p t d -> p (t d)"), ALU.add).then_inc(S["res1"], 1)
                    norm(a, 1, x1, "x1")
                    need(dve, "rinv", a)
                    prev(dve, "xn_mm", a)
                    for t in range(NT):
                        nc.vector.tensor_scalar(xn[:, t], x1[:, t], rinv[:, t:t + 1], None, ALU.mult).then_inc(S["xn"], 1)

            pipelined(dve, iteration)

            cslot = con[0:E, CONST["slot"]]
            nc.vector.scalar_tensor_tensor(zslot[:], chosen[:], 0.0, cslot, ALU.is_equal, ALU.mult).then_inc(S["slots"], 1)
            nc.vector.tensor_scalar(tok[:], chosen[:], -1.0, float(NTOK), ALU.mult, ALU.add).then_inc(S["slots"], 1)
            dve.wait_ge(S["slots"], 2)
            for e in range(2):
                nc.vector.tensor_tensor(tokd[:, e], tok[:], zslot[:], ALU.add).then_inc(S["slots"], 1)
            dve.wait_ge(S["tok_mm"], 1)
            for e in range(2):
                r = slice(e * CAP, (e + 1) * CAP)
                src = SB[r, 0:E].rearrange("p (j e) -> p j e", e=2)[:, :, e]
                nc.vector.tensor_copy(idx_in[r], src).then_inc(S["slots"], 1)
                nc.vector.tensor_scalar(idx_out[r], src, float(e * ROWS), None, ALU.add).then_inc(S["slots"], 1)

            def gathered(p):
                dve.wait_ge(S["gt_mm"], p + 1)
                if p >= 2:
                    dve.wait_ge(S["gu_mm"], p - 1)
                nc.vector.tensor_copy(xin[:, p % 2].rearrange("p c s -> p (c s)"), O[:, p % 2, 0:D]).then_inc(S["xin"], 1)

            def hidden(p):
                dve.wait_ge(S["hexp"], p + 1)
                he, hs = hexp[:, p % 2, :], hsig[:, p % 2, :]
                nc.vector.tensor_scalar(hs, he, 1.0, None, ALU.add).then_inc(S["hstep"], 1)
                dve.wait_ge(S["hstep"], 3 * p + 1)
                nc.vector.reciprocal(hs, hs).then_inc(S["hstep"], 1)
                dve.wait_ge(S["hstep"], 3 * p + 2)
                nc.vector.tensor_tensor(hs, M[0:INNER, p % 2, 0:P], hs, ALU.mult).then_inc(S["hstep"], 1)
                dve.wait_ge(S["hstep"], 3 * p + 3)
                if p >= 2:
                    dve.wait_ge(S["wd_mm"], p - 1)
                nc.vector.tensor_tensor(hid[:, p % 2, :], M[0:INNER, p % 2, P:2 * P], hs, ALU.mult).then_inc(S["hid"], 1)

            for p in range(PAIRS + 1):
                if p < PAIRS:
                    gathered(p)
                if p >= 1:
                    hidden(p - 1)

            for t in range(NTOK // P):
                dve.wait_ge(S["fin"][t % 2], 16 * CHAINS * (t // 2 + 1))
                f = fin[:, t % 2]
                nc.vector.tensor_tensor(f[:, 0], f[:, 0], f[:, 1], ALU.add).then_inc(S["fadd"], 1)
                nc.vector.tensor_tensor(f[:, 2], f[:, 2], f[:, 3], ALU.add).then_inc(S["fadd"], 1)
                dve.wait_ge(S["fadd"], 3 * t + 2)
                if t >= 2:
                    dve.wait_ge(S["stored"][t % 2], 16 * (t // 2))
                nc.vector.tensor_tensor(fsum[:, t % 2], f[:, 0], f[:, 2], ALU.add).then_inc(S["fadd"], 1)
                dve.wait_ge(S["fadd"], 3 * t + 3)
                nc.vector.bn_stats(stats[:, t % 2], fsum[:, t % 2]).then_inc(S["fstat"], 1)
                dve.wait_ge(S["fstat"], t + 1)
                nc.vector.bn_aggr(mv[:, t % 2], stats[:, t % 2]).then_inc(S["fmv"], 1)
                dve.wait_ge(S["fmv"], t + 1)
                dve.wait_ge(S["frstd"], t + 1)
                nc.vector.tensor_scalar(fsum[:, t % 2], fsum[:, t % 2], mv[:, t % 2, 0:1], rstd[:, t % 2:t % 2 + 1],
                                        ALU.subtract, ALU.mult).then_inc(S["fout"], 1)

        @block.tensor
        def _(pe):
            seed(pe, SEEDED["tensor"])
            def mm(o, l, r, start=True, stop=True):
                return nc.tensor.matmul(o, l, r, start=start, stop=stop)

            pe.wait_ge(S["ctx_in"], 48)
            pe.wait_ge(S["w_in"], 16 * 8)
            for o in range(NC):
                for c in range(NC):
                    i = mm(SA[:, o * 256:(o + 1) * 256], w_sb["xk"][:, c, o * P:(o + 1) * P], ctx_sb[:, c, :, 0, :],
                           c == 0, c == NC - 1)
            i.then_inc(S["xk_mm"], 1)
            for b in range(B):
                for c in range(NC):
                    i = mm(O[:, b // 2, (b % 2) * D:(b % 2 + 1) * D], ctx_sb[:, c, b], w_sb["xv"][:, c], c == 0, c == NC - 1)
                if b % 2:
                    i.then_inc(S["xv_mm"], 1)
            pe.wait_ge(S["xk_ev"], 1)
            pe.wait_ge(S["wqk_in"], 32)
            pe.wait_ge(S["consts"], 16)
            pe.wait_ge(S["setup"], 4)
            pe.wait_ge(S["k_rows"], 2)
            pe.wait_ge(S["mbias"], 1)
            pe.wait_ge(S["xv_blk"], 2)

            def project(dst, wname, src):
                for o in range(NC):
                    for c in range(NC):
                        i = mm(dst[:, o * T:(o + 1) * T], w_sb[wname][:, c, o * P:(o + 1) * P], src[:, c, :], c == 0, c == NC - 1)
                return i

            def project_tok(dst, wname, src):
                for t in range(NT):
                    for c in range(NC):
                        i = mm(dst[:, t * D:(t + 1) * D], src[:, c, t * P:(t + 1) * P], w_sb[wname][:, c], c == 0, c == NC - 1)
                return i

            def turn(dst, src):
                for t in range(NT):
                    for c in range(NC):
                        i = nc.tensor.transpose(dst[:, c * T + t * P:c * T + (t + 1) * P], src[:, t, c * P:(c + 1) * P], ident)
                return i

            def iteration(a, b):
                def second(g):
                    if g < 2:
                        need(pe, "nmax_rows", a, 1)
                        need(pe, "s1_max", a)
                    else:
                        need(pe, "s2_exp", a, g - 1)
                        need(pe, "nmax_rows", a, g // 2 + 1)
                    if g == 0:
                        need(pe, "nmax_rows", a)
                    for i in range(2):
                        for k in range(NT):
                            n = i * NT + k
                            m = mm(slot[g % 2][:, n * T:(n + 1) * T], k_op[:, 2 * g + i, k * P:(k + 1) * P], q_op[:, 2 * g + i, :])
                    m.then_inc(S["s2_mm"], 1)

                def weighted(g):
                    need(pe, "s2_exp", a, g + 1)
                    for i in range(2):
                        h = head_of(2 * g + i)
                        r, c = h % HG, h // HG
                        for k in range(NT):
                            m = mm(O[r * VW:(r + 1) * VW, c // 2, (c % 2) * T:(c % 2 + 1) * T], vaug[:, k, h, :],
                                   probs[:, g % 2, i, k, :], k == 0, k == NT - 1)
                    m.then_inc(S["av_mm"], 1)

                if a is not None:
                    need(pe, "xf_in", a)
                    prev(pe, "mix", a)
                    project(SA[:, 0:512], "q", xf)
                    project(SA[:, 512:1024], "k", xf).then_inc(S["qk_mm"], 1)
                    project_tok(O[:, 0, :], "v", xf).then_inc(S["v_mm"], 1)
                if b is not None:
                    need(pe, "xn", b)
                    prev(pe, "eprob", b)
                    prev(pe, "keys_ev", b)
                    turn(M[:, 0, :], xn).then_inc(S["xn_mm"], 1)
                    need(pe, "xn_ev", b)
                    project(M[:, 1, :], "xq", xn_f).then_inc(S["xq_mm"], 1)
                    project_tok(M[:, 0, :], "xg", xn_f).then_inc(S["gate_mm"], 1)
                if a is not None:
                    need(pe, "feat", a)
                    need(pe, "v_ev", a)
                    for t in range(NT):
                        for c in range(NC):
                            i = nc.tensor.transpose(O[:, 1, t * D + c * P:t * D + (c + 1) * P], feat[:, 1, c, t * P:(t + 1) * P], ident)
                    i.then_inc(S["kfeat_mm"], 1)

                def context_scores(t):
                    need(pe, "kblk", b)
                    if t == 0:
                        need(pe, "xq_ev", b)
                        need(pe, "gate_th", b)
                    else:
                        need(pe, "xsub", b, t)
                    for c in range(NC):
                        mm(M[:, c, :], xq_f[:, c, t * P:(t + 1) * P], xk_blk[:, c], True, False)
                        i = mm(M[:, c, :], ones_row[:], mbias[:, bass.ds(b, 1)].rearrange("o b h m -> o (b h m)"), False, True)
                    i.then_inc(S["x_mm"], 1)

                if b is not None:
                    context_scores(0)
                if a is not None:
                    need(pe, "kfeat_ev", a)
                    for c in range(NC):
                        for t in range(NT):
                            i = mm(O[:, 0, c * HC * HV:(c + 1) * HC * HV], kfeat_tok[:, t, c * P:(c + 1) * P],
                                   vaug[:, t, c * HC:(c + 1) * HC, 0:HV], t == 0, t == NT - 1)
                    i.then_inc(S["mem_mm"], 1)
                if b is not None:
                    context_scores(1)
                if a is not None:
                    need(pe, "memory", a)
                    for t in range(NT):
                        for c in range(NC):
                            i = mm(O[:, t, c * HC * HV:(c + 1) * HC * HV], feat[:, 0, c, t * P:(t + 1) * P], memory[:, c])
                    i.then_inc(S["lin_mm"], 1)
                if b is not None:
                    for t in range(NT):
                        need(pe, "xexp", b, t + 1)
                        if t == 0:
                            need(pe, "xsub", b)
                        else:
                            need(pe, "xpt_ev", b, t)
                        for j in range(NH // 2):
                            i = nc.tensor.transpose(M[:, j // 4, (j % 4) * P:(j % 4 + 1) * P],
                                                    xp[:, t, 2 * j:2 * j + 2, :].rearrange("p h m -> p (h m)"), ident)
                        i.then_inc(S["xpt_mm"], 1)
                    need(pe, "xpt_ev", b)
                    for t in range(NT):
                        for j in range(NH // 2):
                            i = mm(M[:, t, 2 * j * HV:(2 * j + 2) * HV], xp_t[:, t, j, :],
                                   xv_blk[:, bass.ds(b, 1), j].rearrange("p b e v -> p (b e v)"))
                        i.then_inc(S["xav_mm"], 1)
                if b is not None and a is None:
                    cross_out(b, 0)
                    cross_out(b, 1)
                if a is not None:
                    need(pe, "op_in", a)
                    need(pe, "rope", a)
                    prev(pe, "res1", a)
                    for g in range(GRP):
                        if g >= 2:
                            need(pe, "s1_max", a, g - 1)
                        for n in range(2 * NT):
                            j, t = 2 * g + n // NT, n % NT
                            i = mm(slot[g % 2][:, n * T:(n + 1) * T], q_op[0:SPLIT_ROWS, j, t * P:(t + 1) * P],
                                   k_op[0:SPLIT_ROWS, j, :])
                        i.then_inc(S["s1_mm"], 1)
                        if b is not None and g in (1, 3):
                            cross_out(b, g // 2)
                    need(pe, "nmax_lo", a)
                    for t in range(NT):
                        i = nc.tensor.transpose(SA[0:32, 0:512].bitcast(BF16)[:, t * P:(t + 1) * P],
                                                nmax_parts[:, t].rearrange("p s h -> p (s h)"), identb[:])
                    i.then_inc(S["nmax_mm"], 1)
                    need(pe, "lin_mm", a)
                    need(pe, "mix", a, 1)

                def router_rows():
                    need(pe, "x2", b)
                    turn(M[:, 0, :], row).then_inc(S["x2_mm"], 1)

                def router_scores():
                    need(pe, "x2_ev", b)
                    for t in range(NT):
                        for c in range(NC):
                            i = mm(M[:, 1, t * E:(t + 1) * E], x2_f[:, c, t * P:(t + 1) * P], router_sb[:, c], c == 0, c == NC - 1)
                    i.then_inc(S["lg_mm"], 1)

                def router_keys():
                    need(pe, "keys", b)
                    passed(pe)
                    for t in range(NT):
                        i = nc.tensor.transpose(M[0:E, 1, 256 + t * P:256 + (t + 1) * P], keys[:, t], ident)
                    i.then_inc(S["keys_mm"], 1)

                for g in range(GRP + 1):
                    if a is not None and g < GRP:
                        second(g)
                    if b is not None:
                        for at, f in ((X2_AT, router_rows), (LG_AT, router_scores), (KEYS_AT, router_keys)):
                            if g == at:
                                f()
                    if a is not None and g >= 1:
                        weighted(g - 1)
                if a is not None:
                    for t in range(NT):
                        for c in range(NH // HG):
                            need(pe, "att_ev", a, c // 2 + 1)
                            i = nc.tensor.transpose(SA[:, t * 512 + c * P:t * 512 + (c + 1) * P], att_f[:, c, t * P:(t + 1) * P], ident)
                    i.then_inc(S["att_mm"], 1)
                    need(pe, "mixed", a)
                    turn(SB[:, 0:512], mixed).then_inc(S["mixed_mm"], 1)
                    need(pe, "mixed_ev", a)
                    project_tok(SB[:, 512:1024], "o", mixed_f).then_inc(S["o_mm"], 1)

            def cross_out(b, step):
                if step == 0:
                    need(pe, "xatt", b)
                    turn(M[:, 0, :], xatt).then_inc(S["xatt_mm"], 1)
                else:
                    need(pe, "xatt_ev", b)
                    project_tok(M[:, 1, :], "xo", xatt_f).then_inc(S["xo_mm"], 1)

            pe.wait_ge(S["w_in"], 16 * 8)
            pipelined(pe, iteration)

            pe.wait_ge(S["slots"], 4)
            nc.tensor.transpose(SB[:, 0:E], tokd[:].rearrange("e a c -> e (a c)"), ident[0:E, 0:E]).then_inc(S["tok_mm"], 1)
            pe.wait_ge(S["slots"], 8)

            def turn_rows(p):
                pe.wait_ge(S["gath"][p % GRING], 16 * (p // GRING + 1))
                if p >= 2:
                    pe.wait_ge(S["xin"], p - 1)
                for c in range(NC):
                    i = nc.tensor.transpose(O[:, p % 2, c * P:(c + 1) * P], gath[:, p % GRING, c * P:(c + 1) * P], ident)
                i.then_inc(S["gt_mm"], 1)

            def gate_up(p):
                pe.wait_ge(S["xin"], p + 1)
                pe.wait_ge(S["gu"][p % RING], 32 * (p // RING + 1))
                if p >= 2:
                    pe.wait_ge(S["hid"], p - 1)
                for e in range(2):
                    for u in range(2):
                        for c in range(NC):
                            i = mm(M[0:INNER, p % 2, u * P + e * CAP:u * P + (e + 1) * CAP], gu_sb[:, p % RING, e, u, c, :],
                                   xin[:, p % 2, c, e * CAP:(e + 1) * CAP], c == 0, c == NC - 1)
                i.then_inc(S["gu_mm"], 1)

            def down(p):
                pe.wait_ge(S["hid"], p + 1)
                if p >= 2:
                    pe.wait_ge(S["yw"], 2 * (p - 1))
                for e in range(2):
                    i = mm(slot[p % 2][e * CAP:(e + 1) * CAP, 0:D], hid[:, p % 2, e * CAP:(e + 1) * CAP], wd_sb[:, p % RING, e])
                i.then_inc(S["wd_mm"], 1)

            for p in range(PAIRS + 2):
                if p < PAIRS:
                    turn_rows(p)
                if 1 <= p <= PAIRS:
                    gate_up(p - 1)
                if p >= 2:
                    down(p - 2)


def head_of(j):
    return (j % NC) * HC + j // NC


_IN = ["x_tok", "x_feat", "weights", "router", "params", "ctx_feat", "mask_row", "mask_col", "consts",
       "wgu", "wd"]


def lay_out(i):
    f = np.float32
    x = np.asarray(i["x"])
    x = np.concatenate([x, np.zeros_like(x[:1])])
    a = {"x_tok": x.reshape(B + 1, NT, P, D).transpose(0, 2, 1, 3),
         "x_feat": x.transpose(0, 2, 1).reshape(B + 1, NC, P, T).transpose(0, 2, 1, 3)}
    perm = np.arange(D).reshape(NC, HC, HD).transpose(0, 2, 1).ravel()
    ws = {"q": np.asarray(i["L0_attn_Wq"])[perm].T, "k": np.asarray(i["L0_attn_Wk"])[perm].T,
          "v": np.asarray(i["L0_attn_Wv"]).T, "o": np.asarray(i["L0_attn_Wo"]).T,
          "xq": np.asarray(i["L0_xattn_wq"]).T, "xk": np.asarray(i["L0_xattn_wk"]).T, "xv": np.asarray(i["L0_xattn_wv"]).T,
          "xo": np.asarray(i["L0_xattn_wo"]).T, "xg": np.asarray(i["L0_xattn_wg"]).T}
    a["weights"] = np.stack([ws[n].reshape(NC, P, D).transpose(1, 0, 2) for n in W_NAMES])
    a["router"] = np.asarray(i["L0_ffn_gate_w"]).T.reshape(NC, P, E).transpose(1, 0, 2)
    gate = np.broadcast_to(np.asarray(i["L0_attn_gate"]).reshape(1, NH), (P, NH))
    a["params"] = np.concatenate([gate, np.asarray(i["L0_xattn_norm_w"]).reshape(NC, P).T], 1)
    c = np.asarray(i["ctx_2048"]).transpose(2, 0, 1).reshape(NC, P, B, 1, MEM).transpose(1, 0, 2, 3, 4)
    a["ctx_feat"] = np.broadcast_to(c, (P, NC, B, 2, MEM))
    m = np.asarray(i["mask_BxS2_bk0"])
    a["mask_row"] = m[None]
    a["mask_col"] = np.concatenate([m.T, m.T])
    con = np.zeros((P, CONST_W), f)
    inv = (f(1) / np.power(f(10000), np.arange(0, D, 2, dtype=f) / f(D))).astype(f)
    ang = np.arange(T, dtype=f)[None, :] * inv[perm[:P]][:, None]
    p = np.arange(P)[:, None]
    con[:, CONST["cos"]], con[:, CONST["sin"]] = np.cos(ang), np.sin(ang)
    con[:, CONST["ident"]] = np.eye(P)
    con[:, CONST["head_of_row"]] = p % HC == np.arange(HC)
    con[:, CONST["xhead_of_row"]] = p // HD == np.arange(HC)
    con[:, CONST["half_of_row"]] = p // MEM == np.arange(2)
    con[:, CONST["key"]] = NTOK - (np.arange(NT) * P + p)
    con[:, CONST["slot"]] = np.arange(CAP)
    a["consts"] = con
    con[:, CONST["place_of_row"]] = p % NH == np.arange(NH)
    gu = np.stack([np.asarray(i["L0_ffn_wg"]), np.asarray(i["L0_ffn_wu"])], 1).reshape(PAIRS, 2, 2, NC, P, INNER)
    a["wgu"] = gu.transpose(0, 4, 1, 2, 3, 5)
    a["wd"] = np.asarray(i["L0_ffn_wd"]).reshape(PAIRS, 2, INNER, D).transpose(0, 2, 1, 3)
    return {n: np.ascontiguousarray(a[n]) for n in _IN}


def kernel(**inputs):
    import concourse.bacc as bacc
    from concourse.bass_utils import run_bass_kernel_spmd

    nc = bacc.Bacc("TRN2", target_bir_lowering=False, num_devices=1)
    arrays = lay_out(inputs)
    args = [nc.dram_tensor(n, a.shape, mybir.dt.from_np(a.dtype), kind="ExternalInput").ap() for n, a in arrays.items()]
    out = nc.dram_tensor("out", (NTOK // P, P, D), F32, kind="ExternalOutput").ap()
    build(nc, *args, out)
    r = run_bass_kernel_spmd(nc, [arrays], core_ids=[0])
    return r.results[0]["out"].reshape(B, T, D)
```

```python
from contextlib import ExitStack

import concourse.bass as bass
from concourse import mybir
import numpy as np

ALU = mybir.AluOpType
ACT = mybir.ActivationFunctionType
F32 = mybir.dt.float32
BF16 = mybir.dt.bfloat16
I32 = mybir.dt.int32
U8 = mybir.dt.uint8
AX = mybir.AxisListType

B, T, D = 4, 256, 256
P = 128
NT, NC = T // P, D // P
NH, HD = 16, 16
HC = NH // NC
HV = HD + 1
VW = 32
HG = P // VW
MEM = 64
E, TOPK, INNER, CAP = 64, 8, 96, 64
PAIRS = E // 2
RING = 8
LATE = 11
LATE_GRP = 4
GU_W, WD_W = 2 * 2 * NC * INNER, 2 * D
ROW = D + E
NTOK = B * T
EARLY_TOK = NTOK - T
TILES = NTOK // P
ROWS = NTOK + CAP
GRING = 10
YRING = 6
LAG = 9
CHAINS = 3
NEG = -1.0e30
GROUPS_Q = ((0, 3), (0, 2), (0, 1))
GROUPS_K = ((0, 1), (0, 1), (0, 1), (1, 2), (1, 2), (2, 3))
SPLIT_ROWS = 6 * HD
GRP = 8

W_NAMES = ("q", "k", "v", "o", "xq", "xg", "xo", "xk", "xv")
CONST = {}
_at = 0
for _n, _w in (("cos", T), ("sin", T), ("ident", P), ("head_of_row", HC), ("xhead_of_row", HC),
               ("half_of_row", 2), ("key", NT), ("slot", CAP), ("place_of_row", NH)):
    CONST[_n] = slice(_at, _at + _w)
    _at += _w
CONST_W = _at
PARAM_W = NH + NC


def build(nc, x_tok, x_feat, weights, router, params, ctx_feat, mask_row, mask_col, consts,
          wgu, wd, out):
    with ExitStack() as ctx:
        def sb(name, shape, dt=F32):
            return ctx.enter_context(nc.sbuf_tensor(name, shape, dt))

        def ps(name, shape, dt=F32):
            return ctx.enter_context(nc.psum_tensor(name, shape, dt))

        early = sb("early", [P, LATE * (GU_W + WD_W)])
        taken = [0]

        def carve(shape, dt=F32):
            n = int(np.prod(shape)) * (1 if dt == F32 else 2) // (1 if dt == F32 else 4)
            v = early[:, taken[0]:taken[0] + n]
            taken[0] += n
            assert taken[0] <= LATE * (GU_W + WD_W)
            names = " ".join("abcdef"[:len(shape)])
            v = v if dt == F32 else v.bitcast(dt)
            return v.rearrange(f"p ({names}) -> p {names}", **dict(zip("abcdef", shape)))

        w_sb = {n: carve([NC, D]) if n in ("q", "k", "v", "o") else sb(f"w_{n}", [P, NC, D]) for n in W_NAMES}
        router_sb = sb("router_sb", [P, NC, E])
        con = sb("con", [P, CONST_W])
        identb = sb("identb", [P, P], BF16)
        par = sb("par", [P, PARAM_W])
        gate_mem = sb("gate_mem", [P, NH])
        gate_att = sb("gate_att", [P, NH])
        gate_tmp = sb("gate_tmp", [P, NH])
        cos, sin, ident = (con[:, CONST[n]] for n in ("cos", "sin", "ident"))

        xf = sb("xf", [P, NC, T])
        xt = sb("xt", [P, NT, D])
        vaug = carve([NT, NH, VW])
        rot_a = carve([2, NC, T])
        rot_b = carve([2, NC, T])
        qk = carve([2, NC, T])
        parts = carve([2, 3, NC, T], BF16)
        rest = rot_b
        feat = carve([2, NC, T])
        kfeat_tok = carve([NT, D])
        memory = sb("memory", [P, NC, HC * HV])
        q_op = carve([NH, T], BF16)
        k_op = carve([NH, T], BF16)
        nmax = sb("nmax", [P, NH, NT])
        nmax_parts = sb("nmax_parts", [P, NT, 2, NH], BF16)
        probs = sb("probs", [P, 2, 2, NT, T])
        r_lin = sb("r_lin", [P, NT, NH])
        r_att = sb("r_att", [P, NT, NH])
        att_f = sb("att_f", [P, NH // HG, T])
        mix_a = sb("mix_a", [P, NT, NH, HD])
        mix_b = sb("mix_b", [P, NT, NH, HD])
        mixed = sb("mixed", [P, NT, D])
        mixed_f = sb("mixed_f", [P, NC, T])
        res = sb("res", [P, NT, D])
        stats = sb("stats", [P, NT, 6])
        mv = sb("mv", [P, NT, 2])
        mhalf = sb("mhalf", [P, 8])
        rstd = sb("rstd", [P, NT])
        x1 = sb("x1", [P, NT, D])
        sq = sb("sq", [P, NT, D])
        ssum = sb("ssum", [P, NT])
        rinv = sb("rinv", [P, NT])
        xn = sb("xn", [P, NT, D])
        xn_f = sb("xn_f", [P, NC, T])
        xq_f = sb("xq_f", [P, NC, T])
        ctx_sb = sb("ctx_sb", [P, NC, B, 2, MEM])
        maskr = sb("maskr", [1, B, MEM], U8)
        maskc = sb("maskc", [P, B], U8)
        maskf = sb("maskf", [P, B])
        mbias = sb("mbias", [1, B, HC, MEM], BF16)
        ones_row = sb("ones_row", [1, P], BF16)
        xk_f = sb("xk_f", [P, NC, B, MEM])
        xk_blk = sb("xk_blk", [P, NC, HC, MEM])
        xv_m = sb("xv_m", [P, B, NH, HV])
        xv_blk = sb("xv_blk", [P, B, NH // 2, 2, HV])
        xmax = sb("xmax", [P, NT, NH])
        xp = sb("xp", [P, NT, NH, MEM])
        xp_t = sb("xp_t", [P, NT, NH // 2, P])
        sgate = sb("sgate", [P, NT, D])
        rsum = sb("rsum", [P, NT, NH])
        xatt = sb("xatt", [P, NT, D])
        xatt_f = sb("xatt_f", [P, NC, T])
        ygate = sb("ygate", [P, NT, D])
        row = sb("row", [P, NT, ROW])
        x2_f = sb("x2_f", [P, NC, T])
        lmax = sb("lmax", [P, NT])
        eprob = sb("eprob", [P, NT, E])
        top = sb("top", [P, NT, TOPK])
        tsum = sb("tsum", [P, NT])
        left = sb("left", [P, NT, E])
        wrow = sb("wrow", [P, NT, E])
        keycol = sb("keycol", [P, NT])
        keys = sb("keys", [P, NT, E])
        cand = sb("cand", [E, NTOK + CAP])
        chosen = sb("chosen", [E, CAP])
        zslot = sb("zslot", [E, CAP])
        tok = sb("tok", [E, CAP])
        tokd = sb("tokd", [E, 2, CAP])
        idx_in = sb("idx_in", [P, PAIRS], I32)
        idx_out = sb("idx_out", [P, PAIRS], I32)
        zeros = sb("zeros", [P, ROW])

        flat = probs[:].rearrange("p a b k t -> p (a b k t)")
        in_probs = flat.shape[1] // ROW
        gath_a = flat[:, 0:in_probs * ROW].rearrange("p (g r) -> p g r", g=in_probs)
        flat = xp[:].rearrange("p t h m -> p (t h m)")
        htanh, hgate, hid = (flat[:, i * 2 * INNER:(i + 1) * 2 * INNER].rearrange("p (g s) -> p g s", g=2)
                             for i in range(3))
        gath_b = flat[:, 6 * INNER:6 * INNER + (GRING - in_probs) * ROW].rearrange("p (g r) -> p g r", g=GRING - in_probs)

        def gath(p):
            r = p % GRING
            return gath_a[:, r] if r < in_probs else gath_b[:, r - in_probs]

        hid_f = mix_a[:].rearrange("p t h d -> p (t h d)")[0:INNER, 0:2 * P].rearrange("p (g s) -> p g s", g=2)
        flat = xp_t[:].rearrange("p t j q -> p (t j q)")
        yw = flat[:, 0:YRING * D].rearrange("p (g d) -> p g d", g=YRING)
        xin = flat[:, YRING * D:(YRING + 2) * D].rearrange("p (g c s) -> p g c s", g=2, c=NC)
        gu_sb = sb("gu_sb", [P, RING, 2, NC, 2, INNER])
        wd_sb = sb("wd_sb", [INNER, RING, 2, D])

        late_gu = early[:, 0:LATE * GU_W].rearrange("p (r e c u i) -> p r e c u i", r=LATE, e=2, c=NC, u=2)
        late_wd = early[0:INNER, LATE * GU_W:].rearrange("p (r e d) -> p r e d", r=LATE, e=2)

        def place(p):
            if RING <= p < RING + LATE:
                return late_gu[:, p - RING], late_wd[:, p - RING]
            r = p if p < RING else (p - LATE) % RING
            return gu_sb[:, r], wd_sb[:, r]

        def loaded(p):
            if RING <= p < RING + LATE:
                g = (p - RING) // LATE_GRP
                return S["late"][g], 32 * (min((g + 1) * LATE_GRP, LATE) - g * LATE_GRP)
            n = p if p < RING else p - LATE
            return S["gu"][n % RING], 32 * (n // RING + 1)

        ACCS = 2 * CHAINS
        fin = early[:, 0:TILES * ACCS * D].rearrange("p (t f d) -> p t f d", t=TILES, f=ACCS)
        fin_base = [32 * len(range(t, PAIRS - LATE, RING)) for t in range(TILES)]

        SA = ps("SA", [P, 1024])
        SB = ps("SB", [P, 1024])
        O = ps("O", [P, 2, 512])
        M = ps("M", [P, 2, 512])
        slot = (SA, SB)

        def gate_place(a):
            return O[:, 0, :] if a is not None else SA[:, 0:512]

        def context_place(a, t):
            return M if a is not None or t == 0 else O

        part_d = nc.dram_tensor("part_d", [B, 2, 3, P, NC, T], BF16, kind="Internal").ap()
        row_d = nc.dram_tensor("row_d", [ROWS, ROW], F32, kind="Internal").ap()
        acc_d = [nc.dram_tensor(f"acc_d{c}", [2 * ROWS, D], F32, kind="Internal").ap() for c in range(CHAINS)]

        PER = dict(
            xf_in=16, xt_in=16, qk_mm=1, v_mm=1, rot=2, rope=2, v_ev=1, high=1, rest_r=1, mid=1, low=1, parts_out=16,
            op_in=16 * (len(GROUPS_Q) + len(GROUPS_K)), fmin=1, fexp=1, feat=1, kfeat_mm=1, kfeat_ev=1,
            mem_mm=1, memory=1, lin_mm=1, s1_mm=GRP, s1_max=GRP, nmax_hi=1, nmax_lo=1, nmax_mm=1, nmax_rows=2, nmax_rows2=2,
            s2_mm=GRP, s2_exp=GRP, av_mm=GRP, att_ev=2, att_mm=1, r_lin=2, r_att=2, mix=2, mixed=1, mixed_mm=1, mixed_ev=1, o_mm=1,
            res1=1, stats=4, mv=4, var=2, rstd=2, x1=2, sq=2, ssum=1, rinv=1, xn=2, xn_mm=1, xn_ev=2,
            xq_mm=1, xq_ev=1, gate_mm=1, gate_th=1, kblk=2, x_mm=2, xmax=2, xsub=2, xexp=2,
            xpt_mm=2, xpt_ev=2, xav_mm=2, rsum=2, xatt=1, xatt_mm=1, xatt_ev=1, xo_mm=1, ygate=1, res2=1,
            x2=2, x2_mm=1, x2_ev=1, lg_mm=1, lmax=1, eprob=2, top=2, tsum=1,
            trec=1, left=2, wraw=1, wrow=2, keys=2, keycol=1, keys_mm=1, keys_ev=1, row_out=32,
        )
        S = {n: ctx.enter_context(nc.semaphore(n)) for n in PER}
        for n in ("consts", "wqk_in", "wv_in", "w_in", "par_in", "ctx_in", "gates", "setup", "zeroed", "first_key", "vzero",
                  "zero_out", "maskf", "mbias", "xk_mm", "xk_ev", "xv_mm", "xv_ev", "xv_blk", "k_rows",
                  "slots", "tok_mm", "gt_mm", "xin", "gu_mm", "htanh",
                  "hgate", "hid", "hid_mm", "hid_ev", "wd_mm", "yw", "fadd", "fpool", "fstat", "fmv", "fvar",
                  "frstd", "fout", "stored", "passed", "first", "drop", "kept"):
            S[n] = ctx.enter_context(nc.semaphore(n))
        S["gu"] = [ctx.enter_context(nc.semaphore(f"gu_in{r}")) for r in range(RING)]
        S["gath"] = [ctx.enter_context(nc.semaphore(f"gathered{r}")) for r in range(GRING)]
        S["late"] = [ctx.enter_context(nc.semaphore(f"late_in{r}")) for r in range(-(-LATE // LATE_GRP))]
        S["scat"] = [ctx.enter_context(nc.semaphore(f"scatter{c}")) for c in range(CHAINS)]

        SEEDED = dict(
            sync=("parts_out", "row_out"), gpsimd=("low",), scalar=("eprob",),
            vector=("x2", "xn", "feat", "nmax_lo", "ygate", "mix", "res1", "keys_ev"),
            tensor=("x_mm", "s2_mm", "av_mm", "lin_mm", "xn_mm"))
        BASE = {n: 1 for names in SEEDED.values() for n in names}

        def seed(eng, names):
            for n in names:
                eng.sem_inc(S[n], 1)

        def need(eng, name, b, k=None):
            eng.wait_ge(S[name], b * PER[name] + (PER[name] if k is None else k) + BASE.get(name, 0))
            if eng is nc.sync:
                passed(eng, "passed")

        def prev(eng, name, b):
            eng.wait_ge(S[name], b * PER[name] + BASE[name])
            if eng is nc.sync:
                passed(eng, "passed")

        def passed(eng, which="passed"):
            eng.sem_inc(S[which], 1)

        def pipelined(eng, iteration):
            iteration(None, None, 0)
            iteration(0, None, 1)
            with eng.Fori(1, B - 1) as a:
                iteration(a, a - 1, a + 1)
            iteration(B - 1, B - 2, None)
            iteration(None, B - 1, None)

        def load_pair(eng, p):
            gu_p, wd_p = place(p)
            sem, _ = loaded(p)
            eng.dma_start(gu_p, wgu[p]).then_inc(sem, 16)
            eng.dma_start(wd_p, wd[p]).then_inc(sem, 16)

        block = ctx.enter_context(nc.Block())

        @block.sync
        def _(sp):
            seed(sp, SEEDED["sync"])
            sp.dma_start(xf[:], x_feat[0]).then_inc(S["xf_in"], 16)
            sp.dma_start(w_sb["k"][:], weights[1]).then_inc(S["wqk_in"], 16)
            sp.dma_start(con[:], consts).then_inc(S["consts"], 16)
            sp.dma_start(w_sb["v"][:], weights[2]).then_inc(S["wv_in"], 16)
            sp.dma_start(ctx_sb[:], ctx_feat).then_inc(S["ctx_in"], 16)
            sp.dma_start(xt[:], x_tok[0]).then_inc(S["xt_in"], 16)
            for i, n in enumerate(W_NAMES[3:], 3):
                sp.dma_start(w_sb[n][:], weights[i]).then_inc(S["w_in"], 16)
            sp.dma_start(router_sb[:], router).then_inc(S["w_in"], 16)
            def iteration(a, b, c):
                if b is not None:
                    need(sp, "res1", b)
                    sp.dma_start(xt[:], x_tok[b + 1]).then_inc(S["xt_in"], 16)
                if c is not None:
                    need(sp, "high", c)
                    need(sp, "mid", c)
                    need(sp, "low", c)
                    sp.dma_start(part_d[c].rearrange("a s p c t -> p (a s) (c t)"),
                                 parts[:].rearrange("p a s c t -> p (a s) (c t)")).then_inc(S["parts_out"], 16)
                    need(sp, "parts_out", c)
                    prev(sp, "s2_mm", c)
                    for op, w, groups in ((q_op, 0, GROUPS_Q), (k_op, 1, GROUPS_K)):
                        at = 0
                        for lo, hi in groups:
                            n = (hi - lo) * HD
                            sp.dma_start(op[at:at + n].rearrange("r h t -> r (h t)"),
                                         part_d[c, w, lo:hi].rearrange("s (d h) c t -> (s d) (h c t)", h=HC)
                                         ).then_inc(S["op_in"], 16)
                            at += n
                    need(sp, "v_mm", c)
                    sp.dma_start(xf[:], x_feat[c + 1]).then_inc(S["xf_in"], 16)
                    if a is None:
                        sp.wait_ge(S["zeroed"], 1)
                        sp.dma_start(row_d[NTOK:ROWS, :], zeros[0:CAP, 0:ROW]).then_inc(S["zero_out"], 16)
                        for n in range(CHAINS):
                            sp.dma_start(acc_d[n].rearrange("(p r) d -> p r d", p=P),
                                         zeros[:, 0:D].unsqueeze(1).broadcast_to([P, 2 * ROWS // P, D])
                                         ).then_inc(S["zero_out"], 16)
                if a is not None and b is None:
                    for p in range(RING):
                        load_pair(sp, p)
                if b is not None and a is None:
                    need(sp, "o_mm", b)
                    for p in range(RING, RING + LATE):
                        load_pair(sp, p)
                if b is not None:
                    need(sp, "x2", b)
                    need(sp, "wrow", b)
                    sp.dma_start(row_d[0:NTOK].rearrange("(b t p) d -> b p t d", t=NT, p=P)[b], row[:]).then_inc(S["row_out"], 16)
                    sp.wait_ge(S["zero_out"], 16 * (1 + CHAINS))
                    sp.dma_start(acc_d[0][0:NTOK].rearrange("(b t p) d -> b p t d", t=NT, p=P)[b],
                                 row[:, :, 0:D]).then_inc(S["row_out"], 16)
            pipelined(sp, iteration)
            sp.wait_ge(S["xf_in"], 16 * (B + 1))
            sp.wait_ge(S["xt_in"], 16 * (B + 1))

            for p in range(RING + LATE, PAIRS):
                before = p - LATE - RING
                if before >= RING:
                    before += LATE
                sp.wait_ge(S["wd_mm"], before + 1)
                load_pair(sp, p)

            sp.wait_ge(S["wd_mm"], PAIRS)
            for c in range(CHAINS):
                sp.wait_ge(S["scat"][c], 16 * len(range(c, PAIRS, CHAINS)))
            for t in range(TILES):
                for c in range(CHAINS):
                    sp.dma_start(fin[:, t, 2 * c:2 * c + 2, :],
                                 acc_d[c].rearrange("(h r) d -> r h d", h=2)[t * P:(t + 1) * P]).then_inc(S["gu"][t], 16)
            for t in range(TILES):
                sp.wait_ge(S["fout"], t + 1)
                sp.dma_start(out[t], fin[:, t, 0, :]).then_inc(S["stored"], 16)
            sp.wait_ge(S["stored"], 16 * TILES)
            sp.wait_ge(S["row_out"], 32 * B + 1)

        @block.gpsimd
        def _(pool):
            seed(pool, SEEDED["gpsimd"])
            nc.gpsimd.memset(zeros[:], 0.0).then_inc(S["zeroed"], 1)
            nc.gpsimd.memset(mhalf[:], -0.5).then_inc(S["setup"], 1)
            nc.gpsimd.memset(vaug[:], 0.0).then_inc(S["vzero"], 1)
            pool.wait_ge(S["vzero"], 1)
            nc.gpsimd.memset(vaug[:, :, :, HD:HV], 1.0).then_inc(S["setup"], 1)
            nc.gpsimd.memset(ones_row[:], 1.0).then_inc(S["setup"], 1)

            def norm_scale(b, ln):
                need(pool, "mv", b, NT * ln)
                if ln == 2:
                    need(pool, "x1", b)
                else:
                    prev(pool, "x2", b)
                passed(pool)
                nc.gpsimd.tensor_scalar(rstd[:], mv[:, :, 1], 1e-5, None, ALU.add).then_inc(S["var"], 1)
                need(pool, "var", b, ln)
                nc.gpsimd.tensor_tensor(rstd[:], rstd[:], mhalf[:, 0:NT], ALU.pow).then_inc(S["rstd"], 1)

            def iteration(a, b, c):
                if b is not None:
                    norm_scale(b, 1)
                    need(pool, "sq", b)
                    prev(pool, "xn", b)
                    passed(pool)
                    nc.gpsimd.tensor_scalar(rinv[:], ssum[:], 1.0 / D, 1e-6, ALU.mult, ALU.add).then_inc(S["ssum"], 1)
                    need(pool, "ssum", b)
                    nc.gpsimd.tensor_tensor(rinv[:], rinv[:], mhalf[:, 0:NT], ALU.pow).then_inc(S["rinv"], 1)
                    pool.wait_ge(S["xk_ev"], 1)
                    pool.wait_ge(S["consts"], 16)
                    prev(pool, "x_mm", b)
                    for n in range(NC):
                        nc.gpsimd.tensor_tensor(
                            xk_blk[:, n], xk_f[:, n, bass.ds(b, 1), :].broadcast_to([P, HC, MEM]),
                            con[:, CONST["xhead_of_row"]].unsqueeze(2).broadcast_to([P, HC, MEM]), ALU.mult
                        ).then_inc(S["kblk"], 1)
                if c is not None:
                    need(pool, "high", c)
                    nc.gpsimd.tensor_tensor(rest[:], qk[:], parts[:, :, 0], ALU.subtract).then_inc(S["rest_r"], 1)
                    need(pool, "mid", c)
                    nc.gpsimd.tensor_tensor(parts[:, :, 2], rest[:], parts[:, :, 1], ALU.subtract).then_inc(S["low"], 1)
                if b is not None:
                    norm_scale(b, 2)

            pipelined(pool, iteration)

            pool.wait_ge(S["slots"], 8)
            pool.wait_ge(S["row_out"], 32 * B + 1)
            pool.wait_ge(S["zero_out"], 16 * (1 + CHAINS))

            def gather(p):
                if p >= GRING:
                    pool.wait_ge(S["hid"], 2 * (p - GRING + 1))
                nc.gpsimd.indirect_dma_start(gath(p), None, row_d,
                                             bass.IndirectOffsetOnAxis(ap=idx_in[:, p:p + 1], axis=0)).then_inc(S["gath"][p % GRING], 16)

            def scatter(p):
                pool.wait_ge(S["yw"], p + 1)
                if p >= CHAINS:
                    pool.wait_ge(S["scat"][p % CHAINS], 16 * (p // CHAINS))
                nc.gpsimd.indirect_dma_start(acc_d[p % CHAINS], bass.IndirectOffsetOnAxis(ap=idx_out[:, p:p + 1], axis=0),
                                             yw[:, p % YRING, :], None, bounds_check=2 * ROWS - 1, oob_is_err=True,
                                             compute_op=ALU.add).then_inc(S["scat"][p % CHAINS], 16)

            for p in range(PAIRS + LAG):
                if p < PAIRS:
                    gather(p)
                if p >= LAG:
                    scatter(p - LAG)

            def final_half(t):
                pool.wait_ge(S["gu"][t], fin_base[t] + 16 * CHAINS)
                by_two = fin[:, t].rearrange("p (c h) d -> p c h d", h=2)
                nc.gpsimd.tensor_tensor(by_two[:, 1:, 0], by_two[:, 1:, 0], by_two[:, 1:, 1], ALU.add).then_inc(S["fpool"], 1)

            final_half(0)
            for t in range(TILES):
                if t + 1 < TILES:
                    final_half(t + 1)
                pool.wait_ge(S["fmv"], t + 1)
                nc.gpsimd.tensor_scalar(rstd[:, t % 2:t % 2 + 1], mv[:, t % 2, 1:2], 1e-5, None, ALU.add).then_inc(S["fvar"], 1)
                pool.wait_ge(S["fvar"], t + 1)
                nc.gpsimd.tensor_tensor(rstd[:, t % 2:t % 2 + 1], rstd[:, t % 2:t % 2 + 1], mhalf[:, 0:1],
                                        ALU.pow).then_inc(S["frstd"], 1)

        @block.scalar
        def _(act):
            seed(act, SEEDED["scalar"])
            act.dma_start(w_sb["q"][:], weights[0]).then_inc(S["wqk_in"], 16)
            act.dma_start(par[:], params).then_inc(S["par_in"], 16)
            act.dma_start(maskr[:], mask_row).then_inc(S["ctx_in"], 16)
            act.dma_start(maskc[:], mask_col).then_inc(S["ctx_in"], 16)

            act.wait_ge(S["par_in"], 16)
            nc.scalar.activation(gate_tmp[:], par[:, 0:NH], ACT.Exp, scale=-1.0).then_inc(S["gates"], 1)

            def setup():
                act.wait_ge(S["xk_mm"], 1)
                nc.scalar.activation(xk_f[:].rearrange("p c b m -> p (c b m)"), M[:, 0, :], ACT.Copy).then_inc(S["xk_ev"], 1)
                nc.scalar.activation(k_op[SPLIT_ROWS:P],
                                     con[SPLIT_ROWS:P, CONST["place_of_row"]].unsqueeze(2).broadcast_to([32, NH, T]),
                                     ACT.Copy).then_inc(S["k_rows"], 1)
                nc.scalar.activation(identb[:], ident, ACT.Copy).then_inc(S["k_rows"], 1)

            def iteration(a, b, c):
                def exp_group(g):
                    need(act, "s2_mm", a, g + 1)
                    if g >= 2:
                        need(act, "av_mm", a, g - 1)
                    nc.scalar.activation(probs[:, g % 2].rearrange("p a k t -> p (a k t)"), slot[g % 2][:], ACT.Exp,
                                         scale=HD ** -0.5).then_inc(S["s2_exp"], 1)

                def features_exp():
                    need(act, "fmin", c)
                    nc.scalar.activation(rot_a[:], rot_a[:], ACT.Exp).then_inc(S["fexp"], 1)

                def high_part():
                    need(act, "rope", c)
                    prev(act, "parts_out", c)
                    nc.scalar.activation(parts[:, :, 0], qk[:], ACT.Copy).then_inc(S["high"], 1)

                def middle_part():
                    need(act, "rest_r", c)
                    nc.scalar.activation(parts[:, :, 1], rest[:], ACT.Copy).then_inc(S["mid"], 1)

                def context_weights_exp(t):
                    need(act, "xsub", b, t + 1)
                    nc.scalar.activation(xp[:, t], xp[:, t], ACT.Exp, scale=HD ** -0.5).then_inc(S["xexp"], 1)

                def context_turned(t):
                    need(act, "xpt_mm", b, t + 1)
                    nc.scalar.activation(xp_t[:, t].rearrange("p j q -> p (j q)"), context_place(a, t)[:].rearrange("p a c -> p (a c)"),
                                         ACT.Copy).then_inc(S["xpt_ev"], 1)

                def context_out():
                    need(act, "xatt_mm", b)
                    nc.scalar.activation(xatt_f[:].rearrange("p c t -> p (c t)"), M[:, 0, :], ACT.Copy).then_inc(S["xatt_ev"], 1)

                def router_rows():
                    need(act, "x2_mm", b)
                    nc.scalar.activation(x2_f[:].rearrange("p c t -> p (c t)"), M[:, 0, :], ACT.Copy).then_inc(S["x2_ev"], 1)

                def router_exp():
                    need(act, "lmax", b)
                    for t in range(NT):
                        nc.scalar.activation(eprob[:, t], M[:, 1, t * E:(t + 1) * E], ACT.Exp,
                                             bias=lmax[:, t:t + 1]).then_inc(S["eprob"], 1)

                if b is not None:
                    for t in range(NT):
                        need(act, "x1", b, t + 1)
                        nc.scalar.activation(sq[:, t], x1[:, t], ACT.Square, accum_out=ssum[:, t:t + 1]).then_inc(S["sq"], 1)
                    need(act, "xn_mm", b)
                    for n in range(NC):
                        nc.scalar.activation(xn_f[:, n], M[:, 0, n * T:(n + 1) * T], ACT.Copy,
                                             scale=par[:, NH + n:NH + n + 1]).then_inc(S["xn_ev"], 1)
                    need(act, "xq_mm", b)
                    nc.scalar.activation(xq_f[:].rearrange("p c t -> p (c t)"), M[:, 1, :], ACT.Copy).then_inc(S["xq_ev"], 1)
                    need(act, "gate_mm", b)
                    prev(act, "ygate", b)
                    nc.scalar.activation(sgate[:].rearrange("p t d -> p (t d)"), gate_place(a), ACT.Tanh, scale=0.5
                                         ).then_inc(S["gate_th"], 1)
                    context_weights_exp(0)
                    if a is None:
                        context_weights_exp(1)
                        context_turned(0)
                if a is not None:
                    need(act, "nmax_mm", a)
                    for i in range(2):
                        nc.scalar.activation(q_op[SPLIT_ROWS:P, 4 * i:4 * i + 4],
                                             SB[0:32, 0:512].bitcast(BF16)[:, 0:T].unsqueeze(1).broadcast_to([32, 4, T]),
                                             ACT.Copy).then_inc(S["nmax_rows"], 1)
                    exp_group(0)
                    exp_group(1)
                    if b is not None:
                        context_weights_exp(1)
                        context_turned(0)
                if b is not None:
                    context_turned(1)
                if c is not None:
                    high_part()
                if a is not None:
                    exp_group(2)
                if c is not None:
                    features_exp()
                if a is not None:
                    exp_group(3)
                if c is not None:
                    middle_part()
                if a is not None:
                    exp_group(4)
                if b is not None:
                    context_out()
                if a is not None:
                    exp_group(5)
                    exp_group(6)
                    exp_group(7)
                    for i in range(2):
                        need(act, "av_mm", a)
                        nc.scalar.activation(att_f[:, 2 * i:2 * i + 2].rearrange("p g t -> p (g t)"), O[:, i, :],
                                             ACT.Copy).then_inc(S["att_ev"], 1)
                if b is not None:
                    router_rows()
                def values():
                    need(act, "v_mm", c)
                    prev(act, "av_mm", c)
                    act.wait_ge(S["setup"], 3)
                    nc.scalar.activation(vaug[:, :, :, 0:HD], O[:, 0, :].rearrange("p (t h d) -> p t h d", t=NT, h=NH),
                                         ACT.Copy).then_inc(S["v_ev"], 1)

                if c is not None and a is None:
                    values()
                if c is not None:
                    need(act, "kfeat_mm", c)
                    nc.scalar.activation(kfeat_tok[:].rearrange("p t d -> p (t d)"), O[:, 1, :], ACT.Copy).then_inc(S["kfeat_ev"], 1)
                if c is not None and a is None:
                    setup()
                if a is not None:
                    need(act, "mixed_mm", a)
                    nc.scalar.activation(mixed_f[:].rearrange("p c t -> p (c t)"), SB[:, 0:512], ACT.Copy).then_inc(S["mixed_ev"], 1)
                if b is not None:
                    router_exp()
                if a is not None and c is not None:
                    values()

            pipelined(act, iteration)

            for i in range(PAIRS + 3):
                if 1 <= i <= PAIRS:
                    p = i - 1
                    act.wait_ge(S["gu_mm"], p + 1)
                    if p >= 2:
                        act.wait_ge(S["hgate"], p - 1)
                    nc.scalar.activation(htanh[:, p % 2, :], M[:, p % 2, 0:INNER], ACT.Tanh, scale=0.5).then_inc(S["htanh"], 1)
                if 2 <= i <= PAIRS + 1:
                    p = i - 2
                    act.wait_ge(S["hid_mm"], p + 1)
                    if p >= 2:
                        act.wait_ge(S["wd_mm"], p - 1)
                    nc.scalar.activation(hid_f[:, p % 2, :], slot[p % 2][0:INNER, 512:512 + P], ACT.Copy).then_inc(S["hid_ev"], 1)
                if i >= 3:
                    p = i - 3
                    act.wait_ge(S["wd_mm"], p + 1)
                    if p >= YRING:
                        act.wait_ge(S["scat"][(p - YRING) % CHAINS], 16 * ((p - YRING) // CHAINS + 1))
                    nc.scalar.activation(yw[:, p % YRING, :], slot[p % 2][:, 0:D], ACT.Copy, scale=0.5).then_inc(S["yw"], 1)

        @block.vector
        def _(dve):
            seed(dve, SEEDED["vector"])
            dve.wait_ge(S["consts"], 16)
            nc.vector.tensor_copy(keycol[:], con[:, CONST["key"]]).then_inc(S["first_key"], 1)
            def setup():
                dve.wait_ge(S["gates"], 1)
                nc.vector.tensor_scalar(gate_tmp[:], gate_tmp[:], 1.0, None, ALU.add).then_inc(S["gates"], 1)
                dve.wait_ge(S["gates"], 2)
                nc.vector.reciprocal(gate_mem[:], gate_tmp[:]).then_inc(S["gates"], 1)
                dve.wait_ge(S["gates"], 3)
                nc.vector.tensor_scalar(gate_att[:], gate_mem[:], -1.0, 1.0, ALU.mult, ALU.add).then_inc(S["gates"], 1)
                dve.wait_ge(S["ctx_in"], 48)
                nc.vector.tensor_copy(maskf[:], maskc[:]).then_inc(S["maskf"], 1)
                nc.vector.tensor_scalar(mbias[:], maskr[:].unsqueeze(2).broadcast_to([1, B, HC, MEM]), -1.0, -NEG,
                                        ALU.add, ALU.mult).then_inc(S["mbias"], 1)
                dve.wait_ge(S["maskf"], 1)
                nc.vector.tensor_copy(xv_m[:, :, :, HD:HV], maskf[:].unsqueeze(2).unsqueeze(3).broadcast_to([P, B, NH, 1])
                                      ).then_inc(S["xv_ev"], 1)
                for b in range(B):
                    if b % 2 == 0:
                        dve.wait_ge(S["xv_mm"], b // 2 + 1)
                    nc.vector.tensor_scalar(xv_m[:, b, :, 0:HD],
                                            SB[:, b * D:(b + 1) * D].rearrange("p (h d) -> p h d", h=NH),
                                            maskf[:, b:b + 1], None, ALU.mult).then_inc(S["xv_ev"], 1)
                dve.wait_ge(S["xv_ev"], 1 + B)
                for e in range(2):
                    nc.vector.tensor_scalar(
                        xv_blk[:, :, :, e, :].rearrange("p b j v -> p (b j) v"),
                        xv_m[:].rearrange("p b (j e) v -> p (b j) e v", e=2)[:, :, e, :],
                        con[:, CONST["half_of_row"]][:, e:e + 1], None, ALU.mult).then_inc(S["xv_blk"], 1)

            def statistics(b, ln):
                need(dve, f"res{ln}", b)
                for t in range(NT):
                    nc.vector.bn_stats(stats[:, t], res[:, t]).then_inc(S["stats"], 1)
                need(dve, "stats", b, NT * ln)
                passed(dve, "passed")
                for t in range(NT):
                    nc.vector.bn_aggr(mv[:, t], stats[:, t]).then_inc(S["mv"], 1)

            def normalized(b, ln, dst, x_sem):
                need(dve, "mv", b, NT * ln)
                need(dve, "rstd", b, ln)
                for t in range(NT):
                    nc.vector.tensor_scalar(dst[:, t, 0:D], res[:, t], mv[:, t, 0:1], rstd[:, t:t + 1],
                                            ALU.subtract, ALU.mult).then_inc(S[x_sem], 1)

            def scores_less_max(a, b, t):
                need(dve, "x_mm", b, t + 1)
                sc = context_place(a, t)[:].rearrange("p a c -> p (a c)").rearrange("p (h m) -> p h m", m=MEM)
                nc.vector.tensor_reduce(xmax[:, t], sc, AX.X, ALU.max).then_inc(S["xmax"], 1)
                need(dve, "xmax", b, t + 1)
                nc.vector.tensor_tensor(xp[:, t], sc, xmax[:, t].unsqueeze(2).broadcast_to([P, NH, MEM]),
                                        ALU.subtract).then_inc(S["xsub"], 1)

            def choose(last, rounds):
                some = cand[:, EARLY_TOK:] if last else cand[:, 0:EARLY_TOK]
                for r in rounds:
                    n = (CAP // 8 if last else 0) + r
                    eight = chosen[:, 8 * r:8 * r + 8]
                    if r == 0:
                        need(dve, "keys_ev", B - 1 if last else B - 2)
                        if last:
                            dve.wait_ge(S["kept"], 1)
                    nc.vector.max(eight, some).then_inc(S["first"], 1)
                    dve.wait_ge(S["first"], n + 1)
                    nc.vector.match_replace(some, eight, some, 0.0).then_inc(S["drop"], 1)
                    dve.wait_ge(S["drop"], n + 1)
                if r == CAP // 8 - 1 and not last:
                    nc.vector.tensor_copy(cand[:, EARLY_TOK:EARLY_TOK + CAP], chosen[:]).then_inc(S["kept"], 1)

            def iteration(a, b, c):
                def score_max(g):
                    need(dve, "s1_mm", a, g + 1)
                    nc.vector.tensor_reduce(nmax[:, 2 * g:2 * g + 2, :].rearrange("p h t -> p (h t)"),
                                            slot[g % 2][:].rearrange("p (n k) -> p n k", k=T), AX.X, ALU.max,
                                            negate=True).then_inc(S["s1_max"], 1)

                def rotate():
                    need(dve, "qk_mm", c)
                    prev(dve, "feat", c)
                    src = O[:].rearrange("p a (c t) -> p (a c) t", c=NC)
                    nc.vector.tensor_tensor(rot_a[:].rearrange("p a c t -> p (a c) t"), src,
                                            cos.unsqueeze(1).broadcast_to([P, 2 * NC, T]), ALU.mult).then_inc(S["rot"], 1)
                    nc.vector.tensor_tensor(rot_b[:].rearrange("p a c t -> p (a c) t"), src,
                                            sin.unsqueeze(1).broadcast_to([P, 2 * NC, T]), ALU.mult).then_inc(S["rot"], 1)
                    need(dve, "rot", c)
                    prev(dve, "low", c)
                    nc.vector.tensor_tensor(qk[:, :, 0], rot_a[:, :, 0], rot_b[:, :, 1], ALU.subtract).then_inc(S["rope"], 1)
                    nc.vector.tensor_tensor(qk[:, :, 1], rot_a[:, :, 1], rot_b[:, :, 0], ALU.add).then_inc(S["rope"], 1)
                    need(dve, "rope", c)
                    nc.vector.tensor_scalar(rot_a[:], qk[:], 0.0, None, ALU.min).then_inc(S["fmin"], 1)

                def features():
                    need(dve, "fexp", c)
                    prev(dve, "lin_mm", c)
                    nc.vector.scalar_tensor_tensor(feat[:].rearrange("p a c t -> p (a c t)"),
                                                   qk[:].rearrange("p a c t -> p (a c t)"), 0.0,
                                                   rot_a[:].rearrange("p a c t -> p (a c t)"), ALU.max, ALU.add
                                                   ).then_inc(S["feat"], 1)

                def memory_heads():
                    need(dve, "mem_mm", c)
                    nc.vector.tensor_tensor(
                        memory[:].rearrange("p c (h v) -> p c h v", v=HV),
                        O[:, 0, 0:NC * HC * HV].rearrange("p (c h v) -> p c h v", c=NC, h=HC),
                        con[:, CONST["head_of_row"]].unsqueeze(1).unsqueeze(3).broadcast_to([P, NC, HC, HV]), ALU.mult
                    ).then_inc(S["memory"], 1)

                def memory_out():
                    need(dve, "lin_mm", a)
                    lin = O[:, :, 0:NH * HV].rearrange("p t (h v) -> p t h v", v=HV)
                    nc.vector.reciprocal(r_lin[:], lin[:, :, :, HD]).then_inc(S["r_lin"], 1)
                    need(dve, "r_lin", a, 1)
                    nc.vector.tensor_tensor(r_lin[:], r_lin[:], gate_mem[:].unsqueeze(1).broadcast_to([P, NT, NH]),
                                            ALU.mult).then_inc(S["r_lin"], 1)
                    need(dve, "r_lin", a)
                    nc.vector.tensor_tensor(mix_a[:], lin[:, :, :, 0:HD], r_lin[:].unsqueeze(3).broadcast_to([P, NT, NH, HD]),
                                            ALU.mult).then_inc(S["mix"], 1)

                def context_out():
                    need(dve, "xav_mm", b)
                    xo = M[:, :, 0:NH * HV].rearrange("p t (h v) -> p t h v", v=HV)
                    nc.vector.tensor_scalar(rsum[:], xo[:, :, :, HD], 1e-30, None, ALU.max).then_inc(S["rsum"], 1)
                    need(dve, "rsum", b, 1)
                    nc.vector.reciprocal(rsum[:], rsum[:]).then_inc(S["rsum"], 1)
                    need(dve, "rsum", b)
                    nc.vector.tensor_tensor(xatt[:].rearrange("p t (h d) -> p t h d", h=NH), xo[:, :, :, 0:HD],
                                            rsum[:].unsqueeze(3).broadcast_to([P, NT, NH, HD]), ALU.mult).then_inc(S["xatt"], 1)

                def second_norm():
                    need(dve, "xo_mm", b)
                    nc.vector.scalar_tensor_tensor(ygate[:].rearrange("p t d -> p (t d)"), sgate[:].rearrange("p t d -> p (t d)"),
                                                   1.0, M[:, 1, :], ALU.add, ALU.mult).then_inc(S["ygate"], 1)
                    need(dve, "ygate", b)
                    nc.vector.scalar_tensor_tensor(res[:].rearrange("p t d -> p (t d)"), ygate[:].rearrange("p t d -> p (t d)"),
                                                   0.5, x1[:].rearrange("p t d -> p (t d)"), ALU.mult, ALU.add
                                                   ).then_inc(S["res2"], 1)
                    prev(dve, "row_out", b)
                    statistics(b, 2)
                    normalized(b, 2, row, "x2")

                def router_max():
                    need(dve, "lg_mm", b)
                    nc.vector.tensor_reduce(lmax[:], M[:, 1, 0:NT * E].rearrange("p (t e) -> p t e", e=E), AX.X, ALU.max,
                                            negate=True).then_inc(S["lmax"], 1)

                def route():
                    need(dve, "eprob", b)
                    passed(dve)
                    for t in range(NT):
                        nc.vector.max(top[:, t], eprob[:, t]).then_inc(S["top"], 1)
                    need(dve, "top", b)
                    nc.vector.tensor_reduce(tsum[:], top[:], AX.X, ALU.add).then_inc(S["tsum"], 1)
                    need(dve, "tsum", b)
                    nc.vector.reciprocal(tsum[:], tsum[:]).then_inc(S["trec"], 1)
                    for t in range(NT):
                        nc.vector.match_replace(left[:, t], top[:, t], eprob[:, t], -1.0).then_inc(S["left"], 1)
                    need(dve, "left", b)
                    dve.wait_ge(S["first_key"], 1)
                    for t in range(NT):
                        nc.vector.tensor_scalar(keys[:, t], left[:, t], 0.0, keycol[:, t:t + 1], ALU.is_lt, ALU.mult
                                                ).then_inc(S["keys"], 1)
                    nc.vector.scalar_tensor_tensor(wrow[:].rearrange("p t e -> p (t e)"), left[:].rearrange("p t e -> p (t e)"),
                                                   0.0, eprob[:].rearrange("p t e -> p (t e)"), ALU.is_lt, ALU.mult
                                                   ).then_inc(S["wraw"], 1)
                    need(dve, "trec", b)
                    need(dve, "wraw", b)
                    for t in range(NT):
                        nc.vector.tensor_scalar(row[:, t, D:ROW], wrow[:, t], tsum[:, t:t + 1], None, ALU.mult
                                                ).then_inc(S["wrow"], 1)
                    need(dve, "keys", b)
                    nc.vector.tensor_scalar(keycol[:], keycol[:], -float(T), None, ALU.add).then_inc(S["keycol"], 1)

                def candidates():
                    need(dve, "keys_mm", b)
                    dst = cand[:, EARLY_TOK + CAP:] if a is None else cand[:, bass.ds(b * T, T)]
                    nc.vector.tensor_copy(dst, M[0:E, 1, 256:512]).then_inc(S["keys_ev"], 1)

                def mix():
                    need(dve, "att_mm", a)
                    att = SA[:].rearrange("p (t h v) -> p t h v", t=NT, v=VW)
                    nc.vector.reciprocal(r_att[:], att[:, :, :, HD]).then_inc(S["r_att"], 1)
                    need(dve, "r_att", a, 1)
                    nc.vector.tensor_tensor(r_att[:], r_att[:], gate_att[:].unsqueeze(1).broadcast_to([P, NT, NH]),
                                            ALU.mult).then_inc(S["r_att"], 1)
                    need(dve, "r_att", a)
                    nc.vector.tensor_tensor(mix_b[:], att[:, :, :, 0:HD], r_att[:].unsqueeze(3).broadcast_to([P, NT, NH, HD]),
                                            ALU.mult).then_inc(S["mix"], 1)
                    need(dve, "mix", a)
                    nc.vector.tensor_tensor(mixed[:].rearrange("p t d -> p (t d)"), mix_a[:].rearrange("p t h d -> p (t h d)"),
                                            mix_b[:].rearrange("p t h d -> p (t h d)"), ALU.add).then_inc(S["mixed"], 1)

                if b is not None:
                    normalized(b, 1, x1, "x1")
                if a is not None:
                    score_max(0)
                if b is not None:
                    need(dve, "rinv", b)
                    prev(dve, "xn_mm", b)
                    for t in range(NT):
                        nc.vector.tensor_scalar(xn[:, t], x1[:, t], rinv[:, t:t + 1], None, ALU.mult).then_inc(S["xn"], 1)
                if a is not None:
                    memory_out()
                    for g in range(1, 7):
                        score_max(g)
                if b is not None:
                    if a is None:
                        choose(False, range(0, 3))
                    scores_less_max(a, b, 0)
                if a is not None:
                    score_max(7)
                    need(dve, "s1_max", a)
                    prev(dve, "nmax_lo", a)
                    by_t = nmax[:].rearrange("p h t -> p t h")
                    nc.vector.tensor_copy(nmax_parts[:, :, 0, :], by_t).then_inc(S["nmax_hi"], 1)
                    need(dve, "nmax_hi", a)
                    nc.vector.tensor_tensor(nmax_parts[:, :, 1, :], by_t, nmax_parts[:, :, 0, :], ALU.subtract
                                            ).then_inc(S["nmax_lo"], 1)
                    need(dve, "nmax_mm", a)
                    for i in range(2, 4):
                        nc.vector.tensor_copy(q_op[SPLIT_ROWS:P, 4 * i:4 * i + 4],
                                              SB[0:32, 512:1024].bitcast(BF16)[:, 0:T].unsqueeze(1).broadcast_to([32, 4, T])
                                              ).then_inc(S["nmax_rows2"], 1)
                if b is not None:
                    scores_less_max(a, b, 1)
                if c is not None:
                    rotate()
                if b is not None:
                    if a is None:
                        choose(False, range(3, 6))
                if c is not None:
                    features()
                if b is not None:
                    context_out()
                    if a is None:
                        choose(False, range(6, CAP // 8))
                    second_norm()
                if c is not None and a is None:
                    setup()
                if a is not None:
                    mix()
                if b is not None:
                    router_max()
                    route()
                if a is not None:
                    need(dve, "o_mm", a)
                    need(dve, "xt_in", a)
                    nc.vector.tensor_tensor(res[:].rearrange("p t d -> p (t d)"), SB[:, 512:1024],
                                            xt[:].rearrange("p t d -> p (t d)"), ALU.add).then_inc(S["res1"], 1)
                    statistics(a, 1)
                if b is not None:
                    candidates()
                if c is not None:
                    memory_heads()

            pipelined(dve, iteration)
            choose(True, range(CAP // 8))

            cslot = con[0:E, CONST["slot"]]
            nc.vector.scalar_tensor_tensor(zslot[:], chosen[:], 0.0, cslot, ALU.is_equal, ALU.mult).then_inc(S["slots"], 1)
            nc.vector.tensor_scalar(tok[:], chosen[:], -1.0, float(NTOK), ALU.mult, ALU.add).then_inc(S["slots"], 1)
            dve.wait_ge(S["slots"], 2)
            for e in range(2):
                nc.vector.tensor_tensor(tokd[:, e], tok[:], zslot[:], ALU.add).then_inc(S["slots"], 1)
            dve.wait_ge(S["tok_mm"], 1)
            for e in range(2):
                r = slice(e * CAP, (e + 1) * CAP)
                src = SB[r, 0:E].rearrange("p (j e) -> p j e", e=2)[:, :, e]
                nc.vector.tensor_copy(idx_in[r], src).then_inc(S["slots"], 1)
                nc.vector.tensor_scalar(idx_out[r], src, float(e * ROWS), None, ALU.add).then_inc(S["slots"], 1)

            for i in range(PAIRS + 1):
                if i < PAIRS:
                    p = i
                    dve.wait_ge(S["gt_mm"], p + 1)
                    if p >= 2:
                        dve.wait_ge(S["gu_mm"], p - 1)
                    nc.vector.tensor_copy(xin[:, p % 2].rearrange("p c s -> p (c s)"), O[:, p % 2, 0:D]).then_inc(S["xin"], 1)
                if i >= 1:
                    p = i - 1
                    dve.wait_ge(S["htanh"], p + 1)
                    nc.vector.scalar_tensor_tensor(hgate[:, p % 2, :], htanh[:, p % 2, :], 1.0, M[:, p % 2, 0:INNER],
                                                   ALU.add, ALU.mult).then_inc(S["hgate"], 1)
                    dve.wait_ge(S["hgate"], p + 1)
                    if p >= 2:
                        dve.wait_ge(S["hid_mm"], p - 1)
                    for e in range(2):
                        h = slice(e * CAP, (e + 1) * CAP)
                        c = D + 2 * p + e
                        nc.vector.scalar_tensor_tensor(hid[h, p % 2, :], hgate[h, p % 2, :], gath(p)[h, c:c + 1],
                                                       M[h, p % 2, INNER:2 * INNER], ALU.mult, ALU.mult).then_inc(S["hid"], 1)

            def total(t):
                dve.wait_ge(S["gu"][t], fin_base[t] + 16 * CHAINS)
                f = fin[:, t]
                nc.vector.tensor_tensor(f[:, 0], f[:, 0], f[:, 1], ALU.add).then_inc(S["fadd"], 1)
                dve.wait_ge(S["fpool"], t + 1)
                for c in range(1, CHAINS):
                    dve.wait_ge(S["fadd"], CHAINS * t + c)
                    nc.vector.tensor_tensor(f[:, 0], f[:, 0], f[:, 2 * c], ALU.add).then_inc(S["fadd"], 1)
                dve.wait_ge(S["fadd"], CHAINS * (t + 1))
                nc.vector.bn_stats(stats[:, t % 2], f[:, 0]).then_inc(S["fstat"], 1)
                dve.wait_ge(S["fstat"], t + 1)
                nc.vector.bn_aggr(mv[:, t % 2], stats[:, t % 2]).then_inc(S["fmv"], 1)

            total(0)
            for t in range(TILES):
                if t + 1 < TILES:
                    total(t + 1)
                dve.wait_ge(S["fmv"], t + 1)
                dve.wait_ge(S["frstd"], t + 1)
                nc.vector.tensor_scalar(fin[:, t, 0], fin[:, t, 0], mv[:, t % 2, 0:1], rstd[:, t % 2:t % 2 + 1],
                                        ALU.subtract, ALU.mult).then_inc(S["fout"], 1)

        @block.tensor
        def _(pe):
            seed(pe, SEEDED["tensor"])
            def mm(o, l, r, start=True, stop=True):
                return nc.tensor.matmul(o, l, r, start=start, stop=stop)

            def setup():
                pe.wait_ge(S["ctx_in"], 48)
                pe.wait_ge(S["w_in"], 16 * 7)
                project_ctx = [(o, c) for o in range(NC) for c in range(NC)]
                for o, c in project_ctx:
                    i = mm(M[:, 0, o * 256:(o + 1) * 256], w_sb["xk"][:, c, o * P:(o + 1) * P], ctx_sb[:, c, :, 0, :],
                           c == 0, c == NC - 1)
                i.then_inc(S["xk_mm"], 1)
                for b in range(B):
                    for c in range(NC):
                        i = mm(SB[:, b * D:(b + 1) * D], ctx_sb[:, c, b], w_sb["xv"][:, c], c == 0, c == NC - 1)
                    if b % 2:
                        i.then_inc(S["xv_mm"], 1)

            def project(dst, wname, src):
                for o in range(NC):
                    for c in range(NC):
                        i = mm(dst[:, o * T:(o + 1) * T], w_sb[wname][:, c, o * P:(o + 1) * P], src[:, c, :], c == 0, c == NC - 1)
                return i

            def project_tok(dst, wname, src):
                for t in range(NT):
                    for c in range(NC):
                        i = mm(dst[:, t * D:(t + 1) * D], src[:, c, t * P:(t + 1) * P], w_sb[wname][:, c], c == 0, c == NC - 1)
                return i

            def turn(dst, src):
                for t in range(NT):
                    for c in range(NC):
                        i = nc.tensor.transpose(dst[:, c * T + t * P:c * T + (t + 1) * P], src[:, t, c * P:(c + 1) * P], ident)
                return i

            def iteration(a, b, c):
                def first(g):
                    if g == 0:
                        need(pe, "op_in", a)
                        prev(pe, "mix", a)
                    if g == 1:
                        prev(pe, "res1", a)
                        if b is None:
                            pe.wait_ge(S["xv_ev"], 1 + B)
                    if g >= 2:
                        need(pe, "s1_max", a, g - 1)
                    for n in range(2 * NT):
                        j, t = 2 * g + n // NT, n % NT
                        i = mm(slot[g % 2][:, n * T:(n + 1) * T], q_op[0:SPLIT_ROWS, j, t * P:(t + 1) * P],
                               k_op[0:SPLIT_ROWS, j, :])
                    i.then_inc(S["s1_mm"], 1)

                def maxima_turned():
                    need(pe, "nmax_lo", a)
                    if b is None:
                        pe.wait_ge(S["k_rows"], 2)
                    for n in range(2):
                        for t in range(NT):
                            i = nc.tensor.transpose(SB[0:32, n * 512:(n + 1) * 512].bitcast(BF16)[:, t * P:(t + 1) * P],
                                                    nmax_parts[:, t].rearrange("p s h -> p (s h)"), identb[:])
                    i.then_inc(S["nmax_mm"], 1)

                def second(g):
                    if g < 2:
                        need(pe, "s1_max", a)
                    else:
                        need(pe, "s2_exp", a, g - 1)
                    if g == 1:
                        need(pe, "nmax_rows", a)
                        need(pe, "nmax_rows2", a)
                    elif g < 4:
                        need(pe, "nmax_rows", a, g // 2 + 1)
                    else:
                        need(pe, "nmax_rows2", a, g // 2 - 1)
                    for i in range(2):
                        for k in range(NT):
                            n = i * NT + k
                            m = mm(slot[g % 2][:, n * T:(n + 1) * T], k_op[:, 2 * g + i, k * P:(k + 1) * P], q_op[:, 2 * g + i, :])
                    m.then_inc(S["s2_mm"], 1)

                def weighted(g):
                    if g == 0:
                        need(pe, "mix", a, 1)
                        if c is not None:
                            need(pe, "rot", c)
                    need(pe, "s2_exp", a, g + 1)
                    for i in range(2):
                        h = head_of(2 * g + i)
                        r, q = h % HG, h // HG
                        for k in range(NT):
                            m = mm(O[r * VW:(r + 1) * VW, q // 2, (q % 2) * T:(q % 2 + 1) * T], vaug[:, k, h, :],
                                   probs[:, g % 2, i, k, :], k == 0, k == NT - 1)
                    m.then_inc(S["av_mm"], 1)

                def queries():
                    need(pe, "xf_in", c)
                    if a is not None:
                        need(pe, "mix", a, 1)
                    if b is not None:
                        need(pe, "gate_th", b)
                    project(O[:, 0, :], "q", xf)

                def keys_of_self():
                    project(O[:, 1, :], "k", xf).then_inc(S["qk_mm"], 1)

                def values():
                    if a is None:
                        need(pe, "rot", c)
                        pe.wait_ge(S["wv_in"], 16)
                    project_tok(O[:, 0, :], "v", xf).then_inc(S["v_mm"], 1)

                def key_features():
                    need(pe, "feat", c)
                    if a is not None:
                        need(pe, "att_ev", a)
                    if a is None:
                        pe.wait_ge(S["consts"], 16)
                    for t in range(NT):
                        for n in range(NC):
                            i = nc.tensor.transpose(O[:, 1, t * D + n * P:t * D + (n + 1) * P], feat[:, 1, n, t * P:(t + 1) * P], ident)
                    i.then_inc(S["kfeat_mm"], 1)

                def memory_products():
                    need(pe, "v_ev", c)
                    need(pe, "kfeat_ev", c)
                    for n in range(NC):
                        for t in range(NT):
                            i = mm(O[:, 0, n * HC * HV:(n + 1) * HC * HV], kfeat_tok[:, t, n * P:(n + 1) * P],
                                   vaug[:, t, n * HC:(n + 1) * HC, 0:HV], t == 0, t == NT - 1)
                    i.then_inc(S["mem_mm"], 1)

                def memory_read():
                    need(pe, "memory", c)
                    for t in range(NT):
                        for n in range(NC):
                            i = mm(O[:, t, n * HC * HV:(n + 1) * HC * HV], feat[:, 0, n, t * P:(t + 1) * P], memory[:, n])
                    i.then_inc(S["lin_mm"], 1)

                def context_scores(t):
                    need(pe, "kblk", b)
                    if t == 0:
                        need(pe, "xq_ev", b)
                    elif a is not None:
                        need(pe, "xsub", b, t)
                    dst = context_place(a, t)
                    for n in range(NC):
                        mm(dst[:, n, :], xq_f[:, n, t * P:(t + 1) * P], xk_blk[:, n], True, False)
                        i = mm(dst[:, n, :], ones_row[:], mbias[:, bass.ds(b, 1)].rearrange("o b h m -> o (b h m)"), False, True)
                    i.then_inc(S["x_mm"], 1)

                def context_turned(t):
                    need(pe, "xexp", b, t + 1)
                    dst = context_place(a, t)
                    if a is None:
                        need(pe, "xsub", b, t + 1)
                    elif t == 0:
                        need(pe, "xsub", b)
                    else:
                        need(pe, "xpt_ev", b, t)
                    for j in range(NH // 2):
                        i = nc.tensor.transpose(dst[:, j // 4, (j % 4) * P:(j % 4 + 1) * P],
                                                xp[:, t, 2 * j:2 * j + 2, :].rearrange("p h m -> p (h m)"), ident)
                    i.then_inc(S["xpt_mm"], 1)

                def context_weighted(t):
                    need(pe, "xpt_ev", b)
                    for j in range(NH // 2):
                        i = mm(M[:, t, 2 * j * HV:(2 * j + 2) * HV], xp_t[:, t, j, :],
                               xv_blk[:, bass.ds(b, 1), j].rearrange("p b e v -> p (b e v)"))
                    i.then_inc(S["xav_mm"], 1)

                def context_out(step):
                    if step == 0:
                        need(pe, "xatt", b)
                        turn(M[:, 0, :], xatt).then_inc(S["xatt_mm"], 1)
                    else:
                        need(pe, "xatt_ev", b)
                        project_tok(M[:, 1, :], "xo", xatt_f).then_inc(S["xo_mm"], 1)

                def router_rows():
                    need(pe, "x2", b)
                    turn(M[:, 0, :], row).then_inc(S["x2_mm"], 1)

                def router_scores():
                    need(pe, "x2_ev", b)
                    for t in range(NT):
                        for n in range(NC):
                            i = mm(M[:, 1, t * E:(t + 1) * E], x2_f[:, n, t * P:(t + 1) * P], router_sb[:, n], n == 0, n == NC - 1)
                    i.then_inc(S["lg_mm"], 1)

                def router_keys():
                    need(pe, "keys", b)
                    passed(pe)
                    for t in range(NT):
                        i = nc.tensor.transpose(M[0:E, 1, 256 + t * P:256 + (t + 1) * P], keys[:, t], ident)
                    i.then_inc(S["keys_mm"], 1)

                if a is not None:
                    first(0)
                    first(1)
                    first(2)
                if b is not None:
                    pe.wait_ge(S["setup"], 3)
                    pe.wait_ge(S["xk_ev"], 1)
                    pe.wait_ge(S["mbias"], 1)
                    pe.wait_ge(S["xv_blk"], 2)
                    need(pe, "xn", b)
                    prev(pe, "eprob", b)
                    prev(pe, "keys_ev", b)
                    turn(M[:, 0, :], xn).then_inc(S["xn_mm"], 1)
                if a is not None:
                    first(3)
                    first(4)
                if b is not None:
                    need(pe, "xn_ev", b)
                    project(M[:, 1, :], "xq", xn_f).then_inc(S["xq_mm"], 1)
                if a is not None:
                    first(5)
                    first(6)
                if b is not None:
                    context_scores(0)
                if c is not None and b is None:
                    queries()
                if a is not None:
                    first(7)
                if b is not None:
                    if a is not None:
                        need(pe, "mix", a, 1)
                    if a is None:
                        context_scores(1)
                    project_tok(gate_place(a), "xg", xn_f).then_inc(S["gate_mm"], 1)
                if a is not None:
                    if b is not None:
                        context_scores(1)
                    maxima_turned()
                if c is not None and b is not None:
                    queries()
                if a is not None:
                    second(0)
                    second(1)
                if c is not None:
                    keys_of_self()
                if a is not None:
                    second(2)
                if b is not None:
                    context_turned(0)
                    context_turned(1)
                if a is not None:
                    weighted(0)
                if b is not None:
                    context_weighted(0)
                if a is not None:
                    weighted(1)
                if a is not None:
                    second(3)
                if b is not None:
                    context_weighted(1)
                if a is not None:
                    weighted(2)
                    second(4)
                    weighted(3)
                    second(5)
                if b is not None:
                    context_out(0)
                if a is not None:
                    weighted(4)
                if b is not None:
                    context_out(1)
                if a is not None:
                    second(6)
                    weighted(5)
                    second(7)
                    weighted(6)
                    weighted(7)
                if a is not None:
                    for t in range(NT):
                        for n in range(NH // HG):
                            need(pe, "att_ev", a, n // 2 + 1)
                            i = nc.tensor.transpose(SA[:, t * 512 + n * P:t * 512 + (n + 1) * P], att_f[:, n, t * P:(t + 1) * P], ident)
                    i.then_inc(S["att_mm"], 1)
                if b is not None:
                    router_rows()
                if c is not None and a is None:
                    values()
                if c is not None:
                    key_features()
                if b is not None:
                    router_scores()
                if a is not None:
                    need(pe, "mixed", a)
                    turn(SB[:, 0:512], mixed).then_inc(S["mixed_mm"], 1)
                    if c is not None:
                        values()
                    need(pe, "mixed_ev", a)
                    project_tok(SB[:, 512:1024], "o", mixed_f).then_inc(S["o_mm"], 1)
                if b is not None:
                    router_keys()
                if c is not None:
                    memory_products()
                if c is not None and a is None:
                    setup()
                if c is not None:
                    memory_read()

            pe.wait_ge(S["wqk_in"], 32)
            pipelined(pe, iteration)

            pe.wait_ge(S["slots"], 4)
            nc.tensor.transpose(SB[:, 0:E], tokd[:].rearrange("e a c -> e (a c)"), ident[0:E, 0:E]).then_inc(S["tok_mm"], 1)
            pe.wait_ge(S["slots"], 8)

            for i in range(PAIRS + 3):
                if i < PAIRS:
                    pe.wait_ge(S["gath"][i % GRING], 16 * (i // GRING + 1))
                    if i >= 2:
                        pe.wait_ge(S["xin"], i - 1)
                    for c in range(NC):
                        m = nc.tensor.transpose(O[:, i % 2, c * P:(c + 1) * P], gath(i)[:, c * P:(c + 1) * P], ident)
                    m.then_inc(S["gt_mm"], 1)
                if 1 <= i <= PAIRS:
                    p = i - 1
                    pe.wait_ge(S["xin"], p + 1)
                    pe.wait_ge(*loaded(p))
                    if p >= 2:
                        pe.wait_ge(S["hid"], 2 * (p - 1))
                    for e in range(2):
                        h = slice(e * CAP, (e + 1) * CAP)
                        for c in range(NC):
                            m = mm(M[h, p % 2, 0:2 * INNER], xin[:, p % 2, c, h],
                                   place(p)[0][:, e, c].rearrange("p u i -> p (u i)"), c == 0, c == NC - 1)
                    m.then_inc(S["gu_mm"], 1)
                if 2 <= i <= PAIRS + 1:
                    p = i - 2
                    pe.wait_ge(S["hid"], 2 * (p + 1))
                    if p >= 2:
                        pe.wait_ge(S["hid_ev"], p - 1)
                    nc.tensor.transpose(slot[p % 2][0:INNER, 512:512 + P], hid[:, p % 2, :], ident).then_inc(S["hid_mm"], 1)
                if i >= 3:
                    p = i - 3
                    pe.wait_ge(S["hid_ev"], p + 1)
                    if p >= 2:
                        pe.wait_ge(S["yw"], p - 1)
                    for e in range(2):
                        h = slice(e * CAP, (e + 1) * CAP)
                        m = mm(slot[p % 2][h, 0:D], hid_f[:, p % 2, h], place(p)[1][:, e])
                    m.then_inc(S["wd_mm"], 1)


def head_of(j):
    return (j % NC) * HC + j // NC


_IN = ["x_tok", "x_feat", "weights", "router", "params", "ctx_feat", "mask_row", "mask_col", "consts",
       "wgu", "wd"]


def lay_out(i):
    f = np.float32
    x = np.asarray(i["x"])
    x = np.concatenate([x, np.zeros_like(x[:1])])
    a = {"x_tok": x.reshape(B + 1, NT, P, D).transpose(0, 2, 1, 3),
         "x_feat": x.transpose(0, 2, 1).reshape(B + 1, NC, P, T).transpose(0, 2, 1, 3)}
    perm = np.arange(D).reshape(NC, HC, HD).transpose(0, 2, 1).ravel()
    ws = {"q": np.asarray(i["L0_attn_Wq"])[perm].T, "k": np.asarray(i["L0_attn_Wk"])[perm].T,
          "v": np.asarray(i["L0_attn_Wv"]).T, "o": np.asarray(i["L0_attn_Wo"]).T,
          "xq": np.asarray(i["L0_xattn_wq"]).T, "xk": np.asarray(i["L0_xattn_wk"]).T, "xv": np.asarray(i["L0_xattn_wv"]).T,
          "xo": np.asarray(i["L0_xattn_wo"]).T, "xg": np.asarray(i["L0_xattn_wg"]).T}
    a["weights"] = np.stack([ws[n].reshape(NC, P, D).transpose(1, 0, 2) for n in W_NAMES])
    a["router"] = np.asarray(i["L0_ffn_gate_w"]).T.reshape(NC, P, E).transpose(1, 0, 2)
    gate = np.broadcast_to(np.asarray(i["L0_attn_gate"]).reshape(1, NH), (P, NH))
    a["params"] = np.concatenate([gate, np.asarray(i["L0_xattn_norm_w"]).reshape(NC, P).T], 1)
    c = np.asarray(i["ctx_2048"]).transpose(2, 0, 1).reshape(NC, P, B, 1, MEM).transpose(1, 0, 2, 3, 4)
    a["ctx_feat"] = np.broadcast_to(c, (P, NC, B, 2, MEM))
    m = np.asarray(i["mask_BxS2_bk0"])
    a["mask_row"] = m[None]
    a["mask_col"] = np.concatenate([m.T, m.T])
    con = np.zeros((P, CONST_W), f)
    inv = (f(1) / np.power(f(10000), np.arange(0, D, 2, dtype=f) / f(D))).astype(f)
    ang = np.arange(T, dtype=f)[None, :] * inv[perm[:P]][:, None]
    p = np.arange(P)[:, None]
    con[:, CONST["cos"]], con[:, CONST["sin"]] = np.cos(ang), np.sin(ang)
    con[:, CONST["ident"]] = np.eye(P)
    con[:, CONST["head_of_row"]] = p % HC == np.arange(HC)
    con[:, CONST["xhead_of_row"]] = p // HD == np.arange(HC)
    con[:, CONST["half_of_row"]] = p // MEM == np.arange(2)
    con[:, CONST["key"]] = NTOK - (np.arange(NT) * P + p)
    con[:, CONST["slot"]] = np.arange(CAP)
    a["consts"] = con
    con[:, CONST["place_of_row"]] = p % NH == np.arange(NH)
    gu = np.stack([np.asarray(i["L0_ffn_wg"]), np.asarray(i["L0_ffn_wu"])], 1).reshape(PAIRS, 2, 2, NC, P, INNER)
    a["wgu"] = gu.transpose(0, 4, 1, 3, 2, 5)
    a["wd"] = np.asarray(i["L0_ffn_wd"]).reshape(PAIRS, 2, INNER, D).transpose(0, 2, 1, 3)
    return {n: np.ascontiguousarray(a[n]) for n in _IN}


def kernel(**inputs):
    import concourse.bacc as bacc
    from concourse.bass_utils import run_bass_kernel_spmd

    nc = bacc.Bacc("TRN2", target_bir_lowering=False, num_devices=1)
    arrays = lay_out(inputs)
    args = [nc.dram_tensor(n, a.shape, mybir.dt.from_np(a.dtype), kind="ExternalInput").ap() for n, a in arrays.items()]
    out = nc.dram_tensor("out", (NTOK // P, P, D), F32, kind="ExternalOutput").ap()
    build(nc, *args, out)
    r = run_bass_kernel_spmd(nc, [arrays], core_ids=[0])
    return r.results[0]["out"].reshape(B, T, D)
```
